# Optimizing a Trainium2 kernel written in Bass

```python
import numpy as np
import jax
import jax.numpy as jnp

def _softmax(x, axis=-1):
    return jax.nn.softmax(x, axis=axis)

def _gelu(x):
    return jax.nn.gelu(x, approximate=True)

def _silu(x):
    return jax.nn.silu(x)

def _sigmoid(x):
    return jax.nn.sigmoid(x)

def _layernorm(x, axis=-1, eps=1e-05):
    m = jnp.mean(x, axis=axis, keepdims=True)
    v = jnp.var(x, axis=axis, keepdims=True)
    return (x - m) / jnp.sqrt(v + eps)

def _scatter_add(tgt, idx, src, axis=0):
    return tgt.at[idx].add(src)

def _segment_sum(src, seg, n):
    return jax.ops.segment_sum(src, seg, n)
kernel_name = 'mk_seq_preln_d2_jaxref_r8_2d8334'

def setup_inputs(seed: int=0):
    np.random.seed(seed)
    _w = jnp.asarray

    def _L0_attn_setup():
        import jax, jax.numpy as jnp
        import numpy as np
        DIM = 128
        N_HEADS = 16
        HEAD_DIM = DIM // N_HEADS
        D_LATENT = 32
        B, T = (1, 512)
        key = jax.random.key(seed)
        ks = jax.random.split(key, 6)
        s = 0.02
        return {'x': jax.random.normal(ks[0], (B, T, DIM), dtype=jnp.float32), 'W_DKV': jax.random.normal(ks[1], (DIM, D_LATENT), dtype=jnp.float32) * s, 'W_UK': jax.random.normal(ks[2], (D_LATENT, DIM), dtype=jnp.float32) * s, 'W_UV': jax.random.normal(ks[3], (D_LATENT, DIM), dtype=jnp.float32) * s, 'W_UQ': jax.random.normal(ks[4], (DIM, DIM), dtype=jnp.float32) * s, 'W_O': jax.random.normal(ks[5], (DIM, DIM), dtype=jnp.float32) * s}
    _L0_attn_in = _L0_attn_setup()

    def _L0_ffn_setup():
        import math
        import jax, jax.numpy as jnp
        import numpy as np
        NUM_EXPERTS = 8
        CAPACITY_FACTOR = 1.5
        key = jax.random.key(seed)
        ks = jax.random.split(key, 4)
        B, T, D, F, E = (4, 256, 128, 512, NUM_EXPERTS)
        scale = 0.02
        return {'x': jax.random.normal(ks[0], (B, T, D), dtype=jnp.float32), 'router_w': jax.random.normal(ks[1], (E, D), dtype=jnp.float32) * scale, 'w1': jax.random.normal(ks[2], (E, D, F), dtype=jnp.float32) * scale, 'b1': jnp.zeros((E, F), dtype=jnp.float32), 'w2': jax.random.normal(ks[3], (E, F, D), dtype=jnp.float32) * scale, 'b2': jnp.zeros((E, D), dtype=jnp.float32)}
    _L0_ffn_in = _L0_ffn_setup()

    def _L1_attn_setup():
        import jax, jax.numpy as jnp
        import numpy as np
        N_INPUT = 128
        N_HEAD = 16
        ATT_DIM = N_INPUT // N_HEAD * N_HEAD
        V_DIM = N_INPUT // 2 * N_HEAD
        COMB_DIM = 2 * ATT_DIM + V_DIM
        SCALE = (N_INPUT // N_HEAD) ** 0.5
        key = jax.random.key(seed)
        k1, k2, k3 = jax.random.split(key, 3)
        B, T = (8, 128)
        representations = jax.random.normal(k1, (B, T, N_INPUT), dtype=jnp.float32)
        Wc = jax.random.normal(k2, (COMB_DIM, N_INPUT), dtype=jnp.float32) * (0.1 * np.sqrt(2.0 / (COMB_DIM + N_INPUT)))
        bc = jnp.zeros((COMB_DIM,), dtype=jnp.float32)
        Wo = jax.random.normal(k3, (N_INPUT, V_DIM), dtype=jnp.float32) * (0.1 * np.sqrt(2.0 / (N_INPUT + V_DIM)))
        bo = jnp.zeros((N_INPUT,), dtype=jnp.float32)
        return {'representations': representations, 'Wc': Wc, 'bc': bc, 'Wo': Wo, 'bo': bo}
    _L1_attn_in = _L1_attn_setup()

    def _L1_ffn_setup():
        import jax, jax.numpy as jnp
        import numpy as np
        TOP_K = 2

        def _moe(x, Wr, br, W1, b1, W2, b2):
            B, S, D = x.shape
            E = Wr.shape[1]
            xt = x.reshape(-1, D)
            logits = xt @ Wr + br
            top_vals, top_idx = jax.lax.top_k(logits, TOP_K)
            mask = jnp.zeros_like(logits, dtype=bool).at[jnp.arange(xt.shape[0])[:, None], top_idx].set(True)
            sparse_logits = jnp.where(mask, logits, -jnp.inf)
            gate = jax.nn.softmax(sparse_logits, axis=-1)
            h = jax.nn.relu(jnp.einsum('td,edh->teh', xt, W1) + b1)
            y = jnp.einsum('teh,ehd->ted', h, W2) + b2
            out = jnp.einsum('ted,te->td', y, gate)
            return out.reshape(B, S, D)
        key = jax.random.key(seed)
        ks = jax.random.split(key, 5)
        B, S, D, E, H = (2, 256, 128, 8, 512)
        scale = 1.0 / np.sqrt(D)
        return {'x': jax.random.normal(ks[0], (B, S, D), dtype=jnp.float32), 'Wr': jax.random.normal(ks[1], (D, E), dtype=jnp.float32) * scale, 'br': jnp.zeros((E,), dtype=jnp.float32), 'W1': jax.random.normal(ks[2], (E, D, H), dtype=jnp.float32) * scale, 'b1': jnp.zeros((E, H), dtype=jnp.float32), 'W2': jax.random.normal(ks[3], (E, H, D), dtype=jnp.float32) * (1.0 / np.sqrt(H)), 'b2': jnp.zeros((E, D), dtype=jnp.float32)}
    _L1_ffn_in = _L1_ffn_setup()
    _d = {'L0_attn_x': _L0_attn_in['x'], 'L0_attn_W_DKV': _L0_attn_in['W_DKV'], 'L0_attn_W_UK': _L0_attn_in['W_UK'], 'L0_attn_W_UV': _L0_attn_in['W_UV'], 'L0_attn_W_UQ': _L0_attn_in['W_UQ'], 'L0_attn_W_O': _L0_attn_in['W_O'], 'L0_ffn_router_w': _L0_ffn_in['router_w'], 'L0_ffn_w1': _L0_ffn_in['w1'], 'L0_ffn_b1': _L0_ffn_in['b1'], 'L0_ffn_w2': _L0_ffn_in['w2'], 'L0_ffn_b2': _L0_ffn_in['b2'], 'L1_attn_Wc': _L1_attn_in['Wc'], 'L1_attn_bc': _L1_attn_in['bc'], 'L1_attn_Wo': _L1_attn_in['Wo'], 'L1_attn_bo': _L1_attn_in['bo'], 'L1_ffn_Wr': _L1_ffn_in['Wr'], 'L1_ffn_br': _L1_ffn_in['br'], 'L1_ffn_W1': _L1_ffn_in['W1'], 'L1_ffn_b1': _L1_ffn_in['b1'], 'L1_ffn_W2': _L1_ffn_in['W2'], 'L1_ffn_b2': _L1_ffn_in['b2']}
    _x0 = _d['L0_attn_x']
    _d['L0_attn_x'] = jax.random.normal(jax.random.fold_in(jax.random.key(seed), 1), (8, 512, 128), dtype=_x0.dtype)
    del _x0
    return _d

def reference(L0_attn_x, L0_attn_W_DKV, L0_attn_W_UK, L0_attn_W_UV, L0_attn_W_UQ, L0_attn_W_O, L0_ffn_router_w, L0_ffn_w1, L0_ffn_b1, L0_ffn_w2, L0_ffn_b2, L1_attn_Wc, L1_attn_bc, L1_attn_Wo, L1_attn_bo, L1_ffn_Wr, L1_ffn_br, L1_ffn_W1, L1_ffn_b1, L1_ffn_W2, L1_ffn_b2):

    def _L0_attn_ref(x, W_DKV, W_UK, W_UV, W_UQ, W_O):
        import jax, jax.numpy as jnp
        import numpy as np
        DIM = 128
        N_HEADS = 16
        HEAD_DIM = DIM // N_HEADS
        D_LATENT = 32
        B, T = (1, 512)
        b, t, d = x.shape
        h, hd = (N_HEADS, HEAD_DIM)
        c_kv = x @ W_DKV
        k = (c_kv @ W_UK).reshape(b, t, h, hd)
        v = (c_kv @ W_UV).reshape(b, t, h, hd)
        q = (x @ W_UQ).reshape(b, t, h, hd)
        scale = 1.0 / jnp.sqrt(jnp.asarray(hd, x.dtype))
        scores = jnp.einsum('bqhd,bkhd->bhqk', q, k) * scale
        causal = jnp.tril(jnp.ones((t, t), dtype=bool))
        scores = jnp.where(causal, scores, jnp.asarray(-jnp.inf, scores.dtype))
        probs = jax.nn.softmax(scores, axis=-1)
        ctx = jnp.einsum('bhqk,bkhd->bqhd', probs, v).reshape(b, t, d)
        return ctx @ W_O

    def _L0_ffn_ref(x, router_w, w1, b1, w2, b2):
        import math
        import jax, jax.numpy as jnp
        import numpy as np
        NUM_EXPERTS = 8
        CAPACITY_FACTOR = 1.5
        B, T, D = x.shape
        E = router_w.shape[0]
        N = B * T
        C = max(math.ceil(CAPACITY_FACTOR * N / E), 1)
        x_flat = x.reshape(N, D)
        logits = x_flat @ router_w.T
        probs = jax.nn.softmax(logits, axis=-1)
        chosen_e = jnp.argmax(probs, axis=-1)
        chosen_p = jnp.max(probs, axis=-1)
        onehot = jax.nn.one_hot(chosen_e, E, dtype=jnp.float32)
        pos = jnp.take_along_axis(jnp.cumsum(onehot, axis=0), chosen_e[:, None], axis=1)[:, 0] - 1.0
        pos = pos.astype(jnp.int32)
        kept = pos < C
        pos_c = jnp.clip(pos, 0, C - 1)
        buf = jnp.zeros((E, C, D), dtype=x.dtype).at[chosen_e, pos_c].add(x_flat * kept[:, None].astype(x.dtype))
        h = jax.nn.gelu(jnp.einsum('ecd,edf->ecf', buf, w1) + b1[:, None, :], approximate=False)
        eo = jnp.einsum('ecf,efd->ecd', h, w2) + b2[:, None, :]
        y = eo[chosen_e, pos_c] * (chosen_p * kept.astype(x.dtype))[:, None]
        return y.reshape(B, T, D)

    def _L1_attn_ref(representations, Wc, bc, Wo, bo):
        import jax, jax.numpy as jnp
        import numpy as np
        N_INPUT = 128
        N_HEAD = 16
        ATT_DIM = N_INPUT // N_HEAD * N_HEAD
        V_DIM = N_INPUT // 2 * N_HEAD
        COMB_DIM = 2 * ATT_DIM + V_DIM
        SCALE = (N_INPUT // N_HEAD) ** 0.5
        B, T, D = representations.shape
        H = N_HEAD
        dh = ATT_DIM // H
        dv = V_DIM // H
        cp = jax.nn.leaky_relu(jnp.einsum('btd,cd->btc', representations, Wc) + bc)
        q = cp[..., :ATT_DIM].reshape(B, T, H, dh)
        k = cp[..., ATT_DIM:2 * ATT_DIM].reshape(B, T, H, dh)
        v = cp[..., 2 * ATT_DIM:].reshape(B, T, H, dv)
        scores = jnp.einsum('bqhd,bkhd->bhqk', q, k) / SCALE
        attn = jax.nn.softmax(scores, axis=-1)
        out = jnp.einsum('bhqk,bkhd->bqhd', attn, v).reshape(B, T, V_DIM)
        proj = jax.nn.leaky_relu(jnp.einsum('btv,dv->btd', out, Wo) + bo)
        return representations + proj

    def _L1_ffn_ref(x, Wr, br, W1, b1, W2, b2):
        import jax, jax.numpy as jnp
        import numpy as np
        TOP_K = 2

        def _moe(x, Wr, br, W1, b1, W2, b2):
            B, S, D = x.shape
            E = Wr.shape[1]
            xt = x.reshape(-1, D)
            logits = xt @ Wr + br
            top_vals, top_idx = jax.lax.top_k(logits, TOP_K)
            mask = jnp.zeros_like(logits, dtype=bool).at[jnp.arange(xt.shape[0])[:, None], top_idx].set(True)
            sparse_logits = jnp.where(mask, logits, -jnp.inf)
            gate = jax.nn.softmax(sparse_logits, axis=-1)
            h = jax.nn.relu(jnp.einsum('td,edh->teh', xt, W1) + b1)
            y = jnp.einsum('teh,ehd->ted', h, W2) + b2
            out = jnp.einsum('ted,te->td', y, gate)
            return out.reshape(B, S, D)
        return _moe(x, Wr, br, W1, b1, W2, b2)
    x = L0_attn_x
    x = x + _L0_attn_ref(_layernorm(x, axis=-1), L0_attn_W_DKV, L0_attn_W_UK, L0_attn_W_UV, L0_attn_W_UQ, L0_attn_W_O)
    x = x + _L0_ffn_ref(_layernorm(x, axis=-1), L0_ffn_router_w, L0_ffn_w1, L0_ffn_b1, L0_ffn_w2, L0_ffn_b2)
    x = x + _L1_attn_ref(_layernorm(x, axis=-1), L1_attn_Wc, L1_attn_bc, L1_attn_Wo, L1_attn_bo)
    x = x + _L1_ffn_ref(_layernorm(x, axis=-1), L1_ffn_Wr, L1_ffn_br, L1_ffn_W1, L1_ffn_b1, L1_ffn_W2, L1_ffn_b2)
    return x

_drawn_inputs = setup_inputs


def setup_inputs(seed=0):
    import zlib

    import numpy as np

    out = dict(_drawn_inputs(seed))
    spreads = {'L0_ffn_b1': (0.0, 0.588),
     'L0_ffn_b2': (0.0, 0.579),
     'L1_attn_bc': (0.0, 0.632),
     'L1_attn_bo': (0.0, 0.32),
     'L1_ffn_br': (0.0, 0.1),
     'L1_ffn_b1': (0.0, 0.31),
     'L1_ffn_b2': (0.0, 0.33)}
    factors = {'L0_attn_W_DKV': 8.0,
     'L0_attn_W_UK': 8.0,
     'L0_attn_W_UV': 8.0,
     'L0_attn_W_UQ': 8.0,
     'L0_attn_W_O': 8.0,
     'L0_ffn_w1': 2.786,
     'L0_ffn_w2': 2.799,
     'L1_attn_Wc': 56.3,
     'L1_attn_Wo': 5.273}
    for name, (base, spread) in spreads.items():
        noise = np.random.default_rng([zlib.crc32(name.encode()), seed]).standard_normal(out[name].shape)
        drawn = base * np.exp(spread * noise) if base else spread * noise
        out[name] = jnp.asarray(drawn.astype(out[name].dtype))
    for name, factor in factors.items():
        out[name] = (out[name] * factor).astype(out[name].dtype)
    return out
```

```python
from contextlib import ExitStack

import concourse.bass as bass
from concourse import mybir

ALU = mybir.AluOpType
ACT = mybir.ActivationFunctionType
AX = mybir.AxisListType
F32 = mybir.dt.float32
BF16 = mybir.dt.bfloat16

P = 128
D = 128
T = 512
B = 8
TT = T // P
NT = B * TT
HEADS = 16
PAIRS = HEADS // 2
DQ = 8
PARTS = 3
PRODS = 6
KQ = PRODS * DQ
KM = KQ + PARTS
EPS = 1e-5
MASKED = -1e30


def attention(nc, ctx, layer, X, MV, RSTD, C, w, scratch):
    causal = layer == 0
    DV = 8 if layer == 0 else 64
    scale = float(DQ) ** -0.5
    L = f"L{layer}_"
    identf, identb, maskq, maskk, bcast = C["identf"], C["identb"], C["maskq"], C["maskk"], C["bcast"]

    buffers = ExitStack()

    def sb(name, shape, dt=F32):
        return buffers.enter_context(nc.sbuf_tensor(L + name, shape, dt))

    def ps(name, shape):
        return buffers.enter_context(nc.psum_tensor(L + name, shape, F32))

    def sem(name):
        return ctx.enter_context(nc.semaphore(L + name))

    with buffers:
        XN = sb("xn", [P, 2, TT, D])
        XT = sb("xT", [P, T])
        QF = sb("qkf", [P, 2, T])
        QR = sb("qk_rest", [P, 2, T])
        QP = sb("qk_parts", [P, 2, PARTS, T], BF16)
        QA = sb("q_stack", [P, 2, PAIRS, T], BF16)
        KA = sb("k_stack", [P, 2, PAIRS, T], BF16)
        M = sb("neg_max", [P, 2, TT, 4])
        MR = sb("max_rest", [P, TT, 4])
        MP = sb("max_parts", [P, 2, TT, 4, PARTS], BF16)
        MT = sb("max_rows", [4 * PARTS, 2, T], BF16)
        PT = sb("probs", [P, 2, TT, 2, T])
        W = ps("work", [P, 2, T])
        S = ps("scores", [P, 2, 2, T])
        if layer == 0:
            WDKV = sb("w_dkv", [P, 32])
            WUK = sb("w_uk", [32, D])
            WUV = sb("w_uv", [32, D])
            WUQ = sb("w_uq", [P, D])
            WO = sb("w_o", [P, 4, D])
            CT = sb("ctxT", [P, 4, T])
            CKV = sb("c_kvT", [32, T])
            V = sb("v", [P, 2, TT, HEADS, 32])
            OU = sb("o_raw", [P, 2, T])
            RB = sb("recip", [P, 2, T])
            O = ps("o", [P, 2, T])
        else:
            WC = sb("w_c", [P, 256 + HEADS * DV])
            WO = sb("w_oT", [P, PAIRS, D])
            BQK = sb("b_qk", [P, 2])
            BV = sb("b_v", [P, 2, T])
            BO = sb("b_o", [P, 1])
            CT = sb("ctxT", [P, PAIRS, T])
            V = sb("v", [P, 2, TT, HEADS, DV])
            VB = sb("v_biased", [P, 2, T])
            PS = sb("prob_sums", [P, 2, 2, T])
            RB = sb("recip", [P, T])
            PJ = sb("proj", [P, T])
            PL = sb("proj_leaky", [P, T])
            ones64 = sb("ones64", [P, 64])
            O = ps("o", [P, T])
            SB = ps("sums", [P, T])

        weights = sem("weights")
        cleared = sem("cleared")
        ln_done = sem("ln_done")
        xt_done = sem("xt_done")
        ckv_done = sem("ckv_done")
        qk_raw = sem("qk_raw")
        rest_done = sem("rest_done")
        parts_done = sem("parts_done")
        spilled = sem("spilled")
        stacked = sem("stacked")
        v_done = sem("v_done")
        w_full = sem("w_full")
        w_free = sem("w_free")
        max_done = sem("max_done")
        mstep = sem("mstep")
        mp_done = sem("mp_done")
        mt_done = sem("mt_done")
        m_loaded = sem("m_loaded")
        s_full = sem("s_full")
        exp_done = sem("exp_done")
        pv_done = sem("pv_done")
        ct_done = sem("ct_done")
        x_done = sem("x_done")
        stat = sem("stat")
        if layer == 0:
            ou_done = sem("ou_done")
            rb_done = sem("rb_done")
        else:
            leaky = sem("leaky")
            ps_done = sem("ps_done")
            sb_done = sem("sb_done")
            rb_done = sem("rb_done")
            qb_done = sem("qb_done")
            pj_done = sem("pj_done")
            pl_done = sem("pl_done")

        if layer == 0:
            AUX = [(0, 1, "MT1", "cur"), (0, 2, "XT", "nxt"), (1, 0, "CQ", "nxt"), (1, 1, "KV", "nxt"),
                   (1, 2, "BC3", "lag"), (2, 1, "MT2", "cur"), (2, 2, "OUT", "lag"), (3, 2, "BC0", "cur"),
                   (4, 1, "MT3", "cur"), (5, 2, "BC1", "cur"), (6, 1, "MT0", "nxt"), (7, 2, "BC2", "cur")]
        else:
            AUX = [(0, 1, "MT1", "cur"), (0, 2, "XT", "nxt"), (1, 0, "PJ", "lag"), (1, 1, "QK", "nxt"),
                   (1, 3, "PTR", "lag"), (2, 1, "MT2", "cur"), (2, 0, "V0", "nxt"), (2, 2, "V1", "nxt"),
                   (3, 0, "V2", "nxt"), (3, 2, "V3", "nxt"), (4, 1, "MT3", "cur"), (6, 1, "MT0", "nxt")]

        def kinds(body):
            return {"first": {"nxt"}, "zero": {"cur", "nxt"}, "mid": {"cur", "nxt", "lag"},
                    "seven": {"cur", "lag"}, "tail": {"lag"}}[body]

        def job_list(body):
            jobs = []
            for p in range(PAIRS):
                for q in range(TT):
                    if ("cur" if p < 4 else "nxt") in kinds(body):
                        jobs.append(("S1", p, q))
                    jobs += [(n, p, q) for (pp, qq, n, k) in AUX if (pp, qq) == (p, q) and k in kinds(body)]
            return jobs

        JOBS = {k: job_list(k) for k in ("first", "zero", "mid", "seven", "tail")}

        def jobs_before(b):
            if isinstance(b, int) and b <= 0:
                return 0 if b < 0 else len(JOBS["first"])
            return (b - 1) * len(JOBS["mid"]) + len(JOBS["first"]) + len(JOBS["zero"])

        def job_before(body, b, name, p, q):
            if body == "tail":
                return (B - 2) * len(JOBS["mid"]) + sum(len(JOBS[k]) for k in ("first", "zero", "seven")) \
                    + JOBS[body].index((name, p, q))
            return jobs_before(b) + JOBS[body].index((name, p, q))

        def bodies(eng, run):
            run("first", -1, 1)
            run("zero", 0, 0)
            with eng.Fori(0, (B - 2) // 2) as i:
                run("mid", 2 * i + 1, 1)
                run("mid", 2 * i + 2, 0)
            run("seven", B - 1, 1)
            run("tail", B, 0)

        def wait_apart(eng, semaphore, value):
            value = value if isinstance(value, int) else eng.to_reg(value)
            eng.wait_ge(weights, LANDED)
            eng.wait_ge(semaphore, value)

        def aux_at(body, p, q):
            return [n for (pp, qq, n, k) in AUX if (pp, qq) == (p, q) and k in kinds(body)]

        LANDED = 16 * (8 if layer == 0 else 5)

        with nc.Block() as block:

            @block.sync
            def _(sp):
                if layer == 0:
                    sp.dma_start(WDKV[:], w["W_DKV"]).then_inc(weights, 16)
                    sp.dma_start(WUK[:], w["W_UK"]).then_inc(weights, 16)
                    sp.dma_start(WUV[:], w["W_UV"]).then_inc(weights, 16)
                    sp.dma_start(WUQ[:], w["W_UQ"]).then_inc(weights, 16)
                    sp.wait_ge(cleared, 1)
                    rows = w["W_O"].rearrange("(g j d) n -> j d g n", g=4, j=4)
                    for j in range(4):
                        sp.dma_start(WO[32 * j:32 * j + DV, :, :], rows[j]).then_inc(weights, 16)
                else:
                    sp.dma_start(WC[:], w["WcT"]).then_inc(weights, 16)
                    sp.dma_start(WO[:], w["WoT"].rearrange("(c p) n -> p c n", p=P)).then_inc(weights, 16)
                    sp.dma_start(BQK[:], w["bc"][0:256].rearrange("(a p) -> p a", p=P),
                                 allow_slow_non_contiguous=True).then_inc(weights, 16)
                    sp.dma_start(BO[:], w["bo"].rearrange("(p a) -> p a", a=1),
                                 allow_slow_non_contiguous=True).then_inc(weights, 16)
                    sp.dma_start(BV[:, :, :], w["bc"][256:].rearrange("(a h n) -> a h n", a=1, h=2)
                                 .broadcast_to([P, 2, T])).then_inc(weights, 16)
                    sp.wait_ge(cleared, 1)

                def max_rows(b, par, g):
                    n = 4 * b + g
                    wait_apart(sp, mt_done, n + 1)
                    for hh in range(4):
                        pair, half = 2 * g + hh // 2, 64 * (hh % 2)
                        sp.dma_start(QA[half + KQ:half + KM, par, pair, :],
                                     MT[PARTS * hh:PARTS * hh + PARTS, g % 2, :]).then_inc(m_loaded, 16)

                def body(kind, b, par):
                    k = kinds(kind)
                    nxt = 1 - par
                    if "cur" in k:
                        max_rows(b, par, 1)
                    if "nxt" in k:
                        wait_apart(sp, parts_done, b + 2)
                        sl = bass.ds(b + 1, 1) if not isinstance(b, int) else slice(b + 1, b + 2)
                        for a in range(2):
                            sp.dma_start(scratch[sl, a].rearrange("o i p t -> p (o i) t"),
                                         QP[:, a, :, :]).then_inc(spilled, 16)
                        wait_apart(sp, spilled, 32 * (b + 2))
                        if kind not in ("first", "zero"):
                            wait_apart(sp, s_full, 4 * PAIRS * b)
                        for half in range(2):
                            for a, dst in ((0, QA), (1, KA)):
                                src = scratch[sl, a].rearrange("o i (r h d) t -> o h i d r t", h=2, d=DQ)
                                src = src.rearrange("o h i d r t -> (o h) i d r t")[half]
                                row = 64 * half
                                if a == 0:
                                    for r0, n in ((0, 3), (3, 2), (5, 1)):
                                        for i in range(n):
                                            sp.dma_start(dst[row + DQ * (r0 + i):row + DQ * (r0 + i + 1), nxt, :, :],
                                                         src[i]).then_inc(stacked, 16)
                                else:
                                    for r0, i in enumerate((0, 0, 0, 1, 1, 2)):
                                        sp.dma_start(dst[row + DQ * r0:row + DQ * (r0 + 1), nxt, :, :],
                                                     src[i]).then_inc(stacked, 16)
                    if "cur" in k:
                        max_rows(b, par, 2)
                        max_rows(b, par, 3)
                    if "nxt" in k:
                        max_rows(b + 1, nxt, 0)

                bodies(sp, body)

            STACKED = 24 * 16
            MROWS = 4 * 16

            @block.gpsimd
            def _(pool):
                if layer == 0:
                    pool.memset(WO[:], 0.0).then_inc(cleared, 1)
                    pool.memset(V[:], 0.0).then_inc(rest_done, 1)
                    pool.wait_ge(rest_done, 1)
                    pool.memset(V[:, :, :, :, DV:DV + 1], 1.0).then_inc(cleared, 1)
                    pool.memset(KA[:], 1.0).then_inc(cleared, 1)
                else:
                    pool.memset(KA[:], 1.0).then_inc(cleared, 1)
                    pool.memset(ones64[:], 1.0).then_inc(cleared, 1)
                RS0 = 1 if layer == 0 else 0

                def split(b):
                    n = b + 1
                    wait_apart(pool, qk_raw, n)
                    if b is not None and not (isinstance(b, int) and b == 0):
                        wait_apart(pool, spilled, 32 * b)
                    pool.tensor_copy(QP[:, :, 0, :], QF[:, :, :]).then_inc(rest_done, 1)
                    pool.wait_ge(rest_done, RS0 + 3 * b + 1)
                    pool.tensor_tensor(QR[:, :, :], QF[:, :, :], QP[:, :, 0, :], ALU.subtract).then_inc(rest_done, 1)
                    wait_apart(pool, rest_done, RS0 + 3 * b + 2)
                    pool.tensor_copy(QP[:, :, 1, :], QR[:, :, :]).then_inc(rest_done, 1)
                    pool.wait_ge(rest_done, RS0 + 3 * b + 3)
                    pool.tensor_tensor(QP[:, :, 2, :], QR[:, :, :], QP[:, :, 1, :], ALU.subtract).then_inc(parts_done, 1)

                def split_max(b, g):
                    n = 4 * b + g
                    wait_apart(pool, max_done, n + 1)
                    if not (isinstance(b, int) and n < 2):
                        wait_apart(pool, mt_done, n - 1)
                    m, mp = M[:, g % 2], MP[:, g % 2]
                    pool.tensor_copy(mp[:, :, :, 0], m).then_inc(mstep, 1)
                    pool.wait_ge(mstep, 3 * n + 1)
                    pool.tensor_tensor(MR[:, :, :], m, mp[:, :, :, 0], ALU.subtract).then_inc(mstep, 1)
                    wait_apart(pool, mstep, 3 * n + 2)
                    pool.tensor_copy(mp[:, :, :, 1], MR[:, :, :]).then_inc(mstep, 1)
                    pool.wait_ge(mstep, 3 * n + 3)
                    pool.tensor_tensor(mp[:, :, :, 2], MR[:, :, :], mp[:, :, :, 1], ALU.subtract).then_inc(mp_done, 1)

                def sum_keys(b, p, par):
                    s = PAIRS * b + p
                    pp = p % 2
                    if not (isinstance(b, int) and s < 2):
                        pool.wait_ge(sb_done, s - 1)
                    for kt in range(1, TT):
                        pool.wait_ge(exp_done, 4 * s + kt + 1)
                        a = PT[:, pp, 0] if kt == 1 else PS[:, pp]
                        if kt > 1:
                            pool.wait_ge(ps_done, 3 * s + kt - 1)
                        pool.tensor_tensor(PS[:, pp], a, PT[:, pp, kt], ALU.add).then_inc(ps_done, 1)

                def context0(b, g):
                    n = 4 * b + g
                    pool.wait_ge(ou_done, n + 1)
                    pool.wait_ge(rb_done, n + 1)
                    if g == 0 and not (isinstance(b, int) and b == 0):
                        pool.wait_ge(x_done, b)
                    pool.tensor_tensor(CT[:, g, :], OU[:, g % 2, :], RB[:, g % 2, :], ALU.mult).then_inc(ct_done, 1)

                def body(kind, b, par):
                    k = kinds(kind)
                    for p in range(PAIRS):
                        if layer == 1 and "cur" in k:
                            sum_keys(b, p, par)
                        if p == 2 and "nxt" in k:
                            split(b + 1)
                        if p % 2 == 1:
                            g = (p // 2 + 2) % 4
                            if ("cur" if p < 4 else "nxt") in k:
                                split_max(b if p < 4 else b + 1, g)
                        if layer == 0:
                            if p == 1 and "lag" in k:
                                context0(b - 1, 3)
                            if p in (3, 5, 7) and "cur" in k:
                                context0(b, (p - 3) // 2)

                bodies(pool, body)

            @block.vector
            def _(dve):
                dve.wait_ge(weights, LANDED)

                def layernorm(b, par):
                    tile0 = b * TT
                    for t in range(TT):
                        if t == 0 and not (isinstance(b, int) and b < 2):
                            dve.wait_ge(xt_done, b - 1)
                        x = X[:, tile0 + t, :] if isinstance(b, int) else X[:, bass.ds(tile0 + t, 1), :]
                        mean = MV[:, tile0 + t, 0:1] if isinstance(b, int) else \
                            MV[:, bass.ds(tile0 + t, 1), 0:1].rearrange("p a o -> p (a o)")
                        rstd = RSTD[:, tile0 + t:tile0 + t + 1] if isinstance(b, int) else \
                            RSTD[:, bass.ds(tile0 + t, 1)]
                        o = XN[:, par, t, :] if isinstance(b, int) else XN[:, par, t:t + 1, :]
                        dve.tensor_scalar(o, x, mean, rstd, ALU.subtract, ALU.mult).then_inc(ln_done, 1)
                    if layer == 1:
                        dve.wait_ge(ln_done, 5 * b + 4)
                        xs = X[:, bass.ds(tile0, TT), :]
                        dve.tensor_tensor(xs, xs, XN[:, par], ALU.add).then_inc(ln_done, 1)

                def max_unit(kind, b, p, q):
                    w = ("cur" if p < 4 else "nxt")
                    if w not in kinds(kind):
                        return
                    j = job_before(kind, b, "S1", p, q)
                    bb, pair = (b, p + 4) if p < 4 else (b + 1, p - 4)
                    n = 4 * bb + pair // 2
                    if q == 0 and pair % 2 == 0 and not (isinstance(bb, int) and n < 2):
                        dve.wait_ge(mp_done, n - 1)
                    dve.wait_ge(w_full, j + 1)
                    width = (q + 1) * P if causal else T
                    i = dve.tensor_reduce(M[:, (pair // 2) % 2, q, 2 * (pair % 2):2 * (pair % 2) + 2],
                                          W[:, :, 0:width], AX.X, ALU.max, negate=True)
                    i.then_inc(w_free, 1)
                    if q == TT - 1 and pair % 2 == 1:
                        dve.wait_ge(w_free, j + 1)
                        dve.nop().then_inc(max_done, 1)

                def residual(kind, b, name, p, q):
                    j = job_before(kind, b + 1, name, p, q)
                    dve.wait_ge(w_full, j + 1)
                    xs = X[:, bass.ds(b * TT, TT), :]
                    if layer == 1:
                        dve.wait_ge(ln_done, 5 * b + 5)
                    dve.tensor_tensor(xs, xs, W[:, 0, :].rearrange("p (t d) -> p t d", t=TT), ALU.add).then_inc(w_free, 1)
                    wait_apart(dve, w_free, j + 1)
                    for t in range(TT):
                        dve.bn_stats(ST[:, t, :], X[:, bass.ds(b * TT + t, 1), :]).then_inc(stat, 1)
                    wait_apart(dve, stat, 8 * b + 4)
                    for t in range(TT):
                        dve.bn_aggr(AG[:, t, :], ST[:, t, :]).then_inc(stat, 1)
                    dve.wait_ge(stat, 8 * b + 8)
                    dve.tensor_copy(MV[:, bass.ds(b * TT, TT), :], AG[:, :, :]).then_inc(x_done, 1)

                ST, AG = C["stats"], C["aggregate"]

                def body(kind, b, par):
                    k = kinds(kind)
                    nxt = 1 - par
                    for p in range(PAIRS):
                        if p == 0 and "nxt" in k:
                            layernorm(b + 1, nxt)
                        for q in range(TT):
                            max_unit(kind, b, p, q)
                            if layer == 1 and q == 2:
                                if (p > 0 and "cur" in k) or (p == 0 and "lag" in k):
                                    s1 = PAIRS * b + p
                                    dve.wait_ge(sb_done, s1)
                                    if not (isinstance(b, int) and s1 < 2):
                                        dve.wait_ge(ct_done, s1 - 1)
                                    dve.reciprocal(RB[:, :], SB[:, :]).then_inc(rb_done, 1)
                            for n in aux_at(kind, p, q):
                                j = job_before(kind, b, n, p, q)
                                if n.startswith("BC"):
                                    g = int(n[2])
                                    m = 4 * (b - 1 if g == 3 else b) + g
                                    dve.wait_ge(w_full, j + 1)
                                    if not (isinstance(b, int) and m < 2):
                                        dve.wait_ge(ct_done, m - 1)
                                    dve.reciprocal(RB[:, g % 2, :], W[:, 0, :]).then_inc(w_free, 1)
                                    dve.wait_ge(w_free, j + 1)
                                    dve.nop().then_inc(rb_done, 1)
                                elif n in ("OUT", "PTR"):
                                    residual(kind, b - 1, n, p, q)
                                elif n == "QK":
                                    dve.wait_ge(qb_done, 2 * b + 4)
                                    if not (isinstance(b, int) and b < 0):
                                        dve.wait_ge(parts_done, b + 1)
                                    dve.scalar_tensor_tensor(QF[:, :, :], QR2[:, :, :], 0.01, QR2[:, :, :],
                                                             ALU.mult, ALU.max).then_inc(qk_raw, 1)
                                elif n == "PJ":
                                    dve.wait_ge(pj_done, b)
                                    dve.scalar_tensor_tensor(PL[:, :], PJ[:, :], 0.01, PJ[:, :],
                                                             ALU.mult, ALU.max).then_inc(pl_done, 1)
                                elif n[0] == "V":
                                    t = int(n[1])
                                    dve.wait_ge(w_full, j + 1)
                                    dve.wait_ge(weights, LANDED)
                                    if t == 0 and not (isinstance(b, int) and b < 1):
                                        dve.wait_ge(pv_done, PAIRS * b)
                                    if not (isinstance(b, int) and b < 0 and t == 0):
                                        dve.wait_ge(v_done, TT * (b + 1) + t)
                                    dve.tensor_tensor(VB[:, :, :], W[:, :, :], BV[:, :, :], ALU.add).then_inc(w_free, 1)
                                    dve.wait_ge(w_free, j + 1)
                                    dve.scalar_tensor_tensor(V[:, nxt, t].rearrange("p h d -> p (h d)"),
                                                             VB[:, :, :].rearrange("p a n -> p (a n)"), 0.01,
                                                             VB[:, :, :].rearrange("p a n -> p (a n)"),
                                                             ALU.mult, ALU.max).then_inc(v_done, 1)
                        if layer == 1 and ((p > 0 and "cur" in k) or (p == 0 and "lag" in k)):
                            s1 = PAIRS * b + p
                            pair = (p - 1) % PAIRS
                            dve.wait_ge(pv_done, s1)
                            dve.wait_ge(rb_done, s1)
                            if pair == 0 and not (isinstance(b, int) and b == 0):
                                dve.wait_ge(pj_done, b)
                            dve.tensor_tensor(CT[:, pair, :], O[:, :], RB[:, :], ALU.mult).then_inc(ct_done, 1)

                QR2 = C["qk_biased"]
                bodies(dve, body)

            @block.scalar
            def _(act):
                QR2 = C["qk_biased"]

                def body(kind, b, par):
                    k = kinds(kind)
                    nxt = 1 - par
                    for p in range(PAIRS):
                        s = PAIRS * b + p
                        for q in range(TT):
                            if "cur" in k:
                                act.wait_ge(s_full, 4 * s + q + 1)
                                if q == 0 and not (isinstance(b, int) and s < 2):
                                    act.wait_ge(pv_done, s - 1)
                                    if layer == 1:
                                        act.wait_ge(ps_done, 3 * (s - 1))
                                q0 = q * P if causal else 0
                                act.activation(PT[:, p % 2, q, :, q0:T], S[:, q % 2, :, q0:T], ACT.Exp,
                                               scale=scale).then_inc(exp_done, 1)
                            if layer == 0 and q == 1 and p % 2 == 1:
                                if (p == 1 and "lag" in k) or (p > 1 and "cur" in k):
                                    m = 4 * b + (p - 3) // 2
                                    act.wait_ge(pv_done, 2 * m + 2)
                                    if not (isinstance(b, int) and m < 2):
                                        act.wait_ge(ct_done, m - 1)
                                    act.activation(OU[:, ((p - 3) // 2) % 2, :], O[:, ((p - 3) // 2) % 2, :],
                                                   ACT.Copy).then_inc(ou_done, 1)
                            for n in aux_at(kind, p, q):
                                j = job_before(kind, b, n, p, q)
                                if n.startswith("BC") or n in ("OUT", "PTR") or n[0] == "V":
                                    continue
                                act.wait_ge(w_full, j + 1)
                                if n.startswith("MT"):
                                    g = int(n[2])
                                    m = 4 * (b + 1 if g == 0 else b) + g
                                    if not (isinstance(b, int) and m < 2):
                                        act.wait_ge(m_loaded, MROWS * (m - 1))
                                    act.activation(MT[:, g % 2, :], W[0:4 * PARTS, 0, 0:T // 2].bitcast(BF16),
                                                   ACT.Copy).then_inc(w_free, 1)
                                    act.wait_ge(w_free, j + 1)
                                    act.nop().then_inc(mt_done, 1)
                                elif n == "XT":
                                    act.activation(XT[:, :], W[:, 0, :], ACT.Copy).then_inc(w_free, 1)
                                    act.wait_ge(w_free, j + 1)
                                    act.nop().then_inc(xt_done, 1)
                                elif n == "CQ":
                                    if not (isinstance(b, int) and b < 0):
                                        act.wait_ge(parts_done, b + 1)
                                    act.activation(CKV[:, :], W[0:32, 0, :], ACT.Copy).then_inc(ckv_done, 1)
                                    act.activation(QF[:, 0, :], W[:, 1, :], ACT.Copy).then_inc(w_free, 1)
                                elif n == "KV":
                                    if isinstance(b, int) and b < 1:
                                        act.wait_ge(cleared, 2)
                                    else:
                                        act.wait_ge(pv_done, PAIRS * b)
                                    act.activation(V[:, nxt, :, :, 0:DV],
                                                   W[:, 1, :].rearrange("p (t h d) -> p t h d", t=TT, d=DV),
                                                   ACT.Copy).then_inc(v_done, 1)
                                    act.activation(QF[:, 1, :], W[:, 0, :], ACT.Copy).then_inc(w_free, 1)
                                    act.wait_ge(w_free, j + 1)
                                    act.nop().then_inc(qk_raw, 1)
                                elif n == "QK":
                                    act.wait_ge(weights, LANDED)
                                    if not (isinstance(b, int) and b < 0):
                                        act.wait_ge(qk_raw, b + 1)
                                    act.activation(QR2[:, 0, :], W[:, 0, :], ACT.Identity,
                                                   bias=BQK[:, 0:1]).then_inc(qb_done, 1)
                                    act.activation(QR2[:, 1, :], W[:, 1, :], ACT.Identity,
                                                   bias=BQK[:, 1:2]).then_inc(w_free, 1)
                                    act.wait_ge(w_free, j + 1)
                                    act.nop().then_inc(qb_done, 1)
                                elif n == "PJ":
                                    if not (isinstance(b, int) and b < 2):
                                        act.wait_ge(pl_done, b - 1)
                                    act.activation(PJ[:, :], W[:, 0, :], ACT.Identity, bias=BO[:, 0:1]).then_inc(w_free, 1)
                                    act.wait_ge(w_free, j + 1)
                                    act.nop().then_inc(pj_done, 1)

                bodies(act, body)

            @block.tensor
            def _(pe):
                pe.wait_ge(weights, LANDED)
                pe.wait_ge(cleared, 3 if layer == 0 else 2)

                def s1(kind, b, par, p, q):
                    w = ("cur" if p < 4 else "nxt")
                    if w not in kinds(kind):
                        return
                    j = job_before(kind, b, "S1", p, q)
                    bb, pb, pair = (b, par, p + 4) if p < 4 else (b + 1, 1 - par, p - 4)
                    if j_positive(kind, j):
                        pe.wait_ge(w_free, j)
                    if p == 4 and q == 0:
                        pe.wait_ge(stacked, STACKED * (bb + 1))
                    width = (q + 1) * P if causal else T
                    for half in range(2):
                        r = 64 * half
                        i = pe.matmul(W[:, half, 0:width], QA[r:r + KQ, pb, pair, q * P:(q + 1) * P],
                                      KA[r:r + KQ, pb, pair, 0:width], start=True, stop=not causal)
                    if causal:
                        for half in range(2):
                            i = pe.matmul(W[:, half, q * P:(q + 1) * P], identb[:, :], maskq[:, :],
                                          start=False, stop=True)
                    i.then_inc(w_full, 1)

                def j_positive(kind, j):
                    return not (isinstance(j, int) and j == 0)

                def s2(b, par, p, q):
                    s = PAIRS * b + p
                    if not (isinstance(b, int) and s == 0 and q < 2):
                        pe.wait_ge(exp_done, 4 * s + q - 1)
                    if q == 0 and p % 2 == 0:
                        pe.wait_ge(m_loaded, MROWS * (4 * b + p // 2 + 1))
                    q0 = q * P if causal else 0
                    for half in range(2):
                        r = 64 * half
                        i = pe.matmul(S[:, q % 2, half, q0:T], KA[r:r + KM, par, p, q * P:(q + 1) * P],
                                      QA[r:r + KM, par, p, q0:T], start=True, stop=not causal)
                    if causal:
                        for half in range(2):
                            i = pe.matmul(S[:, q % 2, half, q0:q0 + P], identb[:, :], maskk[:, :],
                                          start=False, stop=True)
                    i.then_inc(s_full, 1)

                def pv(b, par, p, q):
                    s = PAIRS * b + p
                    pe.wait_ge(exp_done, 4 * s + q + 1)
                    if p == 0 and q == 0:
                        pe.wait_ge(v_done, (b + 1) * (1 if layer == 0 else TT))
                    q0 = q * P if causal else 0
                    for half in range(2):
                        if layer == 0:
                            if q == 0 and half == 0 and p % 2 == 0 and not (isinstance(b, int) and s < 4):
                                pe.wait_ge(ou_done, 4 * b + p // 2 - 1)
                            r = 32 * (2 * (p % 2) + half)
                            i = pe.matmul(O[r:r + 32, (p // 2) % 2, q0:T], V[:, par, q, 2 * p + half, :],
                                          PT[:, p % 2, q, half, q0:T], start=(q == 0), stop=(q == TT - 1))
                        else:
                            if q == 0 and half == 0 and not (isinstance(b, int) and s == 0):
                                pe.wait_ge(ct_done, s)
                            r = 64 * half
                            i = pe.matmul(O[r:r + 64, :], V[:, par, q, 2 * p + half, :],
                                          PT[:, p % 2, q, half, :], start=(q == 0), stop=(q == TT - 1))
                    if q == TT - 1:
                        i.then_inc(pv_done, 1)

                def sums(b, p):
                    s = PAIRS * b + p
                    pe.wait_ge(ps_done, 3 * (s + 1))
                    if not (isinstance(b, int) and s == 0):
                        pe.wait_ge(rb_done, s)
                    for half in range(2):
                        i = pe.matmul(SB[64 * half:64 * half + 64, :], ones64[:, :], PS[:, p % 2, half, :],
                                      start=True, stop=True)
                    i.then_inc(sb_done, 1)

                def aux(kind, b, par, n, p, q):
                    j = job_before(kind, b, n, p, q)
                    if j_positive(kind, j):
                        pe.wait_ge(w_free, j)
                    nxt = 1 - par
                    if n.startswith("MT"):
                        g = int(n[2])
                        m = 4 * (b + 1 if g == 0 else b) + g
                        pe.wait_ge(mp_done, m + 1)
                        for t in range(TT):
                            i = pe.transpose(W[0:4 * PARTS, 0, t * 64:t * 64 + 64].bitcast(BF16),
                                             MP[:, g % 2, t].rearrange("p h i -> p (h i)"), identb[:, :])
                    elif n == "XT":
                        pe.wait_ge(ln_done, 4 * (b + 2) if layer == 0 else 5 * (b + 1) + 4)
                        for t in range(TT):
                            i = pe.transpose(W[:, 0, t * P:(t + 1) * P], XN[:, nxt, t, :], identf[:, :])
                    elif n == "CQ":
                        pe.wait_ge(xt_done, b + 2)
                        pe.matmul(W[0:32, 0, :], WDKV[:, :], XT[:, :], start=True, stop=True)
                        i = pe.matmul(W[:, 1, :], WUQ[:, :], XT[:, :], start=True, stop=True)
                    elif n == "KV":
                        pe.wait_ge(ckv_done, b + 2)
                        pe.matmul(W[:, 0, :], WUK[:, :], CKV[:, :], start=True, stop=True)
                        for t in range(TT):
                            i = pe.matmul(W[:, 1, t * P:(t + 1) * P], CKV[:, t * P:(t + 1) * P], WUV[:, :],
                                          start=True, stop=True)
                    elif n == "QK":
                        pe.wait_ge(xt_done, b + 2)
                        for a in range(2):
                            i = pe.matmul(W[:, a, :], WC[:, a * P:(a + 1) * P], XT[:, :], start=True, stop=True)
                    elif n[0] == "V":
                        t = int(n[1])
                        for a in range(2):
                            i = pe.matmul(W[:, a, :], XT[:, t * P:(t + 1) * P], WC[:, 256 + a * T:256 + (a + 1) * T],
                                          start=True, stop=True)
                    elif n.startswith("BC"):
                        g = int(n[2])
                        m = 4 * (b - 1 if g == 3 else b) + g
                        pe.wait_ge(ou_done, m + 1)
                        i = pe.matmul(W[:, 0, :], bcast[:, :], OU[:, g % 2, :], start=True, stop=True)
                    elif n == "OUT":
                        pe.wait_ge(ct_done, 4 * b)
                        for t in range(TT):
                            for g in range(4):
                                i = pe.matmul(W[:, 0, t * P:(t + 1) * P], CT[:, g, t * P:(t + 1) * P], WO[:, g, :],
                                              start=(g == 0), stop=(g == 3))
                    elif n == "PJ":
                        pe.wait_ge(ct_done, PAIRS * b)
                        for c in range(PAIRS):
                            i = pe.matmul(W[:, 0, :], WO[:, c, :], CT[:, c, :], start=(c == 0), stop=(c == PAIRS - 1))
                    elif n == "PTR":
                        pe.wait_ge(pl_done, b)
                        for t in range(TT):
                            i = pe.transpose(W[:, 0, t * P:(t + 1) * P], PL[:, t * P:(t + 1) * P], identf[:, :])
                    i.then_inc(w_full, 1)

                def body(kind, b, par):
                    k = kinds(kind)
                    for p in range(PAIRS):
                        lagging = (p > 0 and "cur" in k) or (p == 0 and "lag" in k)
                        lb, lpar, lp = (b, par, p - 1) if p > 0 else (b - 1, 1 - par, PAIRS - 1)
                        for q in range(TT):
                            if "cur" in k:
                                s2(b, par, p, q)
                            s1(kind, b, par, p, q)
                            if lagging:
                                pv(lb, lpar, lp, q)
                                if layer == 1 and q == 1:
                                    sums(lb, lp)
                            for n in aux_at(kind, p, q):
                                aux(kind, b, par, n, p, q)

                bodies(pe, body)


E = 8
H = 512
HC = H // P
CAP = 768
TS = 256
SC = TS // P


def moe(nc, ctx, layer, X, MV, RSTD, C, w, xbuf, ybuf, tag):
    TOP = 1 if layer == 0 else 2
    NTILES = E * CAP // TS if layer == 0 else TOP * B * T // TS + E
    SLOTS = NTILES * TS
    func = ACT.Gelu if layer == 0 else ACT.Relu
    L = f"F{layer}_"
    buffers = ExitStack()

    def sb(name, shape, dt=F32):
        return buffers.enter_context(nc.sbuf_tensor(L + name, shape, dt))

    def sem(name):
        return ctx.enter_context(nc.semaphore(L + name))

    U32, I32 = mybir.dt.uint32, mybir.dt.int32
    with buffers:
        SLOT = sb("slot", [P, TOP, NT], U32)
        BACK = sb("back", [P, TOP, NT], U32)
        GATE = sb("gate", [P, TOP, NT])
        OWNER = sb("owner", [1, NTILES], I32)
        routing = ExitStack()

        def rb(name, shape, dt=F32):
            return routing.enter_context(nc.sbuf_tensor(L + name, shape, dt))

        with routing:
            XN = rb("xn", [P, NT, D])
            XT = rb("xT", [P, 2, T])
            LG = rb("logits", [P, NT, E])
            WR = rb("w_router", [P, E])
            BR = rb("b_router", [P, E])
            OH = rb("onehot", [P, TOP, NT, E])
            OHB = rb("onehot_b", [P, NT, E], BF16)
            TMP = rb("tmp", [P, NT, E])
            TM2 = rb("tmp2", [P, NT, E])
            CNT = rb("counts", [P, 2, NT + 1, E])
            TOPV = rb("top", [P, TOP, NT])
            PICK = rb("pick", [P, NT])
            RANK = rb("rank", [P, NT])
            KEEP = rb("keep", [P, NT])
            W8 = rb("w8", [P, E])
            ECAP = rb("ecap", [P, E])
            SPILL = rb("spill", [P, NT])
            TRI = rb("tri", [P, P], BF16)
            ONE = rb("one", [P, P], BF16)
            TRIF = rb("trif", [P, P])
            TN = rb("tiles", [P, 2, E])
            TNI = rb("tiles_i", [P, E], I32)
            JT = rb("jt", [1, NTILES])
            JC = rb("jc", [1, NTILES, E])
            JI = rb("jf", [1, NTILES])
            with (nc.psum_tensor(L + "xt_ps", [P, 2, T], F32) as XTP,
                  nc.psum_tensor(L + "lg_ps", [P, 2, T], F32) as LGP,
                  nc.psum_tensor(L + "rk_ps", [P, 2, T], F32) as RKP):
                w_in = sem("w_in")
                ln = sem("ln")
                xtp = sem("xtp")
                xts = sem("xts")
                lgp = sem("lgp")
                lgs = sem("lgs")
                const = sem("const")
                st = sem("st")
                chosen = sem("chosen")
                expd = sem("expd")
                ranked = sem("ranked")
                slotted = sem("slotted")
                scat = sem("scat")

                def sl(t, n):
                    return bass.ds(t, n)

                with nc.Block() as block:
                    @block.sync
                    def _(sp):
                        sp.dma_start(WR[:, :], w["router"]).then_inc(w_in, 16)
                        if layer == 1:
                            sp.dma_start(BR[:, :], w["br"].rearrange("(a e) -> a e", a=1)
                                         .broadcast_to([P, E])).then_inc(w_in, 16)

                    @block.gpsimd
                    def _(pool):
                        pool.iota(W8[:, :], pattern=[[-1, E]], base=E, channel_multiplier=0,
                                  allow_small_or_imprecise_dtypes=True).then_inc(const, 1)
                        pool.iota(ECAP[:, :], pattern=[[CAP, E]], base=0, channel_multiplier=0,
                                  allow_small_or_imprecise_dtypes=True).then_inc(const, 1)
                        pool.iota(SPILL[:, :], pattern=[[P, NT]], base=E * CAP, channel_multiplier=1,
                                  allow_small_or_imprecise_dtypes=True).then_inc(const, 1)
                        if layer == 1:
                            pool.iota(JI[:, :], pattern=[[1, NTILES]], base=0, channel_multiplier=0,
                                      allow_small_or_imprecise_dtypes=True).then_inc(const, 1)
                        else:
                            pool.iota(OWNER[:, :], pattern=[[1, E], [0, CAP // TS]], base=0,
                                      channel_multiplier=0).then_inc(const, 1)
                        pool.memset(ONE[:, :], 1.0).then_inc(const, 1)
                        pool.memset(TRIF[:, :], 1.0).then_inc(const, 1)
                        pool.memset(CNT[:, :, 0:1, :], 0.0).then_inc(const, 1)
                        pool.wait_ge(const, 7)
                        pool.affine_select(out=TRI[:, :], in_=TRIF[:, :], compare_op=ALU.is_gt, fill=0.0,
                                           base=0, pattern=[[1, P]], channel_multiplier=-1).then_inc(const, 1)
                        pool.wait_ge(C["zeroed"], 16 * ZERO_DMAS)
                        pool.wait_ge(slotted, 1)
                        for t in range(NT):
                            for k in range(TOP):
                                pool.indirect_dma_start(
                                    xbuf, bass.IndirectOffsetOnAxis(ap=SLOT[:, k, t:t + 1], axis=0),
                                    XN[:, t, :], None).then_inc(scat, 16)
                        pool.wait_ge(scat, 16 * NT * TOP)

                    @block.vector
                    def _(dve):
                        def batch(b, par, first):
                            for t in range(TT):
                                tile = b * TT + t
                                dve.tensor_scalar(XN[:, sl(tile, 1), :], X[:, sl(tile, 1), :],
                                                  MV[:, sl(tile, 1), 0:1].rearrange("p a o -> p (a o)"),
                                                  RSTD[:, sl(tile, 1)], ALU.subtract, ALU.mult).then_inc(ln, 1)

                        def logits(b, par):
                            dve.wait_ge(lgp, b + 1)
                            o = LG[:, sl(b * TT, TT), :]
                            i = LGP[:, par, 0:TT * E].rearrange("p (t e) -> p t e", t=TT)
                            if layer == 0:
                                dve.tensor_copy(o, i).then_inc(lgs, 1)
                            else:
                                dve.tensor_tensor(o, i, BR[:, :].rearrange("p (a e) -> p a e", a=1)
                                                  .broadcast_to([P, TT, E]), ALU.add).then_inc(lgs, 1)

                        dve.wait_ge(w_in, 16 * (1 + layer))
                        batch(0, 0, True)
                        batch(1, 1, True)
                        with dve.Fori(0, (B - 2) // 2) as i:
                            for u in range(2):
                                logits(2 * i + u, u)
                                batch(2 * i + u + 2, u, False)
                        logits(B - 2, 0)
                        logits(B - 1, 1)

                        n = [0]

                        def step(ins):
                            ins.then_inc(st, 1)
                            n[0] += 1
                            dve.wait_ge(st, n[0])

                        dve.wait_ge(lgs, B)
                        dve.wait_ge(const, 8)

                        def over_e(x):
                            return x.rearrange("p (t a) -> p t a", a=1).broadcast_to([P, NT, E])

                        def over_t(x):
                            return x.rearrange("p (a e) -> p a e", a=1).broadcast_to([P, NT, E])

                        src = LG
                        for k in range(TOP):
                            step(dve.tensor_reduce(TOPV[:, k, :], src[:, :, :], AX.X, ALU.max))
                            step(dve.tensor_tensor(TMP[:, :, :], src[:, :, :], over_e(TOPV[:, k, :]), ALU.is_equal))
                            step(dve.tensor_tensor(TMP[:, :, :], TMP[:, :, :], over_t(W8[:, :]), ALU.mult))
                            step(dve.tensor_reduce(PICK[:, :], TMP[:, :, :], AX.X, ALU.max))
                            step(dve.tensor_tensor(OH[:, k], over_t(W8[:, :]), over_e(PICK[:, :]), ALU.is_equal))
                            if k + 1 < TOP:
                                step(dve.scalar_tensor_tensor(TM2[:, :, :].rearrange("p t e -> p (t e)"),
                                                              OH[:, k].rearrange("p t e -> p (t e)"), -3e38,
                                                              LG[:, :, :].rearrange("p t e -> p (t e)"),
                                                              ALU.mult, ALU.add))
                                src = TM2
                        if layer == 0:
                            step(dve.tensor_copy(OHB[:, :, :], OH[:, 0]))
                            dve.tensor_tensor(TMP[:, :, :], LG[:, :, :], over_e(TOPV[:, 0, :]), ALU.subtract)\
                                .then_inc(chosen, 1)
                        else:
                            step(dve.tensor_tensor(OHB[:, :, :], OH[:, 0], OH[:, 1], ALU.add))
                            dve.tensor_tensor(PICK[:, :], TOPV[:, 1, :], TOPV[:, 0, :], ALU.subtract).then_inc(chosen, 1)
                        dve.wait_ge(chosen, 1)
                        dve.wait_ge(expd, 1)
                        if layer == 0:
                            step(dve.tensor_reduce(PICK[:, :], TM2[:, :, :], AX.X, ALU.add))
                            step(dve.reciprocal(GATE[:, 0, :], PICK[:, :]))
                        else:
                            step(dve.tensor_scalar(RANK[:, :], KEEP[:, :], 1.0, None, ALU.add))
                            step(dve.reciprocal(GATE[:, 0, :], RANK[:, :]))
                            step(dve.tensor_tensor(GATE[:, 1, :], GATE[:, 0, :], KEEP[:, :], ALU.mult))
                        dve.wait_ge(ranked, 1)
                        step(dve.tensor_copy(CNT[:, 0, 1:NT + 1, :],
                                             RKP[:, 1, 0:NT * E].rearrange("p (t e) -> p t e", e=E)))
                        cur, d = 0, 1
                        while d < NT + 1:
                            nx = 1 - cur
                            step(dve.tensor_tensor(CNT[:, nx, d:NT + 1, :], CNT[:, cur, d:NT + 1, :],
                                                   CNT[:, cur, 0:NT + 1 - d, :], ALU.add))
                            step(dve.tensor_copy(CNT[:, nx, 0:d, :], CNT[:, cur, 0:d, :]))
                            cur, d = nx, 2 * d
                        total = CNT[:, cur, NT, :]
                        step(dve.tensor_tensor(TMP[:, :, :], RKP[:, 0, 0:NT * E].rearrange("p (t e) -> p t e", e=E),
                                               CNT[:, cur, 0:NT, :], ALU.add))
                        if layer == 0:
                            step(dve.tensor_tensor(TM2[:, :, :], TMP[:, :, :], OH[:, 0], ALU.mult))
                            step(dve.tensor_reduce(RANK[:, :], TM2[:, :, :], AX.X, ALU.add))
                            step(dve.tensor_scalar(KEEP[:, :], RANK[:, :], CAP - 0.5, None, ALU.is_lt))
                            step(dve.tensor_tensor(GATE[:, 0, :], GATE[:, 0, :], KEEP[:, :], ALU.mult))
                            step(dve.tensor_tensor(TM2[:, :, :], OH[:, 0], over_t(ECAP[:, :]), ALU.mult))
                            step(dve.tensor_reduce(PICK[:, :], TM2[:, :, :], AX.X, ALU.add))
                            step(dve.tensor_tensor(RANK[:, :], RANK[:, :], PICK[:, :], ALU.add))
                            step(dve.tensor_tensor(RANK[:, :], RANK[:, :], SPILL[:, :], ALU.subtract))
                            step(dve.tensor_tensor(RANK[:, :], RANK[:, :], KEEP[:, :], ALU.mult))
                            step(dve.tensor_tensor(RANK[:, :], RANK[:, :], SPILL[:, :], ALU.add))
                            step(dve.tensor_scalar(BACK[:, 0, :], RANK[:, :], float(E * CAP - 1), None, ALU.min))
                            dve.tensor_copy(SLOT[:, 0, :], RANK[:, :]).then_inc(slotted, 1)
                        else:
                            step(dve.tensor_scalar(TN[:, 0, :], total, 1.0 / TS, (TS - 1.0 - (TS - 1) / 2.0) / TS,
                                                   ALU.mult, ALU.add))
                            step(dve.tensor_copy(TNI[:, :], TN[:, 0, :]))
                            step(dve.tensor_copy(TN[:, 0, :], TNI[:, :]))
                            cur, d = 0, 1
                            while d < E:
                                nx = 1 - cur
                                step(dve.tensor_tensor(TN[:, nx, d:E], TN[:, cur, d:E], TN[:, cur, 0:E - d], ALU.add))
                                step(dve.tensor_copy(TN[:, nx, 0:d], TN[:, cur, 0:d]))
                                cur, d = nx, 2 * d
                            ends = TN[:, cur, :]
                            step(dve.tensor_tensor(JC[:, :, :], JI[:, :].rearrange("p (j a) -> p j a", a=1)
                                                   .broadcast_to([1, NTILES, E]),
                                                   ends[0:1].rearrange("p (a e) -> p a e", a=1)
                                                   .broadcast_to([1, NTILES, E]), ALU.is_ge))
                            step(dve.tensor_reduce(JT[:, :], JC[:, :, :], AX.X, ALU.add))
                            step(dve.tensor_scalar(OWNER[:, :], JT[:, :], E - 1.0, None, ALU.min))
                            step(dve.tensor_copy(ECAP[:, :], TNI[:, :]))
                            step(dve.tensor_tensor(ECAP[:, :], ends, ECAP[:, :], ALU.subtract))
                            step(dve.tensor_scalar(ECAP[:, :], ECAP[:, :], float(TS), None, ALU.mult))
                            step(dve.tensor_tensor(TMP[:, :, :], TMP[:, :, :], over_t(ECAP[:, :]), ALU.add))
                            for k in range(TOP):
                                step(dve.tensor_tensor(TM2[:, :, :], TMP[:, :, :], OH[:, k], ALU.mult))
                                step(dve.tensor_reduce(RANK[:, :], TM2[:, :, :], AX.X, ALU.add))
                                step(dve.tensor_copy(BACK[:, k, :], RANK[:, :]))
                                i = dve.tensor_copy(SLOT[:, k, :], RANK[:, :])
                                if k + 1 < TOP:
                                    step(i)
                                else:
                                    i.then_inc(slotted, 1)

                    @block.scalar
                    def _(act):
                        def copy_out(b, par, first):
                            act.wait_ge(xtp, b + 1)
                            if not first:
                                act.wait_ge(lgp, b - 1)
                            act.activation(XT[:, par, :], XTP[:, par, :], ACT.Copy).then_inc(xts, 1)

                        copy_out(0, 0, True)
                        copy_out(1, 1, True)
                        with act.Fori(0, (B - 2) // 2) as i:
                            for u in range(2):
                                copy_out(2 * i + u + 2, u, False)
                        act.wait_ge(chosen, 1)
                        if layer == 0:
                            act.activation(TM2[:, :, :], TMP[:, :, :], ACT.Exp).then_inc(expd, 1)
                        else:
                            act.activation(KEEP[:, :], PICK[:, :], ACT.Exp).then_inc(expd, 1)

                    @block.tensor
                    def _(pe):
                        def transpose(b, par, first):
                            pe.wait_ge(ln, TT * (b + 1))
                            if not first:
                                pe.wait_ge(xts, b - 1)
                            for t in range(TT):
                                i = pe.transpose(XTP[:, par, t * P:(t + 1) * P],
                                                 XN[:, b * TT + t, :], C["identf"][:, :])
                            i.then_inc(xtp, 1)

                        def project(b, par, first):
                            pe.wait_ge(xts, b + 1)
                            if not first:
                                pe.wait_ge(lgs, b - 1)
                            for t in range(TT):
                                i = pe.matmul(LGP[:, par, t * E:(t + 1) * E], XT[:, par, t * P:(t + 1) * P],
                                              WR[:, :], start=True, stop=True)
                            i.then_inc(lgp, 1)

                        pe.wait_ge(w_in, 16 * (1 + layer))
                        transpose(0, 0, True)
                        for b in range(B):
                            if b + 1 < B:
                                transpose(b + 1, (b + 1) % 2, b < 1)
                            project(b, b % 2, b < 2)
                        pe.wait_ge(chosen, 1)
                        pe.wait_ge(const, 8)
                        ohb = OHB[:, :, :].rearrange("p t e -> p (t e)")
                        pe.matmul(RKP[:, 0, 0:NT * E], TRI[:, :], ohb, start=True, stop=True)
                        pe.matmul(RKP[:, 1, 0:NT * E], ONE[:, :], ohb, start=True, stop=True).then_inc(ranked, 1)

        work = ExitStack()

        def wb(name, shape, dt=F32):
            return work.enter_context(nc.sbuf_tensor(L + name, shape, dt))

        def wp(name, shape):
            return work.enter_context(nc.psum_tensor(L + name, shape, F32))

        with work:
            W1 = wb("w1", [P, 3, H + HC])
            W2 = wb("w2", [P, 3, HC, D])
            B2 = wb("b2", [P, 3, D])
            XS = wb("xs", [P, 3, SC, D])
            XST = wb("xsT", [P, 2, TS])
            HT = wb("hT", [P, 2, HC, TS])
            YS = wb("ys", [P, 2, SC, D])
            TP = wp("tp", [P, 2, T])
            HP = wp("hp", [P, 4, T])
            YP = wp("yp", [P, 2, T])
            loaded = [sem(f"loaded{i}") for i in range(3)]
            tp_full = sem("tp_full")
            xst_done = sem("xst_done")
            h_full = sem("h_full")
            h_done = sem("h_done")
            y_full = sem("y_full")
            y_done = sem("y_done")
            y_out = [sem(f"y_out{u}") for u in range(2)]
            NL = 4

            with nc.Block() as block:
                @block.sync
                def _(sp):
                    def load(j, m, first):
                        if not first:
                            sp.wait_ge(y_done, j - 2)
                        e = sp.value_load(OWNER[0:1, j:j + 1] if isinstance(j, int) else OWNER[0:1, bass.ds(j, 1)],
                                          min_val=0, max_val=E - 1)
                        es = bass.ds(e, 1)
                        js = bass.ds(j, 1)
                        sp.dma_start(XS[:, m, :, :], xbuf[0:SLOTS].rearrange("(j c p) d -> j p c d", c=SC, p=P)[js]
                                     .rearrange("o p c d -> (o p) c d")).then_inc(loaded[m], 16)
                        sp.dma_start(W1[:, m, :], w["w1"][es].rearrange("o p n -> (o p) n")).then_inc(loaded[m], 16)
                        sp.dma_start(W2[:, m, :, :], w["w2"][es].rearrange("o (c p) d -> (o p) c d", p=P))\
                            .then_inc(loaded[m], 16)
                        sp.dma_start(B2[:, m, :], w["b2"][es].broadcast_to([P, D])).then_inc(loaded[m], 16)

                    for j in range(3):
                        load(j, j, True)
                    with sp.Fori(1, NTILES // 3) as i:
                        for m in range(3):
                            load(3 * i + m, m, False)
                    for j in range(NTILES // 3 * 3, NTILES):
                        load(j, j % 3, False)

                def tiles(eng, run):
                    full = (NTILES - 2) // 6 * 6
                    for j in range(6):
                        run(j, j % 3, j % 2, j, (j + 1) // 3, (j - 1) // 2)
                    with eng.Fori(1, full // 6) as i:
                        for v in range(6):
                            run(6 * i + v, v % 3, v % 2, None, 2 * i + (v + 1) // 3, 3 * i + (v - 1) // 2)
                    for j in range(full, NTILES):
                        run(j, j % 3, j % 2, j, (j + 1) // 3, (j - 1) // 2)

                @block.tensor
                def _(pe):
                    def transpose(j, m, u, uses):
                        pe.wait_ge(loaded[m], NL * 16 * (uses + 1))
                        if not (isinstance(j, int) and j < 2):
                            pe.wait_ge(xst_done, j - 1)
                        for c in range(SC):
                            i = pe.transpose(TP[:, u, c * P:(c + 1) * P], XS[:, m, c, :], C["identf"][:, :])
                        i.then_inc(tp_full, 1)

                    def hidden(j, m, u):
                        pe.wait_ge(xst_done, j + 1)
                        for half in range(2):
                            if not (isinstance(j, int) and j < 2):
                                pe.wait_ge(h_done, 4 * j - 8 + 2 * half + 2)
                            for a in range(2):
                                c = 2 * half + a
                                i = pe.matmul(HP[:, 2 * u + half, a * TS:(a + 1) * TS], W1[:, m, c * P:(c + 1) * P],
                                              XST[:, u, :], start=True, stop=True)
                            i.then_inc(h_full, 1)

                    def result(j, m, u):
                        pe.wait_ge(h_done, 4 * j + 4)
                        if not (isinstance(j, int) and j < 2):
                            pe.wait_ge(y_done, j - 1)
                        for s in range(SC):
                            for c in range(HC):
                                i = pe.matmul(YP[:, u, s * P:(s + 1) * P], HT[:, u, c, s * P:(s + 1) * P],
                                              W2[:, m, c, :], start=(c == 0), stop=(c == HC - 1))
                        i.then_inc(y_full, 1)

                    def run(j, m, u, k, uses, stores):
                        if k != NTILES - 1:
                            transpose(j + 1, (m + 1) % 3, 1 - u, uses)
                        hidden(j, m, u)
                        if k != 0:
                            result(j - 1, (m - 1) % 3, 1 - u)

                    transpose(0, 0, 0, 0)
                    tiles(pe, run)
                    result(NTILES - 1, (NTILES - 1) % 3, (NTILES - 1) % 2)

                @block.scalar
                def _(act):
                    def run(j, m, u, k, uses, stores):
                        for c in range(HC):
                            act.wait_ge(h_full, 2 * j + c // 2 + 1)
                            if c == 0 and not (isinstance(j, int) and j < 2):
                                act.wait_ge(y_full, j - 1)
                            act.activation(HT[:, u, c, :], HP[:, 2 * u + c // 2, (c % 2) * TS:(c % 2 + 1) * TS],
                                           func, bias=W1[:, m, H + c:H + c + 1]).then_inc(h_done, 1)

                    tiles(act, run)

                @block.vector
                def _(dve):
                    def rows(j, m, u):
                        dve.wait_ge(tp_full, j + 1)
                        if not (isinstance(j, int) and j < 2):
                            dve.wait_ge(h_full, 2 * j - 2)
                        dve.tensor_copy(XST[:, u, :], TP[:, u, 0:TS]).then_inc(xst_done, 1)

                    def result(j, m, u, stores):
                        dve.wait_ge(y_full, j + 1)
                        if not (isinstance(j, int) and j < 2):
                            dve.wait_ge(y_out[u], 16 * stores)
                        dve.tensor_tensor(YS[:, u, :, :], YP[:, u, 0:TS].rearrange("p (s d) -> p s d", s=SC),
                                          B2[:, m, :].rearrange("p (a d) -> p a d", a=1).broadcast_to([P, SC, D]),
                                          ALU.add).then_inc(y_done, 1)

                    def run(j, m, u, k, uses, stores):
                        if k != NTILES - 1:
                            rows(j + 1, (m + 1) % 3, 1 - u)
                        if k != 0:
                            result(j - 1, (m - 1) % 3, 1 - u, stores)

                    rows(0, 0, 0)
                    tiles(dve, run)
                    result(NTILES - 1, (NTILES - 1) % 3, (NTILES - 1) % 2, (NTILES - 1) // 2)

                @block.gpsimd
                def _(pool):
                    def run(j, m, u, k, uses, stores):
                        pool.wait_ge(y_done, j + 1)
                        js = bass.ds(j, 1)
                        pool.dma_start(ybuf.rearrange("(j c p) d -> j p c d", c=SC, p=P)[js]
                                       .rearrange("o p c d -> (o p) c d"), YS[:, u, :, :]).then_inc(y_out[u], 16)

                    tiles(pool, run)
                    for u in range(2):
                        pool.wait_ge(y_out[u], 16 * (NTILES // 2))

        with nc.sbuf_tensor(L + "yg", [P, TOP, NT, D], F32) as YG:
            got = [sem(f"got{b}") for b in range(B)]
            added = sem("added")
            aggr = sem("aggr")
            stored = sem("stored")
            with nc.Block() as block:
                @block.gpsimd
                def _(pool):
                    for t in range(NT):
                        for k in range(TOP):
                            pool.indirect_dma_start(YG[:, k, t, :], None, ybuf,
                                                    bass.IndirectOffsetOnAxis(ap=BACK[:, k, t:t + 1], axis=0))\
                                .then_inc(got[t // TT], 16)

                @block.vector
                def _(dve):
                    n = 0
                    for b in range(B):
                        dve.wait_ge(got[b], 16 * TT * TOP)
                        for k in range(TOP):
                            if k:
                                dve.wait_ge(added, TT * (TOP * b + k))
                            for t in range(b * TT, b * TT + TT):
                                dve.scalar_tensor_tensor(X[:, t, :], YG[:, k, t, :], GATE[:, k, t:t + 1], X[:, t, :],
                                                         ALU.mult, ALU.add).then_inc(added, 1)
                        if layer == 0:
                            dve.wait_ge(added, TT * TOP * (b + 1))
                            for t in range(TT):
                                dve.bn_stats(C["stats"][:, t, :], X[:, b * TT + t, :]).then_inc(aggr, 1)
                            dve.wait_ge(aggr, n + TT)
                            for t in range(TT):
                                dve.bn_aggr(MV[:, b * TT + t, :], C["stats"][:, t, :]).then_inc(aggr, 1)
                            n += 2 * TT
                            dve.wait_ge(aggr, n)

                if layer == 1:
                    @block.sync
                    def _(sp):
                        for b in range(B):
                            sp.wait_ge(added, TT * TOP * (b + 1))
                            sp.dma_start(C["out"][:, b * TT:(b + 1) * TT, :],
                                         X[:, b * TT:(b + 1) * TT, :]).then_inc(stored, 16)
                        sp.wait_ge(stored, 16 * B)


ZERO_ROWS = 1024
ZERO_DMAS = (E * CAP + 2 * B * T + E * TS) // ZERO_ROWS


def program(nc, a, out):
    with ExitStack() as ctx:
        def sb(name, shape, dt=F32):
            return ctx.enter_context(nc.sbuf_tensor(name, shape, dt))

        def sem(name):
            return ctx.enter_context(nc.semaphore(name))

        X = sb("x", [P, NT, D])
        MV = sb("mean_var", [P, NT, 2])
        RSTD = sb("rstd", [P, NT])
        C = {
            "identf": sb("identf", [P, P]), "identb": sb("identb", [P, P], BF16),
            "maskq": sb("maskq", [P, P], BF16), "maskk": sb("maskk", [P, P], BF16),
            "bcast": sb("bcast", [P, P]), "stats": sb("stats", [P, TT, 6]),
            "aggregate": sb("aggregate", [P, TT, 2]),
            "qk_biased": sb("qk_biased", [P, 2, T]),
            "root": sb("root", [P, NT]), "root2": sb("root2", [P, NT]), "eps": sb("eps", [P, 1]),
        }
        scratch = [nc.dram_tensor(f"qk_scratch{i}", [B, 2, PARTS, P, T], BF16).ap() for i in range(2)]

        xbuf = [nc.dram_tensor("x_slots0", [E * CAP + B * T, D], F32).ap(),
                nc.dram_tensor("x_slots1", [2 * B * T + E * TS, D], F32).ap()]
        ybuf = [nc.dram_tensor("y_slots0", [E * CAP, D], F32).ap(),
                nc.dram_tensor("y_slots1", [2 * B * T + E * TS, D], F32).ap()]
        C["zero"] = sb("zero", [P, ZERO_ROWS // P, D])
        C["zeroed"] = sem("zeroed")
        zero_set = sem("zero_set")

        x_in = a["L0_attn_x"].rearrange("b (t p) d -> p (b t) d", p=P)
        out_v = out.rearrange("b (t p) d -> p (b t) d", p=P)

        def rstd(tag, load):
            x_in_done = [sem(f"{tag}_x_in{c}") for c in range(B)] if load else None
            step = sem(f"{tag}_rstd_step")
            rooted = sem(f"{tag}_rooted")
            const = sem(f"{tag}_const")
            with nc.Block() as block:
                if load:
                    @block.sync
                    def _(sp):
                        for c in range(B):
                            sp.dma_start(X[:, c * TT:(c + 1) * TT, :],
                                         x_in[:, c * TT:(c + 1) * TT, :]).then_inc(x_in_done[c], 16)
                        sp.wait_ge(zero_set, 1)
                        for buf, rows in ((xbuf[0], E * CAP), (xbuf[1], 2 * B * T + E * TS)):
                            for r in range(0, rows, ZERO_ROWS):
                                sp.dma_start(buf[r:r + ZERO_ROWS].rearrange("(p c) d -> p c d", p=P),
                                             C["zero"][:, :, :]).then_inc(C["zeroed"], 16)

                    @block.gpsimd
                    def _(pool):
                        pool.memset(C["zero"][:], 0.0).then_inc(zero_set, 1)
                        pool.memset(C["eps"][:], EPS).then_inc(const, 1)
                        for m in ("identf", "identb", "maskq", "maskk", "bcast"):
                            pool.memset(C[m][:], 0.0).then_inc(const, 1)
                        pool.wait_ge(const, 6)
                        for m in ("identf", "identb"):
                            pool.affine_select(out=C[m][:, :], in_=C[m][:, :], compare_op=ALU.not_equal, fill=1.0,
                                               base=0, pattern=[[-1, P]], channel_multiplier=1).then_inc(const, 1)
                        pool.affine_select(out=C["maskq"][:, :], in_=C["maskq"][:, :], compare_op=ALU.is_ge,
                                           fill=MASKED, base=0, pattern=[[-1, P]], channel_multiplier=1)\
                            .then_inc(const, 1)
                        pool.affine_select(out=C["maskk"][:, :], in_=C["maskk"][:, :], compare_op=ALU.is_ge,
                                           fill=MASKED, base=0, pattern=[[1, P]], channel_multiplier=-1)\
                            .then_inc(const, 1)
                        bc = C["bcast"][:, :].rearrange("p (j r) -> p j r", j=4)
                        pool.affine_select(out=bc, in_=bc, compare_op=ALU.not_equal, fill=1.0, base=-DQ,
                                           pattern=[[-32, 4], [0, 32]], channel_multiplier=1).then_inc(const, 1)

                @block.vector
                def _(dve):
                    n = 0
                    if load:
                        for c in range(B):
                            dve.wait_ge(x_in_done[c], 16)
                            for t in range(TT):
                                dve.bn_stats(C["stats"][:, t, :], X[:, c * TT + t, :]).then_inc(step, 1)
                            dve.wait_ge(step, n + TT)
                            for t in range(TT):
                                dve.bn_aggr(MV[:, c * TT + t, :], C["stats"][:, t, :]).then_inc(step, 1)
                            n += 2 * TT
                            dve.wait_ge(step, n)
                    dve.wait_ge(rooted, 1)
                    dve.reciprocal(RSTD[:, :], C["root"][:, :]).then_inc(step, 1)
                    dve.wait_ge(step, n + 1)
                    dve.tensor_tensor(C["root"][:, :], RSTD[:, :], RSTD[:, :], ALU.mult).then_inc(step, 1)
                    dve.tensor_scalar(C["root2"][:, :], MV[:, :, 1], EPS, None, ALU.add).then_inc(step, 1)
                    dve.wait_ge(step, n + 3)
                    dve.tensor_tensor(C["root"][:, :], C["root"][:, :], C["root2"][:, :], ALU.mult).then_inc(step, 1)
                    dve.wait_ge(step, n + 4)
                    dve.tensor_scalar(C["root"][:, :], C["root"][:, :], -0.5, 1.5, ALU.mult, ALU.add)\
                        .then_inc(step, 1)
                    dve.wait_ge(step, n + 5)
                    dve.tensor_tensor(RSTD[:, :], RSTD[:, :], C["root"][:, :], ALU.mult).then_inc(step, 1)
                    dve.wait_ge(step, n + 6)

                @block.scalar
                def _(act):
                    if load:
                        act.wait_ge(const, 1)
                        act.wait_ge(step, 2 * NT)
                    act.activation(C["root"][:, :], MV[:, :, 1], ACT.Sqrt, bias=C["eps"][:, 0:1]).then_inc(rooted, 1)

        C["out"] = out_v
        rstd("start", True)
        if STAGES & 1:
            attention(nc, ctx, 0, X, MV, RSTD, C,
                      {k[8:]: v for k, v in a.items() if k.startswith("L0_attn")}, scratch[0])
            rstd("ffn0", False)
        if STAGES & 2:
            moe(nc, ctx, 0, X, MV, RSTD, C, {k[7:]: v for k, v in a.items() if k.startswith("L0_ffn")},
                xbuf[0], ybuf[0], "ffn0")
            rstd("attn1", False)
        if STAGES & 4:
            attention(nc, ctx, 1, X, MV, RSTD, C,
                      {k[8:]: v for k, v in a.items() if k.startswith("L1_attn")}, scratch[1])
        if STAGES & 8:
            rstd("ffn1", False)
            moe(nc, ctx, 1, X, MV, RSTD, C, {k[7:]: v for k, v in a.items() if k.startswith("L1_ffn")},
                xbuf[1], ybuf[1], "ffn1")
        else:
            stored = sem("stored")
            with nc.Block() as block:
                @block.sync
                def _(sp):
                    sp.dma_start(out_v, X[:, :, :]).then_inc(stored, 16)
                    sp.wait_ge(stored, 16)


STAGES = 15


def kernel(**inputs):
    import numpy as _np
    import concourse.bacc as _bacc
    from concourse import mybir as _mybir
    from concourse.bass_utils import run_bass_kernel_spmd as _run

    laid = {k: _np.ascontiguousarray(v) for k, v in inputs.items()}
    laid["L1_attn_WcT"] = _np.ascontiguousarray(laid.pop("L1_attn_Wc").T)
    laid["L1_attn_WoT"] = _np.ascontiguousarray(laid.pop("L1_attn_Wo").T)
    laid["L0_ffn_router"] = _np.ascontiguousarray(laid.pop("L0_ffn_router_w").T)
    laid["L1_ffn_router"] = laid.pop("L1_ffn_Wr")
    for layer, w1, b1 in (("L0_ffn_", "w1", "b1"), ("L1_ffn_", "W1", "b1")):
        e, d, h = laid[layer + w1].shape
        bias = laid.pop(layer + b1).reshape(e, h // d, d).transpose(0, 2, 1)
        laid[layer + "w1"] = _np.ascontiguousarray(_np.concatenate([laid.pop(layer + w1), bias], axis=2))
    laid["L1_ffn_w2"] = laid.pop("L1_ffn_W2")
    nc = _bacc.Bacc("TRN2", target_bir_lowering=False, num_devices=1)
    arrays, aps = {}, {}
    for name, v in laid.items():
        arrays[f"in_{name}"] = v
        aps[name] = nc.dram_tensor(f"in_{name}", v.shape, _mybir.dt.from_np(v.dtype), kind="ExternalInput").ap()
    out = nc.dram_tensor("out", (B, T, D), F32, kind="ExternalOutput").ap()
    program(nc, aps, out)
    r = _run(nc, [arrays], core_ids=[0])
    return r.results[0]["out"]
```

```python
from contextlib import ExitStack

import concourse.bass as bass
from concourse import mybir

ALU = mybir.AluOpType
ACT = mybir.ActivationFunctionType
AX = mybir.AxisListType
F32 = mybir.dt.float32
BF16 = mybir.dt.bfloat16

P = 128
D = 128
T = 512
B = 8
TT = T // P
NT = B * TT
HEADS = 16
PAIRS = HEADS // 2
DQ = 8
PARTS = 3
PRODS = 6
KQ = PRODS * DQ
KM = KQ + PARTS
EPS = 1e-5
MASKED = -1e30
EXP_AND_LN = 6


def attention(nc, ctx, layer, X, MV, RSTD, C, w, scratch):
    causal = layer == 0
    DV = 8 if layer == 0 else 64
    scale = float(DQ) ** -0.5
    L = f"L{layer}_"
    identf, identb, maskq, maskk, bcast = C["identf"], C["identb"], C["maskq"], C["maskk"], C["bcast"]

    buffers = ExitStack()

    def sb(name, shape, dt=F32):
        return buffers.enter_context(nc.sbuf_tensor(L + name, shape, dt))

    def ps(name, shape):
        return buffers.enter_context(nc.psum_tensor(L + name, shape, F32))

    def sem(name):
        return ctx.enter_context(nc.semaphore(L + name))

    with buffers:
        XN = sb("xn", [P, 2, TT, D])
        XT = sb("xT", [P, T])
        QF = sb("qkf", [P, 2, T])
        QR = sb("qk_rest", [P, 2, T])
        QP = sb("qk_parts", [P, 2, PARTS, T], BF16)
        QA = sb("q_stack", [P, 2, PAIRS, T], BF16)
        KA = sb("k_stack", [P, 2, PAIRS, T], BF16)
        M = sb("neg_max", [P, 2, TT, 4])
        MR = sb("max_rest", [P, TT, 4])
        MP = sb("max_parts", [P, 2, TT, 4, PARTS], BF16)
        MT = sb("max_rows", [2 * PARTS, 2, 2, T], BF16)
        PT = sb("probs", [P, 2, TT, 2, T])
        WORK = ps("work", [P, 2, 2, T])
        S = ps("scores", [P, 2, T])
        if layer == 0:
            WDKV = sb("w_dkv", [P, 32])
            WUK = sb("w_uk", [32, D])
            WUV = sb("w_uv", [32, D])
            WUQ = sb("w_uq", [P, D])
            WO = sb("w_o", [P, 4, D])
            CT = sb("ctxT", [P, 4, T])
            CKV = sb("c_kvT", [32, T])
            V = sb("v", [P, 2, TT, HEADS, 32])
            OU = sb("o_raw", [P, 2, T])
            RB = sb("recip", [P, 2, T])
            LS = sb("log_sum", [P, T])
            R0 = sb("recip0", [P, T])
            N1 = sb("newton", [P, T])
            O = ps("o", [P, 2, T])
        else:
            WC = sb("w_c", [P, 256 + HEADS * DV])
            WO = sb("w_oT", [P, PAIRS, D])
            BQK = sb("b_qk", [P, 2])
            BV = sb("b_v", [P, 2, T])
            BO = sb("b_o", [P, 1])
            CT = sb("ctxT", [P, PAIRS, T])
            V = sb("v", [P, 2, TT, HEADS, DV])
            VB = sb("v_biased", [P, 2, T])
            PS = sb("prob_sums", [P, 2, 2, T])
            RB = sb("recip", [P, T])
            LS = sb("log_sum", [P, T])
            R0 = sb("recip0", [P, T])
            N1 = sb("newton", [P, T])
            PJ = sb("proj", [P, T])
            PL = sb("proj_leaky", [P, T])
            ones64 = sb("ones64", [P, 64])
            O = ps("o", [P, T])
            SB = ps("sums", [P, T])

        weights = sem("weights")
        cleared = sem("cleared")
        ln_done = sem("ln_done")
        xt_done = sem("xt_done")
        ckv_done = sem("ckv_done")
        qk_raw = sem("qk_raw")
        rest_done = sem("rest_done")
        rounded = sem("rounded")
        parts_done = sem("parts_done")
        spilled = sem("spilled")
        stacked = sem("stacked")
        v_done = sem("v_done")
        w_full = [sem(f"w_full{i}") for i in range(2)]
        w_free = [sem(f"w_free{i}") for i in range(2)]
        ls_done = sem("ls_done")
        r0_done = sem("r0_done")
        n1_done = sem("n1_done")
        max_done = sem("max_done")
        mstep = sem("mstep")
        mp_done = sem("mp_done")
        mt_done = sem("mt_done")
        m_loaded = sem("m_loaded")
        s_full = sem("s_full")
        exp_done = sem("exp_done")
        pv_done = sem("pv_done")
        ct_done = sem("ct_done")
        x_done = sem("x_done")
        stat = sem("stat")
        if layer == 0:
            ou_done = sem("ou_done")
            rb_done = sem("rb_done")
        else:
            leaky = sem("leaky")
            ps_done = sem("ps_done")
            sb_done = sem("sb_done")
            rb_done = sem("rb_done")
            qb_done = sem("qb_done")
            pj_done = sem("pj_done")
            pl_done = sem("pl_done")

        if layer == 0:
            AUX = [(0, 0, "XT", "nxt"), (0, 1, "MT1", "cur"), (0, 2, "CQ", "nxt"), (1, 0, "KV", "nxt"),
                   (1, 2, "BC3", "lag"), (2, 1, "MT2", "cur"), (2, 2, "OUT", "lag"), (3, 2, "BC0", "cur"),
                   (4, 1, "MT3", "cur"), (5, 2, "BC1", "cur"), (6, 1, "MT0", "nxt"), (7, 2, "BC2", "cur")]
        else:
            AUX = [(0, 0, "XT", "nxt"), (0, 1, "MT1", "cur"), (0, 2, "QK", "nxt"), (1, 0, "PJ", "lag"),
                   (1, 3, "PTR", "lag"), (2, 1, "MT2", "cur"), (2, 0, "V0", "nxt"), (2, 2, "V1", "nxt"),
                   (3, 0, "V2", "nxt"), (3, 2, "V3", "nxt"), (4, 1, "MT3", "cur"), (6, 1, "MT0", "nxt")]

        def kinds(body):
            return {"first": {"nxt"}, "zero": {"cur", "nxt"}, "mid": {"cur", "nxt", "lag"},
                    "seven": {"cur", "lag"}, "tail": {"lag"}}[body]

        def job_list(body):
            jobs = []
            for p in range(PAIRS):
                for q in range(TT):
                    if ("cur" if p < 4 else "nxt") in kinds(body):
                        jobs.append(("S1", p, q))
                    jobs += [(n, p, q) for (pp, qq, n, k) in AUX if (pp, qq) == (p, q) and k in kinds(body)]
            return jobs

        JOBS = {k: job_list(k) for k in ("first", "zero", "mid", "seven", "tail")}

        MID = len(JOBS["mid"])
        assert MID % 2 == 0

        def turn(body, b, name, p, q):
            before = JOBS[body].index((name, p, q))
            if body != "first":
                before += len(JOBS["first"])
            if body in ("mid", "seven", "tail"):
                before += len(JOBS["zero"])
            if body in ("seven", "tail"):
                before += (B - 2) * MID
            if body == "tail":
                before += len(JOBS["seven"])
            uses = before // 2
            return before % 2, uses if body != "mid" else (b - 1) * (MID // 2) + uses

        def bodies(eng, run):
            run("first", -1, 1)
            run("zero", 0, 0)
            with eng.Fori(0, (B - 2) // 2) as i:
                run("mid", 2 * i + 1, 1)
                run("mid", 2 * i + 2, 0)
            run("seven", B - 1, 1)
            run("tail", B, 0)

        def wait_apart(eng, semaphore, value):
            value = value if isinstance(value, int) else eng.to_reg(value)
            eng.wait_ge(weights, LANDED)
            eng.wait_ge(semaphore, value)

        def aux_at(body, p, q):
            return [n for (pp, qq, n, k) in AUX if (pp, qq) == (p, q) and k in kinds(body)]

        LANDED = 16 * (8 if layer == 0 else 5)

        STACKED = 12 * 16
        SPILLED = 4 * 16
        RS0 = 1 if layer == 0 else 0
        MROWS = 2 * 16

        with nc.Block() as block:

            @block.sync
            def _(sp):
                if layer == 0:
                    sp.dma_start(WDKV[:], w["W_DKV"]).then_inc(weights, 16)
                    sp.dma_start(WUK[:], w["W_UK"]).then_inc(weights, 16)
                    sp.dma_start(WUV[:], w["W_UV"]).then_inc(weights, 16)
                    sp.dma_start(WUQ[:], w["W_UQ"]).then_inc(weights, 16)
                    sp.wait_ge(cleared, 1)
                    rows = w["W_O"].rearrange("(g j d) n -> j d g n", g=4, j=4)
                    for j in range(4):
                        sp.dma_start(WO[32 * j:32 * j + DV, :, :], rows[j]).then_inc(weights, 16)
                else:
                    sp.dma_start(WC[:], w["WcT"]).then_inc(weights, 16)
                    sp.dma_start(WO[:], w["WoT"].rearrange("(c p) n -> p c n", p=P)).then_inc(weights, 16)
                    sp.dma_start(BQK[:], w["bqk"].rearrange("(a p) -> p a", p=P),
                                 allow_slow_non_contiguous=True).then_inc(weights, 16)
                    sp.dma_start(BO[:], w["bo"].rearrange("(p a) -> p a", a=1),
                                 allow_slow_non_contiguous=True).then_inc(weights, 16)
                    sp.dma_start(BV[:, :, :], w["bc"][256:].rearrange("(a h n) -> a h n", a=1, h=2)
                                 .broadcast_to([P, 2, T])).then_inc(weights, 16)
                    sp.wait_ge(cleared, 1)

                def max_rows(b, par, g):
                    n = 4 * b + g
                    wait_apart(sp, mt_done, n + 1)
                    for half in range(2):
                        row = 64 * half + KQ
                        sp.dma_start(QA[row:row + PARTS, par, 2 * g:2 * g + 2, :],
                                     MT[PARTS * half:PARTS * half + PARTS, g % 2, :, :]).then_inc(m_loaded, 16)

                def body(kind, b, par):
                    k = kinds(kind)
                    nxt = 1 - par
                    if "cur" in k:
                        max_rows(b, par, 1)
                    if "nxt" in k:
                        wait_apart(sp, parts_done, b + 2)
                        sl = bass.ds(b + 1, 1)
                        for a in range(2):
                            for half in range(2):
                                sp.dma_start(scratch[sl, a, half].rearrange("o i r t -> r (o i) t"),
                                             QP[64 * half:64 * half + 64, a, :, :]).then_inc(spilled, 16)
                        wait_apart(sp, spilled, SPILLED * (b + 2))
                        if kind not in ("first", "zero"):
                            wait_apart(sp, s_full, 8 * PAIRS * b)
                        for half in range(2):
                            for a, dst in ((0, QA), (1, KA)):
                                src = scratch[sl, a, half].rearrange("o i (d r) t -> (o i) d (r t)", d=DQ)
                                for r0, n, i in ((0, 3, 0), (3, 2, 1), (5, 1, 2)):
                                    row = 64 * half + DQ * r0
                                    part = src[0:n] if a == 0 else src[i:i + 1].broadcast_to([n, DQ, PAIRS * T])
                                    sp.dma_start(dst[row:row + DQ * n, nxt, :, :].rearrange("n r t -> n (r t)"),
                                                 part).then_inc(stacked, 16)
                    if "cur" in k:
                        max_rows(b, par, 2)
                        max_rows(b, par, 3)
                    if "nxt" in k:
                        max_rows(b + 1, nxt, 0)

                bodies(sp, body)

            @block.gpsimd
            def _(pool):
                if layer == 0:
                    pool.memset(WO[:], 0.0).then_inc(cleared, 1)
                    pool.memset(V[:], 0.0).then_inc(rest_done, 1)
                    pool.wait_ge(rest_done, 1)
                    pool.memset(V[:, :, :, :, DV:DV + 1], 1.0).then_inc(cleared, 1)
                    pool.memset(KA[:], 1.0).then_inc(cleared, 1)
                else:
                    pool.memset(KA[:], 1.0).then_inc(cleared, 1)
                    pool.memset(ones64[:], 1.0).then_inc(cleared, 1)
                def split(b):
                    pool.wait_ge(rounded, 2 * b + 1)
                    pool.tensor_tensor(QR[:, :, :], QF[:, :, :], QP[:, :, 0, :], ALU.subtract).then_inc(rest_done, 1)
                    pool.wait_ge(rounded, 2 * b + 2)
                    pool.tensor_tensor(QP[:, :, 2, :], QR[:, :, :], QP[:, :, 1, :], ALU.subtract).then_inc(parts_done, 1)

                def split_max(b, g):
                    n = 4 * b + g
                    wait_apart(pool, max_done, n + 1)
                    if not (isinstance(b, int) and n < 2):
                        wait_apart(pool, mt_done, n - 1)
                    m, mp = M[:, g % 2], MP[:, g % 2]
                    pool.tensor_copy(mp[:, :, :, 0], m).then_inc(mstep, 1)
                    pool.wait_ge(mstep, 3 * n + 1)
                    pool.tensor_tensor(MR[:, :, :], m, mp[:, :, :, 0], ALU.subtract).then_inc(mstep, 1)
                    wait_apart(pool, mstep, 3 * n + 2)
                    pool.tensor_copy(mp[:, :, :, 1], MR[:, :, :]).then_inc(mstep, 1)
                    pool.wait_ge(mstep, 3 * n + 3)
                    pool.tensor_tensor(mp[:, :, :, 2], MR[:, :, :], mp[:, :, :, 1], ALU.subtract).then_inc(mp_done, 1)

                def sum_keys(b, p, par):
                    s = PAIRS * b + p
                    pp = p % 2
                    if not (isinstance(b, int) and s < 2):
                        pool.wait_ge(sb_done, s - 1)
                    for kt in range(1, TT):
                        pool.wait_ge(exp_done, 8 * s + 2 * kt + 2)
                        a = PT[:, pp, 0] if kt == 1 else PS[:, pp]
                        if kt > 1:
                            pool.wait_ge(ps_done, 3 * s + kt - 1)
                        pool.tensor_tensor(PS[:, pp], a, PT[:, pp, kt], ALU.add).then_inc(ps_done, 1)

                def context0(b, g):
                    n = 4 * b + g
                    pool.wait_ge(ou_done, n + 1)
                    pool.wait_ge(rb_done, n + 1)
                    if g == 0 and not (isinstance(b, int) and b == 0):
                        pool.wait_ge(x_done, b)
                    pool.tensor_tensor(CT[:, g, :], OU[:, g % 2, :], RB[:, g % 2, :], ALU.mult).then_inc(ct_done, 1)

                def body(kind, b, par):
                    k = kinds(kind)
                    for p in range(PAIRS):
                        if p == 1 and "nxt" in k:
                            split(b + 1)
                        if layer == 1 and "cur" in k:
                            sum_keys(b, p, par)
                        if p % 2 == 1:
                            g = (p // 2 + 2) % 4
                            if ("cur" if p < 4 else "nxt") in k:
                                split_max(b if p < 4 else b + 1, g)
                        if layer == 0:
                            if p == 1 and "lag" in k:
                                context0(b - 1, 3)
                            if p in (3, 5, 7) and "cur" in k:
                                context0(b, (p - 3) // 2)

                bodies(pool, body)

            @block.vector
            def _(dve):
                dve.wait_ge(weights, LANDED)

                def layernorm(b, par):
                    tile0 = b * TT
                    for t in range(TT):
                        if t == 0 and not (isinstance(b, int) and b < 2):
                            dve.wait_ge(xt_done, b - 1)
                        x = X[:, tile0 + t, :] if isinstance(b, int) else X[:, bass.ds(tile0 + t, 1), :]
                        mean = MV[:, tile0 + t, 0:1] if isinstance(b, int) else \
                            MV[:, bass.ds(tile0 + t, 1), 0:1].rearrange("p a o -> p (a o)")
                        rstd = RSTD[:, tile0 + t:tile0 + t + 1] if isinstance(b, int) else \
                            RSTD[:, bass.ds(tile0 + t, 1)]
                        o = XN[:, par, t, :] if isinstance(b, int) else XN[:, par, t:t + 1, :]
                        dve.tensor_scalar(o, x, mean, rstd, ALU.subtract, ALU.mult).then_inc(ln_done, 1)
                    if layer == 1:
                        dve.wait_ge(ln_done, 5 * b + 4)
                        xs = X[:, bass.ds(tile0, TT), :]
                        dve.tensor_tensor(xs, xs, XN[:, par], ALU.add).then_inc(ln_done, 1)

                def refine(sums, recip, n, used, read, reads):
                    dve.wait_ge(r0_done, n)
                    dve.tensor_tensor(N1[:, :], sums, R0[:, :], ALU.mult).then_inc(read, 1)
                    dve.wait_ge(read, reads)
                    if not (isinstance(used, int) and used < 1):
                        dve.wait_ge(ct_done, used)
                    dve.scalar_tensor_tensor(recip, N1[:, :], 2.0, R0[:, :], ALU.subtract, ALU.mult)\
                        .then_inc(rb_done, 1)

                def max_unit(kind, b, p, q):
                    w = ("cur" if p < 4 else "nxt")
                    if w not in kinds(kind):
                        return
                    h, u = turn(kind, b, "S1", p, q)
                    W = WORK[:, h]
                    bb, pair = (b, p + 4) if p < 4 else (b + 1, p - 4)
                    n = 4 * bb + pair // 2
                    if q == 0 and pair % 2 == 0 and not (isinstance(bb, int) and n < 2):
                        dve.wait_ge(mp_done, n - 1)
                    dve.wait_ge(w_full[h], u + 1)
                    width = (q + 1) * P if causal else T
                    i = dve.tensor_reduce(M[:, (pair // 2) % 2, q, 2 * (pair % 2):2 * (pair % 2) + 2],
                                          W[:, :, 0:width], AX.X, ALU.max, negate=True)
                    i.then_inc(w_free[h], 1)
                    if q == TT - 1 and pair % 2 == 1:
                        dve.wait_ge(w_free[h], u + 1)
                        dve.nop().then_inc(max_done, 1)

                def residual(kind, b, name, p, q):
                    h, u = turn(kind, b + 1, name, p, q)
                    W = WORK[:, h]
                    dve.wait_ge(w_full[h], u + 1)
                    xs = X[:, bass.ds(b * TT, TT), :]
                    if layer == 1:
                        dve.wait_ge(ln_done, 5 * b + 5)
                    dve.tensor_tensor(xs, xs, W[:, 0, :].rearrange("p (t d) -> p t d", t=TT),
                                      ALU.subtract if layer == 0 else ALU.add).then_inc(w_free[h], 1)
                    wait_apart(dve, w_free[h], u + 1)
                    for t in range(TT):
                        dve.bn_stats(ST[:, t, :], X[:, bass.ds(b * TT + t, 1), :]).then_inc(stat, 1)
                    wait_apart(dve, stat, 8 * b + 4)
                    for t in range(TT):
                        dve.bn_aggr(AG[:, t, :], ST[:, t, :]).then_inc(stat, 1)
                    dve.wait_ge(stat, 8 * b + 8)
                    dve.tensor_copy(MV[:, bass.ds(b * TT, TT), :], AG[:, :, :]).then_inc(x_done, 1)

                ST, AG = C["stats"], C["aggregate"]

                def body(kind, b, par):
                    k = kinds(kind)
                    nxt = 1 - par
                    for p in range(PAIRS):
                        if p == 0 and "nxt" in k:
                            layernorm(b + 1, nxt)
                        for q in range(TT):
                            max_unit(kind, b, p, q)
                            if layer == 1 and q == 3:
                                if (p > 0 and "cur" in k) or (p == 0 and "lag" in k):
                                    s1 = PAIRS * b + p
                                    refine(SB[:, :], RB[:, :], s1, s1 - 1, n1_done, s1)
                            for n in aux_at(kind, p, q):
                                h, u = turn(kind, b, n, p, q)
                                W = WORK[:, h]
                                if n.startswith("BC"):
                                    g = int(n[2])
                                    m = 4 * (b - 1 if g == 3 else b) + g
                                    refine(W[:, 0, :], RB[:, g % 2, :], m + 1, m - 1, w_free[h], u + 1)
                                elif n in ("OUT", "PTR"):
                                    residual(kind, b - 1, n, p, q)
                                elif n == "QK":
                                    dve.wait_ge(qb_done, 2 * b + 4)
                                    if not (isinstance(b, int) and b < 0):
                                        dve.wait_ge(parts_done, b + 1)
                                    dve.scalar_tensor_tensor(QF[:, :, :], QR2[:, :, :], 0.01, QR2[:, :, :],
                                                             ALU.mult, ALU.max).then_inc(qk_raw, 1)
                                elif n == "PJ":
                                    dve.wait_ge(pj_done, b)
                                    dve.scalar_tensor_tensor(PL[:, :], PJ[:, :], 0.01, PJ[:, :],
                                                             ALU.mult, ALU.max).then_inc(pl_done, 1)
                                elif n[0] == "V":
                                    t = int(n[1])
                                    dve.wait_ge(w_full[h], u + 1)
                                    dve.wait_ge(weights, LANDED)
                                    if t == 0 and not (isinstance(b, int) and b < 1):
                                        dve.wait_ge(pv_done, PAIRS * b)
                                    if not (isinstance(b, int) and b < 0 and t == 0):
                                        dve.wait_ge(v_done, TT * (b + 1) + t)
                                    dve.tensor_tensor(VB[:, :, :], W[:, :, :], BV[:, :, :], ALU.add).then_inc(w_free[h], 1)
                                    dve.wait_ge(w_free[h], u + 1)
                                    dve.scalar_tensor_tensor(V[:, nxt, t].rearrange("p h d -> p (h d)"),
                                                             VB[:, :, :].rearrange("p a n -> p (a n)"), 0.01,
                                                             VB[:, :, :].rearrange("p a n -> p (a n)"),
                                                             ALU.mult, ALU.max).then_inc(v_done, 1)
                        if layer == 1 and ((p > 0 and "cur" in k) or (p == 0 and "lag" in k)):
                            s1 = PAIRS * b + p
                            pair = (p - 1) % PAIRS
                            dve.wait_ge(pv_done, s1)
                            dve.wait_ge(rb_done, s1)
                            if pair == 0 and not (isinstance(b, int) and b == 0):
                                dve.wait_ge(pj_done, b)
                            dve.tensor_tensor(CT[:, pair, :], O[:, :], RB[:, :], ALU.mult).then_inc(ct_done, 1)

                QR2 = C["qk_biased"]
                bodies(dve, body)

            @block.scalar
            def _(act):
                QR2 = C["qk_biased"]

                def round_parts(b, i):
                    if i == 0:
                        act.wait_ge(qk_raw, b + 1)
                        if not (isinstance(b, int) and b == 0):
                            act.wait_ge(spilled, SPILLED * b)
                    else:
                        act.wait_ge(rest_done, RS0 + b + 1)
                    act.activation(QP[:, :, i, :], (QF if i == 0 else QR)[:, :, :], ACT.Copy).then_inc(rounded, 1)

                def first_reciprocal(sums, n):
                    if not (isinstance(n, int) and n < 2):
                        act.wait_ge(rb_done, n - 1)
                    act.activation(LS[:, :], sums, ACT.Ln).then_inc(ls_done, 1)
                    act.wait_ge(ls_done, n)
                    act.activation(R0[:, :], LS[:, :], ACT.Exp, scale=-1.0).then_inc(r0_done, 1)

                def body(kind, b, par):
                    k = kinds(kind)
                    nxt = 1 - par
                    for p in range(PAIRS):
                        s = PAIRS * b + p
                        for q in range(TT):
                            if "cur" in k:
                                if q == 0 and not (isinstance(b, int) and s < 2):
                                    act.wait_ge(pv_done, s - 1)
                                    if layer == 1:
                                        act.wait_ge(ps_done, 3 * (s - 1))
                                q0 = q * P if causal else 0
                                for half in range(2):
                                    act.wait_ge(s_full, 8 * s + 2 * q + half + 1)
                                    act.activation(PT[:, p % 2, q, half, q0:T], S[:, half, q0:T], ACT.Exp,
                                                   scale=scale).then_inc(exp_done, 1)
                            if layer == 1 and q == 2 and ((p > 0 and "cur" in k) or (p == 0 and "lag" in k)):
                                act.wait_ge(sb_done, s)
                                first_reciprocal(SB[:, :], s)
                            if layer == 0 and q == 1 and p % 2 == 1:
                                if (p == 1 and "lag" in k) or (p > 1 and "cur" in k):
                                    m = 4 * b + (p - 3) // 2
                                    act.wait_ge(pv_done, 2 * m + 2)
                                    if not (isinstance(b, int) and m < 2):
                                        act.wait_ge(ct_done, m - 1)
                                    act.activation(OU[:, ((p - 3) // 2) % 2, :], O[:, ((p - 3) // 2) % 2, :],
                                                   ACT.Copy).then_inc(ou_done, 1)
                            for n in aux_at(kind, p, q):
                                h, u = turn(kind, b, n, p, q)
                                W = WORK[:, h]
                                if n in ("OUT", "PTR") or n[0] == "V":
                                    continue
                                act.wait_ge(w_full[h], u + 1)
                                if n.startswith("BC"):
                                    g = int(n[2])
                                    first_reciprocal(W[:, 0, :], 4 * (b - 1 if g == 3 else b) + g + 1)
                                    continue
                                if n.startswith("MT"):
                                    g = int(n[2])
                                    m = 4 * (b + 1 if g == 0 else b) + g
                                    if not (isinstance(b, int) and m < 2):
                                        act.wait_ge(m_loaded, MROWS * (m - 1))
                                    act.activation(MT[:, g % 2, :, :].rearrange("r p t -> r (p t)"),
                                                   W[0:2 * PARTS, 0, :].bitcast(BF16), ACT.Copy).then_inc(w_free[h], 1)
                                    act.wait_ge(w_free[h], u + 1)
                                    act.nop().then_inc(mt_done, 1)
                                elif n == "XT":
                                    act.activation(XT[:, :], W[:, 0, :], ACT.Copy).then_inc(w_free[h], 1)
                                    act.wait_ge(w_free[h], u + 1)
                                    act.nop().then_inc(xt_done, 1)
                                elif n == "CQ":
                                    if not (isinstance(b, int) and b < 0):
                                        act.wait_ge(parts_done, b + 1)
                                    act.activation(CKV[:, :], W[0:32, 0, :], ACT.Copy).then_inc(ckv_done, 1)
                                    act.activation(QF[:, 0, :], W[:, 1, :], ACT.Copy).then_inc(w_free[h], 1)
                                elif n == "KV":
                                    if isinstance(b, int) and b < 1:
                                        act.wait_ge(cleared, 2)
                                    else:
                                        act.wait_ge(pv_done, PAIRS * b)
                                    act.activation(V[:, nxt, :, :, 0:DV],
                                                   W[:, 1, :].rearrange("p (t h d) -> p t h d", t=TT, d=DV),
                                                   ACT.Copy).then_inc(v_done, 1)
                                    act.activation(QF[:, 1, :], W[:, 0, :], ACT.Copy).then_inc(w_free[h], 1)
                                    act.wait_ge(w_free[h], u + 1)
                                    act.nop().then_inc(qk_raw, 1)
                                elif n == "QK":
                                    act.wait_ge(weights, LANDED)
                                    if not (isinstance(b, int) and b < 0):
                                        act.wait_ge(qk_raw, b + 1)
                                    act.activation(QR2[:, 0, :], W[:, 0, :], ACT.Identity,
                                                   bias=BQK[:, 0:1]).then_inc(qb_done, 1)
                                    act.activation(QR2[:, 1, :], W[:, 1, :], ACT.Identity,
                                                   bias=BQK[:, 1:2]).then_inc(w_free[h], 1)
                                    act.wait_ge(w_free[h], u + 1)
                                    act.nop().then_inc(qb_done, 1)
                                elif n == "PJ":
                                    if not (isinstance(b, int) and b < 2):
                                        act.wait_ge(pl_done, b - 1)
                                    act.activation(PJ[:, :], W[:, 0, :], ACT.Identity, scale=-1.0,
                                                   bias=BO[:, 0:1]).then_inc(w_free[h], 1)
                                    act.wait_ge(w_free[h], u + 1)
                                    act.nop().then_inc(pj_done, 1)
                            if p == 1 and q in (1, 3) and "nxt" in k:
                                round_parts(b + 1, q // 2)

                act.add_instruction(mybir.InstLoadActFuncSet(name=nc.get_next_instruction_name(), ins=[], outs=[],
                                                             act_func_set_id=EXP_AND_LN))
                bodies(act, body)

            @block.tensor
            def _(pe):
                pe.wait_ge(weights, LANDED)
                pe.wait_ge(cleared, 3 if layer == 0 else 2)

                def s1(kind, b, par, p, q):
                    w = ("cur" if p < 4 else "nxt")
                    if w not in kinds(kind):
                        return
                    h, u = turn(kind, b, "S1", p, q)
                    W = WORK[:, h]
                    bb, pb, pair = (b, par, p + 4) if p < 4 else (b + 1, 1 - par, p - 4)
                    if not (isinstance(u, int) and u == 0):
                        pe.wait_ge(w_free[h], u)
                    if p == 4 and q == 0:
                        pe.wait_ge(stacked, STACKED * (bb + 1))
                    width = (q + 1) * P if causal else T
                    for half in range(2):
                        r = 64 * half
                        i = pe.matmul(W[:, half, 0:width], QA[r:r + KQ, pb, pair, q * P:(q + 1) * P],
                                      KA[r:r + KQ, pb, pair, 0:width], start=True, stop=not causal)
                    if causal:
                        for half in range(2):
                            i = pe.matmul(W[:, half, q * P:(q + 1) * P], identb[:, :], maskq[:, :],
                                          start=False, stop=True)
                    i.then_inc(w_full[h], 1)

                def s2(b, par, p, q):
                    s = PAIRS * b + p
                    if q == 0 and p % 2 == 0:
                        pe.wait_ge(m_loaded, MROWS * (4 * b + p // 2 + 1))
                    q0 = q * P if causal else 0
                    for half in range(2):
                        if not (isinstance(b, int) and s == 0 and q == 0):
                            pe.wait_ge(exp_done, 8 * s + 2 * q + half - 1)
                        r = 64 * half
                        i = pe.matmul(S[:, half, q0:T], KA[r:r + KM, par, p, q * P:(q + 1) * P],
                                      QA[r:r + KM, par, p, q0:T], start=True, stop=not causal)
                        if causal:
                            i = pe.matmul(S[:, half, q0:q0 + P], identb[:, :], maskk[:, :],
                                          start=False, stop=True)
                        i.then_inc(s_full, 1)

                def pv(b, par, p, q):
                    s = PAIRS * b + p
                    if p == 0 and q == 0:
                        pe.wait_ge(v_done, (b + 1) * (1 if layer == 0 else TT))
                    q0 = q * P if causal else 0
                    for half in range(2):
                        pe.wait_ge(exp_done, 8 * s + 2 * q + half + 1)
                        if layer == 0:
                            if q == 0 and half == 0 and p % 2 == 0 and not (isinstance(b, int) and s < 4):
                                pe.wait_ge(ou_done, 4 * b + p // 2 - 1)
                            r = 32 * (2 * (p % 2) + half)
                            i = pe.matmul(O[r:r + 32, (p // 2) % 2, q0:T], V[:, par, q, 2 * p + half, :],
                                          PT[:, p % 2, q, half, q0:T], start=(q == 0), stop=(q == TT - 1))
                        else:
                            if q == 0 and half == 0 and not (isinstance(b, int) and s == 0):
                                pe.wait_ge(ct_done, s)
                            r = 64 * half
                            i = pe.matmul(O[r:r + 64, :], V[:, par, q, 2 * p + half, :],
                                          PT[:, p % 2, q, half, :], start=(q == 0), stop=(q == TT - 1))
                    if q == TT - 1:
                        i.then_inc(pv_done, 1)

                def sums(b, p):
                    s = PAIRS * b + p
                    pe.wait_ge(ps_done, 3 * (s + 1))
                    if not (isinstance(b, int) and s == 0):
                        pe.wait_ge(rb_done, s)
                    for half in range(2):
                        i = pe.matmul(SB[64 * half:64 * half + 64, :], ones64[:, :], PS[:, p % 2, half, :],
                                      start=True, stop=True)
                    i.then_inc(sb_done, 1)

                def aux(kind, b, par, n, p, q):
                    h, u = turn(kind, b, n, p, q)
                    W = WORK[:, h]
                    if not (isinstance(u, int) and u == 0):
                        pe.wait_ge(w_free[h], u)
                    nxt = 1 - par
                    if n.startswith("MT"):
                        g = int(n[2])
                        m = 4 * (b + 1 if g == 0 else b) + g
                        pe.wait_ge(mp_done, m + 1)
                        for pair in range(2):
                            for t in range(TT):
                                col = (pair * TT + t) * P // 2
                                i = pe.transpose(W[0:2 * PARTS, 0, col:col + P // 2].bitcast(BF16),
                                                 MP[:, g % 2, t, 2 * pair:2 * pair + 2].rearrange("p h i -> p (h i)"),
                                                 identb[:, :])
                    elif n == "XT":
                        pe.wait_ge(ln_done, 4 * (b + 2) if layer == 0 else 5 * (b + 1) + 4)
                        for t in range(TT):
                            i = pe.transpose(W[:, 0, t * P:(t + 1) * P], XN[:, nxt, t, :], identf[:, :])
                    elif n == "CQ":
                        pe.wait_ge(xt_done, b + 2)
                        pe.matmul(W[0:32, 0, :], WDKV[:, :], XT[:, :], start=True, stop=True)
                        i = pe.matmul(W[:, 1, :], WUQ[:, :], XT[:, :], start=True, stop=True)
                    elif n == "KV":
                        pe.wait_ge(ckv_done, b + 2)
                        pe.matmul(W[:, 0, :], WUK[:, :], CKV[:, :], start=True, stop=True)
                        for t in range(TT):
                            i = pe.matmul(W[:, 1, t * P:(t + 1) * P], CKV[:, t * P:(t + 1) * P], WUV[:, :],
                                          start=True, stop=True)
                    elif n == "QK":
                        pe.wait_ge(xt_done, b + 2)
                        for a in range(2):
                            i = pe.matmul(W[:, a, :], WC[:, a * P:(a + 1) * P], XT[:, :], start=True, stop=True)
                    elif n[0] == "V":
                        t = int(n[1])
                        for a in range(2):
                            i = pe.matmul(W[:, a, :], XT[:, t * P:(t + 1) * P], WC[:, 256 + a * T:256 + (a + 1) * T],
                                          start=True, stop=True)
                    elif n.startswith("BC"):
                        g = int(n[2])
                        m = 4 * (b - 1 if g == 3 else b) + g
                        pe.wait_ge(ou_done, m + 1)
                        i = pe.matmul(W[:, 0, :], bcast[:, :], OU[:, g % 2, :], start=True, stop=True)
                    elif n == "OUT":
                        pe.wait_ge(ct_done, 4 * b)
                        for t in range(TT):
                            for g in range(4):
                                i = pe.matmul(W[:, 0, t * P:(t + 1) * P], CT[:, g, t * P:(t + 1) * P], WO[:, g, :],
                                              start=(g == 0), stop=(g == 3))
                    elif n == "PJ":
                        pe.wait_ge(ct_done, PAIRS * b)
                        for c in range(PAIRS):
                            i = pe.matmul(W[:, 0, :], WO[:, c, :], CT[:, c, :], start=(c == 0), stop=(c == PAIRS - 1))
                    elif n == "PTR":
                        pe.wait_ge(pl_done, b)
                        for t in range(TT):
                            i = pe.transpose(W[:, 0, t * P:(t + 1) * P], PL[:, t * P:(t + 1) * P], identf[:, :])
                    i.then_inc(w_full[h], 1)

                def body(kind, b, par):
                    k = kinds(kind)
                    for p in range(PAIRS):
                        lagging = (p > 0 and "cur" in k) or (p == 0 and "lag" in k)
                        lb, lpar, lp = (b, par, p - 1) if p > 0 else (b - 1, 1 - par, PAIRS - 1)
                        for q in range(TT):
                            if "cur" in k:
                                s2(b, par, p, q)
                            s1(kind, b, par, p, q)
                            if lagging:
                                pv(lb, lpar, lp, q)
                                if layer == 1 and q == 1:
                                    sums(lb, lp)
                            for n in aux_at(kind, p, q):
                                aux(kind, b, par, n, p, q)

                bodies(pe, body)


E = 8
H = 512
HC = H // P
CAP = 768
TS = 256
SC = TS // P
DEPTH = 6
assert E * CAP // TS % DEPTH == 0


def moe(nc, ctx, layer, X, MV, RSTD, C, w, xbuf, ybuf, tag):
    TOP = 1 if layer == 0 else 2
    NTILES = E * CAP // TS if layer == 0 else TOP * B * T // TS + E
    SLOTS = NTILES * TS
    func = ACT.Gelu if layer == 0 else ACT.Relu
    L = f"F{layer}_"
    buffers = ExitStack()

    def sb(name, shape, dt=F32):
        return buffers.enter_context(nc.sbuf_tensor(L + name, shape, dt))

    def sem(name):
        return ctx.enter_context(nc.semaphore(L + name))

    U32, I32 = mybir.dt.uint32, mybir.dt.int32
    with buffers:
        SLOT = sb("slot", [P, TOP, NT], U32)
        BACK = sb("back", [P, TOP, NT], U32)
        GATE = sb("gate", [P, TOP, NT])
        OWNER = sb("owner", [1, NTILES], I32)
        routing = ExitStack()

        def rb(name, shape, dt=F32):
            return routing.enter_context(nc.sbuf_tensor(L + name, shape, dt))

        with routing:
            XN = rb("xn", [P, NT, D])
            XT = rb("xT", [P, 2, T])
            LG = rb("logits", [P, NT, E])
            WR = rb("w_router", [P, E])
            BR = rb("b_router", [P, E])
            OH = rb("onehot", [P, TOP, NT, E])
            OHB = rb("onehot_b", [P, NT, E], BF16)
            TMP = rb("tmp", [P, NT, E])
            TM2 = rb("tmp2", [P, NT, E])
            CNT = rb("counts", [P, 2, NT + 1, E])
            TOPV = rb("top", [P, TOP, NT])
            PICK = rb("pick", [P, NT])
            RANK = rb("rank", [P, NT])
            KEEP = rb("keep", [P, NT])
            W8 = rb("w8", [P, E])
            ECAP = rb("ecap", [P, E])
            SPILL = rb("spill", [P, NT])
            TRI = rb("tri", [P, P], BF16)
            ONE = rb("one", [P, P], BF16)
            TRIF = rb("trif", [P, P])
            TN = rb("tiles", [P, 2, E])
            TNI = rb("tiles_i", [P, E], I32)
            JT = rb("jt", [1, NTILES])
            JC = rb("jc", [1, NTILES, E])
            JI = rb("jf", [1, NTILES])
            with (nc.psum_tensor(L + "xt_ps", [P, 2, T], F32) as XTP,
                  nc.psum_tensor(L + "lg_ps", [P, 2, T], F32) as LGP,
                  nc.psum_tensor(L + "rk_ps", [P, 2, T], F32) as RKP):
                w_in = sem("w_in")
                ln = sem("ln")
                xtp = sem("xtp")
                xts = sem("xts")
                lgp = sem("lgp")
                lgs = sem("lgs")
                const = sem("const")
                st = sem("st")
                chosen = sem("chosen")
                expd = sem("expd")
                ranked = sem("ranked")
                slotted = sem("slotted")
                scat = sem("scat")

                def sl(t, n):
                    return bass.ds(t, n)

                with nc.Block() as block:
                    @block.sync
                    def _(sp):
                        sp.dma_start(WR[:, :], w["router"]).then_inc(w_in, 16)
                        if layer == 1:
                            sp.dma_start(BR[:, :], w["br"].rearrange("(a e) -> a e", a=1)
                                         .broadcast_to([P, E])).then_inc(w_in, 16)

                    @block.gpsimd
                    def _(pool):
                        pool.iota(W8[:, :], pattern=[[-1, E]], base=E, channel_multiplier=0,
                                  allow_small_or_imprecise_dtypes=True).then_inc(const, 1)
                        pool.iota(ECAP[:, :], pattern=[[CAP, E]], base=0, channel_multiplier=0,
                                  allow_small_or_imprecise_dtypes=True).then_inc(const, 1)
                        pool.iota(SPILL[:, :], pattern=[[P, NT]], base=E * CAP, channel_multiplier=1,
                                  allow_small_or_imprecise_dtypes=True).then_inc(const, 1)
                        if layer == 1:
                            pool.iota(JI[:, :], pattern=[[1, NTILES]], base=0, channel_multiplier=0,
                                      allow_small_or_imprecise_dtypes=True).then_inc(const, 1)
                        else:
                            pool.iota(OWNER[:, :], pattern=[[1, E], [0, CAP // TS]], base=0,
                                      channel_multiplier=0).then_inc(const, 1)
                        pool.memset(ONE[:, :], 1.0).then_inc(const, 1)
                        pool.memset(TRIF[:, :], 1.0).then_inc(const, 1)
                        pool.memset(CNT[:, :, 0:1, :], 0.0).then_inc(const, 1)
                        pool.wait_ge(const, 7)
                        pool.affine_select(out=TRI[:, :], in_=TRIF[:, :], compare_op=ALU.is_gt, fill=0.0,
                                           base=0, pattern=[[1, P]], channel_multiplier=-1).then_inc(const, 1)
                        pool.wait_ge(C["zeroed"], 16 * ZERO_DMAS)
                        pool.wait_ge(slotted, 1)
                        for t in range(NT):
                            for k in range(TOP):
                                pool.indirect_dma_start(
                                    xbuf, bass.IndirectOffsetOnAxis(ap=SLOT[:, k, t:t + 1], axis=0),
                                    XN[:, t, :], None).then_inc(scat, 16)
                        pool.wait_ge(scat, 16 * NT * TOP)

                    @block.vector
                    def _(dve):
                        def batch(b, par, first):
                            for t in range(TT):
                                tile = b * TT + t
                                dve.tensor_scalar(XN[:, sl(tile, 1), :], X[:, sl(tile, 1), :],
                                                  MV[:, sl(tile, 1), 0:1].rearrange("p a o -> p (a o)"),
                                                  RSTD[:, sl(tile, 1)], ALU.subtract, ALU.mult).then_inc(ln, 1)

                        def logits(b, par):
                            dve.wait_ge(lgp, b + 1)
                            o = LG[:, sl(b * TT, TT), :]
                            i = LGP[:, par, 0:TT * E].rearrange("p (t e) -> p t e", t=TT)
                            if layer == 0:
                                dve.tensor_copy(o, i).then_inc(lgs, 1)
                            else:
                                dve.tensor_tensor(o, i, BR[:, :].rearrange("p (a e) -> p a e", a=1)
                                                  .broadcast_to([P, TT, E]), ALU.add).then_inc(lgs, 1)

                        dve.wait_ge(w_in, 16 * (1 + layer))
                        batch(0, 0, True)
                        batch(1, 1, True)
                        with dve.Fori(0, (B - 2) // 2) as i:
                            for u in range(2):
                                logits(2 * i + u, u)
                                batch(2 * i + u + 2, u, False)
                        logits(B - 2, 0)
                        logits(B - 1, 1)

                        n = [0]

                        def step(ins):
                            ins.then_inc(st, 1)
                            n[0] += 1
                            dve.wait_ge(st, n[0])

                        dve.wait_ge(lgs, B)
                        dve.wait_ge(const, 8)

                        def over_e(x):
                            return x.rearrange("p (t a) -> p t a", a=1).broadcast_to([P, NT, E])

                        def over_t(x):
                            return x.rearrange("p (a e) -> p a e", a=1).broadcast_to([P, NT, E])

                        src = LG
                        for k in range(TOP):
                            step(dve.tensor_reduce(TOPV[:, k, :], src[:, :, :], AX.X, ALU.max))
                            step(dve.tensor_tensor(TMP[:, :, :], src[:, :, :], over_e(TOPV[:, k, :]), ALU.is_equal))
                            step(dve.tensor_tensor(TMP[:, :, :], TMP[:, :, :], over_t(W8[:, :]), ALU.mult))
                            step(dve.tensor_reduce(PICK[:, :], TMP[:, :, :], AX.X, ALU.max))
                            step(dve.tensor_tensor(OH[:, k], over_t(W8[:, :]), over_e(PICK[:, :]), ALU.is_equal))
                            if k + 1 < TOP:
                                step(dve.scalar_tensor_tensor(TM2[:, :, :].rearrange("p t e -> p (t e)"),
                                                              OH[:, k].rearrange("p t e -> p (t e)"), -3e38,
                                                              LG[:, :, :].rearrange("p t e -> p (t e)"),
                                                              ALU.mult, ALU.add))
                                src = TM2
                        if layer == 0:
                            step(dve.tensor_copy(OHB[:, :, :], OH[:, 0]))
                            dve.tensor_tensor(TMP[:, :, :], LG[:, :, :], over_e(TOPV[:, 0, :]), ALU.subtract)\
                                .then_inc(chosen, 1)
                        else:
                            step(dve.tensor_tensor(OHB[:, :, :], OH[:, 0], OH[:, 1], ALU.add))
                            dve.tensor_tensor(PICK[:, :], TOPV[:, 1, :], TOPV[:, 0, :], ALU.subtract).then_inc(chosen, 1)
                        dve.wait_ge(chosen, 1)
                        dve.wait_ge(expd, 1)
                        if layer == 0:
                            step(dve.tensor_reduce(PICK[:, :], TM2[:, :, :], AX.X, ALU.add))
                            step(dve.reciprocal(GATE[:, 0, :], PICK[:, :]))
                        else:
                            step(dve.tensor_scalar(RANK[:, :], KEEP[:, :], 1.0, None, ALU.add))
                            step(dve.reciprocal(GATE[:, 0, :], RANK[:, :]))
                            step(dve.tensor_tensor(GATE[:, 1, :], GATE[:, 0, :], KEEP[:, :], ALU.mult))
                        dve.wait_ge(ranked, 1)
                        step(dve.tensor_copy(CNT[:, 0, 1:NT + 1, :],
                                             RKP[:, 1, 0:NT * E].rearrange("p (t e) -> p t e", e=E)))
                        cur, d = 0, 1
                        while d < NT + 1:
                            nx = 1 - cur
                            step(dve.tensor_tensor(CNT[:, nx, d:NT + 1, :], CNT[:, cur, d:NT + 1, :],
                                                   CNT[:, cur, 0:NT + 1 - d, :], ALU.add))
                            step(dve.tensor_copy(CNT[:, nx, 0:d, :], CNT[:, cur, 0:d, :]))
                            cur, d = nx, 2 * d
                        total = CNT[:, cur, NT, :]
                        step(dve.tensor_tensor(TMP[:, :, :], RKP[:, 0, 0:NT * E].rearrange("p (t e) -> p t e", e=E),
                                               CNT[:, cur, 0:NT, :], ALU.add))
                        if layer == 0:
                            step(dve.tensor_tensor(TM2[:, :, :], TMP[:, :, :], OH[:, 0], ALU.mult))
                            step(dve.tensor_reduce(RANK[:, :], TM2[:, :, :], AX.X, ALU.add))
                            step(dve.tensor_scalar(KEEP[:, :], RANK[:, :], CAP - 0.5, None, ALU.is_lt))
                            step(dve.tensor_tensor(GATE[:, 0, :], GATE[:, 0, :], KEEP[:, :], ALU.mult))
                            step(dve.tensor_tensor(TM2[:, :, :], OH[:, 0], over_t(ECAP[:, :]), ALU.mult))
                            step(dve.tensor_reduce(PICK[:, :], TM2[:, :, :], AX.X, ALU.add))
                            step(dve.tensor_tensor(RANK[:, :], RANK[:, :], PICK[:, :], ALU.add))
                            step(dve.tensor_tensor(RANK[:, :], RANK[:, :], SPILL[:, :], ALU.subtract))
                            step(dve.tensor_tensor(RANK[:, :], RANK[:, :], KEEP[:, :], ALU.mult))
                            step(dve.tensor_tensor(RANK[:, :], RANK[:, :], SPILL[:, :], ALU.add))
                            step(dve.tensor_scalar(BACK[:, 0, :], RANK[:, :], float(E * CAP - 1), None, ALU.min))
                            dve.tensor_copy(SLOT[:, 0, :], RANK[:, :]).then_inc(slotted, 1)
                        else:
                            step(dve.tensor_scalar(TN[:, 0, :], total, 1.0 / TS, (TS - 1.0 - (TS - 1) / 2.0) / TS,
                                                   ALU.mult, ALU.add))
                            step(dve.tensor_copy(TNI[:, :], TN[:, 0, :]))
                            step(dve.tensor_copy(TN[:, 0, :], TNI[:, :]))
                            cur, d = 0, 1
                            while d < E:
                                nx = 1 - cur
                                step(dve.tensor_tensor(TN[:, nx, d:E], TN[:, cur, d:E], TN[:, cur, 0:E - d], ALU.add))
                                step(dve.tensor_copy(TN[:, nx, 0:d], TN[:, cur, 0:d]))
                                cur, d = nx, 2 * d
                            ends = TN[:, cur, :]
                            step(dve.tensor_tensor(JC[:, :, :], JI[:, :].rearrange("p (j a) -> p j a", a=1)
                                                   .broadcast_to([1, NTILES, E]),
                                                   ends[0:1].rearrange("p (a e) -> p a e", a=1)
                                                   .broadcast_to([1, NTILES, E]), ALU.is_ge))
                            step(dve.tensor_reduce(JT[:, :], JC[:, :, :], AX.X, ALU.add))
                            step(dve.tensor_scalar(OWNER[:, :], JT[:, :], E - 1.0, None, ALU.min))
                            step(dve.tensor_copy(ECAP[:, :], TNI[:, :]))
                            step(dve.tensor_tensor(ECAP[:, :], ends, ECAP[:, :], ALU.subtract))
                            step(dve.tensor_scalar(ECAP[:, :], ECAP[:, :], float(TS), None, ALU.mult))
                            step(dve.tensor_tensor(TMP[:, :, :], TMP[:, :, :], over_t(ECAP[:, :]), ALU.add))
                            for k in range(TOP):
                                step(dve.tensor_tensor(TM2[:, :, :], TMP[:, :, :], OH[:, k], ALU.mult))
                                step(dve.tensor_reduce(RANK[:, :], TM2[:, :, :], AX.X, ALU.add))
                                step(dve.tensor_copy(BACK[:, k, :], RANK[:, :]))
                                i = dve.tensor_copy(SLOT[:, k, :], RANK[:, :])
                                if k + 1 < TOP:
                                    step(i)
                                else:
                                    i.then_inc(slotted, 1)

                    @block.scalar
                    def _(act):
                        def copy_out(b, par, first):
                            act.wait_ge(xtp, b + 1)
                            if not first:
                                act.wait_ge(lgp, b - 1)
                            act.activation(XT[:, par, :], XTP[:, par, :], ACT.Copy).then_inc(xts, 1)

                        copy_out(0, 0, True)
                        copy_out(1, 1, True)
                        with act.Fori(0, (B - 2) // 2) as i:
                            for u in range(2):
                                copy_out(2 * i + u + 2, u, False)
                        act.wait_ge(chosen, 1)
                        if layer == 0:
                            act.activation(TM2[:, :, :], TMP[:, :, :], ACT.Exp).then_inc(expd, 1)
                        else:
                            act.activation(KEEP[:, :], PICK[:, :], ACT.Exp).then_inc(expd, 1)

                    @block.tensor
                    def _(pe):
                        def transpose(b, par, first):
                            pe.wait_ge(ln, TT * (b + 1))
                            if not first:
                                pe.wait_ge(xts, b - 1)
                            for t in range(TT):
                                i = pe.transpose(XTP[:, par, t * P:(t + 1) * P],
                                                 XN[:, b * TT + t, :], C["identf"][:, :])
                            i.then_inc(xtp, 1)

                        def project(b, par, first):
                            pe.wait_ge(xts, b + 1)
                            if not first:
                                pe.wait_ge(lgs, b - 1)
                            for t in range(TT):
                                i = pe.matmul(LGP[:, par, t * E:(t + 1) * E], XT[:, par, t * P:(t + 1) * P],
                                              WR[:, :], start=True, stop=True)
                            i.then_inc(lgp, 1)

                        pe.wait_ge(w_in, 16 * (1 + layer))
                        transpose(0, 0, True)
                        for b in range(B):
                            if b + 1 < B:
                                transpose(b + 1, (b + 1) % 2, b < 1)
                            project(b, b % 2, b < 2)
                        pe.wait_ge(chosen, 1)
                        pe.wait_ge(const, 8)
                        ohb = OHB[:, :, :].rearrange("p t e -> p (t e)")
                        pe.matmul(RKP[:, 0, 0:NT * E], TRI[:, :], ohb, start=True, stop=True)
                        pe.matmul(RKP[:, 1, 0:NT * E], ONE[:, :], ohb, start=True, stop=True).then_inc(ranked, 1)

        work = ExitStack()

        def wb(name, shape, dt=F32):
            return work.enter_context(nc.sbuf_tensor(L + name, shape, dt))

        def wp(name, shape):
            return work.enter_context(nc.psum_tensor(L + name, shape, F32))

        with work:
            W1 = wb("w1", [P, DEPTH, H + HC])
            W2 = wb("w2", [P, DEPTH, HC, D])
            B2 = wb("b2", [P, DEPTH, D])
            XS = wb("xs", [P, DEPTH, SC, D])
            XST = wb("xsT", [P, 2, TS])
            HT = wb("hT", [P, 2, HC, TS])
            YS = wb("ys", [P, 2, SC, D])
            TP = wp("tp", [P, 2, T])
            HP = wp("hp", [P, 4, T])
            YP = wp("yp", [P, 2, T])
            loaded, tiles_before = C["loaded"], layer * (E * CAP // TS) // DEPTH
            tp_full = sem("tp_full")
            xst_done = sem("xst_done")
            h_full = sem("h_full")
            h_done = sem("h_done")
            y_full = sem("y_full")
            y_done = sem("y_done")
            y_out = [sem(f"y_out{u}") for u in range(2)]
            NL = 4

            with nc.Block() as block:
                @block.sync
                def _(sp):
                    def load(j, m, first):
                        if not first:
                            sp.wait_ge(y_done, j - DEPTH + 1)
                        e = sp.value_load(OWNER[0:1, j:j + 1] if isinstance(j, int) else OWNER[0:1, bass.ds(j, 1)],
                                          min_val=0, max_val=E - 1)
                        es = bass.ds(e, 1)
                        js = bass.ds(j, 1)
                        sp.dma_start(XS[:, m, :, :], xbuf[0:SLOTS].rearrange("(j c p) d -> j p c d", c=SC, p=P)[js]
                                     .rearrange("o p c d -> (o p) c d")).then_inc(loaded[m], 16)
                        sp.dma_start(W1[:, m, :], w["w1"][es].rearrange("o p n -> (o p) n")).then_inc(loaded[m], 16)
                        sp.dma_start(W2[:, m, :, :], w["w2"][es].rearrange("o (c p) d -> (o p) c d", p=P))\
                            .then_inc(loaded[m], 16)
                        sp.dma_start(B2[:, m, :], w["b2"][es].broadcast_to([P, D])).then_inc(loaded[m], 16)

                    for j in range(DEPTH):
                        load(j, j, True)
                    with sp.Fori(1, NTILES // DEPTH) as i:
                        for m in range(DEPTH):
                            load(DEPTH * i + m, m, False)
                    for j in range(NTILES // DEPTH * DEPTH, NTILES):
                        load(j, j % DEPTH, False)

                def tiles(eng, run):
                    full = (NTILES - 2) // DEPTH * DEPTH
                    for j in range(DEPTH):
                        run(j, j % DEPTH, j % 2, j, (j + 1) // DEPTH, (j - 1) // 2)
                    with eng.Fori(1, full // DEPTH) as i:
                        for v in range(DEPTH):
                            run(DEPTH * i + v, v, v % 2, None, i + (v + 1) // DEPTH, DEPTH // 2 * i + (v - 1) // 2)
                    for j in range(full, NTILES):
                        run(j, j % DEPTH, j % 2, j, (j + 1) // DEPTH, (j - 1) // 2)

                @block.tensor
                def _(pe):
                    def transpose(j, m, u, uses):
                        pe.wait_ge(loaded[m], NL * 16 * (tiles_before + uses + 1))
                        if not (isinstance(j, int) and j < 2):
                            pe.wait_ge(xst_done, j - 1)
                        for c in range(SC):
                            i = pe.transpose(TP[:, u, c * P:(c + 1) * P], XS[:, m, c, :], C["identf"][:, :])
                        i.then_inc(tp_full, 1)

                    def hidden(j, m, u):
                        pe.wait_ge(xst_done, j + 1)
                        for half in range(2):
                            if not (isinstance(j, int) and j < 2):
                                pe.wait_ge(h_done, 4 * j - 8 + 2 * half + 2)
                            for a in range(2):
                                c = 2 * half + a
                                i = pe.matmul(HP[:, 2 * u + half, a * TS:(a + 1) * TS], W1[:, m, c * P:(c + 1) * P],
                                              XST[:, u, :], start=True, stop=True)
                            i.then_inc(h_full, 1)

                    def result(j, m, u):
                        pe.wait_ge(h_done, 4 * j + 4)
                        if not (isinstance(j, int) and j < 2):
                            pe.wait_ge(y_done, j - 1)
                        for s in range(SC):
                            for c in range(HC):
                                i = pe.matmul(YP[:, u, s * P:(s + 1) * P], HT[:, u, c, s * P:(s + 1) * P],
                                              W2[:, m, c, :], start=(c == 0), stop=(c == HC - 1))
                        i.then_inc(y_full, 1)

                    def run(j, m, u, k, uses, stores):
                        if k != NTILES - 1:
                            transpose(j + 1, (m + 1) % DEPTH, 1 - u, uses)
                        hidden(j, m, u)
                        if k != 0:
                            result(j - 1, (m - 1) % DEPTH, 1 - u)

                    transpose(0, 0, 0, 0)
                    tiles(pe, run)
                    result(NTILES - 1, (NTILES - 1) % DEPTH, (NTILES - 1) % 2)

                @block.scalar
                def _(act):
                    def run(j, m, u, k, uses, stores):
                        for c in range(HC):
                            act.wait_ge(h_full, 2 * j + c // 2 + 1)
                            if c == 0 and not (isinstance(j, int) and j < 2):
                                act.wait_ge(y_full, j - 1)
                            act.activation(HT[:, u, c, :], HP[:, 2 * u + c // 2, (c % 2) * TS:(c % 2 + 1) * TS],
                                           func, bias=W1[:, m, H + c:H + c + 1]).then_inc(h_done, 1)

                    tiles(act, run)

                @block.vector
                def _(dve):
                    def rows(j, m, u):
                        dve.wait_ge(tp_full, j + 1)
                        if not (isinstance(j, int) and j < 2):
                            dve.wait_ge(h_full, 2 * j - 2)
                        dve.tensor_copy(XST[:, u, :], TP[:, u, 0:TS]).then_inc(xst_done, 1)

                    def result(j, m, u, stores):
                        dve.wait_ge(y_full, j + 1)
                        if not (isinstance(j, int) and j < 2):
                            dve.wait_ge(y_out[u], 16 * stores)
                        dve.tensor_tensor(YS[:, u, :, :], YP[:, u, 0:TS].rearrange("p (s d) -> p s d", s=SC),
                                          B2[:, m, :].rearrange("p (a d) -> p a d", a=1).broadcast_to([P, SC, D]),
                                          ALU.add).then_inc(y_done, 1)

                    def run(j, m, u, k, uses, stores):
                        if k != NTILES - 1:
                            rows(j + 1, (m + 1) % DEPTH, 1 - u)
                        if k != 0:
                            result(j - 1, (m - 1) % DEPTH, 1 - u, stores)

                    rows(0, 0, 0)
                    tiles(dve, run)
                    result(NTILES - 1, (NTILES - 1) % DEPTH, (NTILES - 1) % 2, (NTILES - 1) // 2)

                @block.gpsimd
                def _(pool):
                    def run(j, m, u, k, uses, stores):
                        pool.wait_ge(y_done, j + 1)
                        js = bass.ds(j, 1)
                        pool.dma_start(ybuf.rearrange("(j c p) d -> j p c d", c=SC, p=P)[js]
                                       .rearrange("o p c d -> (o p) c d"), YS[:, u, :, :]).then_inc(y_out[u], 16)

                    tiles(pool, run)
                    for u in range(2):
                        pool.wait_ge(y_out[u], 16 * (NTILES // 2))

        with nc.sbuf_tensor(L + "yg", [P, TOP, NT, D], F32) as YG:
            rows_in, before = C["rows_in"], 16 * TT * layer
            added = sem("added")
            aggr = sem("aggr")
            stored = sem("stored")
            with nc.Block() as block:
                @block.gpsimd
                def _(pool):
                    for t in range(NT):
                        for k in range(TOP):
                            pool.indirect_dma_start(YG[:, k, t, :], None, ybuf,
                                                    bass.IndirectOffsetOnAxis(ap=BACK[:, k, t:t + 1], axis=0))\
                                .then_inc(rows_in[t // TT], 16)

                @block.vector
                def _(dve):
                    n = 0
                    for b in range(B):
                        dve.wait_ge(rows_in[b], before + 16 * TT * TOP)
                        for k in range(TOP):
                            if k:
                                dve.wait_ge(added, TT * (TOP * b + k))
                            for t in range(b * TT, b * TT + TT):
                                dve.scalar_tensor_tensor(X[:, t, :], YG[:, k, t, :], GATE[:, k, t:t + 1], X[:, t, :],
                                                         ALU.mult, ALU.add).then_inc(added, 1)
                        if layer == 0:
                            dve.wait_ge(added, TT * TOP * (b + 1))
                            for t in range(TT):
                                dve.bn_stats(C["stats"][:, t, :], X[:, b * TT + t, :]).then_inc(aggr, 1)
                            dve.wait_ge(aggr, n + TT)
                            for t in range(TT):
                                dve.bn_aggr(MV[:, b * TT + t, :], C["stats"][:, t, :]).then_inc(aggr, 1)
                            n += 2 * TT
                            dve.wait_ge(aggr, n)

                if layer == 1:
                    @block.sync
                    def _(sp):
                        for b in range(B):
                            sp.wait_ge(added, TT * TOP * (b + 1))
                            sp.dma_start(C["out"][:, b * TT:(b + 1) * TT, :],
                                         X[:, b * TT:(b + 1) * TT, :]).then_inc(stored, 16)
                        sp.wait_ge(stored, 16 * B)


ZERO_ROWS = 1024
ZERO_DMAS = (E * CAP + 2 * B * T + E * TS) // ZERO_ROWS


def program(nc, a, out):
    with ExitStack() as ctx:
        def sb(name, shape, dt=F32):
            return ctx.enter_context(nc.sbuf_tensor(name, shape, dt))

        def sem(name):
            return ctx.enter_context(nc.semaphore(name))

        X = sb("x", [P, NT, D])
        MV = sb("mean_var", [P, NT, 2])
        RSTD = sb("rstd", [P, NT])
        C = {
            "identf": sb("identf", [P, P]), "identb": sb("identb", [P, P], BF16),
            "maskq": sb("maskq", [P, P], BF16), "maskk": sb("maskk", [P, P], BF16),
            "bcast": sb("bcast", [P, P]), "stats": sb("stats", [P, TT, 6]),
            "aggregate": sb("aggregate", [P, TT, 2]),
            "qk_biased": sb("qk_biased", [P, 2, T]),
            "root": sb("root", [P, NT]), "root2": sb("root2", [P, NT]), "eps": sb("eps", [P, 1]),
        }
        scratch = [nc.dram_tensor(f"qk_scratch{i}", [B, 2, 2, PARTS, P // 2, T], BF16).ap() for i in range(2)]

        xbuf = [nc.dram_tensor("x_slots0", [E * CAP + B * T, D], F32).ap(),
                nc.dram_tensor("x_slots1", [2 * B * T + E * TS, D], F32).ap()]
        ybuf = [nc.dram_tensor("y_slots0", [E * CAP, D], F32).ap(),
                nc.dram_tensor("y_slots1", [2 * B * T + E * TS, D], F32).ap()]
        C["zero"] = sb("zero", [P, ZERO_ROWS // P, D])
        C["zeroed"] = sem("zeroed")
        C["loaded"] = [sem(f"loaded{i}") for i in range(DEPTH)]
        C["rows_in"] = [sem(f"rows_in{b}") for b in range(B)]
        zero_set = sem("zero_set")

        x_in = a["L0_attn_x"].rearrange("b (t p) d -> p (b t) d", p=P)
        out_v = out.rearrange("b (t p) d -> p (b t) d", p=P)

        def rstd(tag, load):
            x_in_done = [sem(f"{tag}_x_in{c}") for c in range(B)] if load else None
            step = sem(f"{tag}_rstd_step")
            rooted = sem(f"{tag}_rooted")
            const = sem(f"{tag}_const")
            with nc.Block() as block:
                if load:
                    @block.sync
                    def _(sp):
                        for c in range(B):
                            sp.dma_start(X[:, c * TT:(c + 1) * TT, :],
                                         x_in[:, c * TT:(c + 1) * TT, :]).then_inc(x_in_done[c], 16)
                        sp.wait_ge(zero_set, 1)
                        for buf, rows in ((xbuf[0], E * CAP), (xbuf[1], 2 * B * T + E * TS)):
                            for r in range(0, rows, ZERO_ROWS):
                                sp.dma_start(buf[r:r + ZERO_ROWS].rearrange("(p c) d -> p c d", p=P),
                                             C["zero"][:, :, :]).then_inc(C["zeroed"], 16)

                    @block.gpsimd
                    def _(pool):
                        pool.memset(C["zero"][:], 0.0).then_inc(zero_set, 1)
                        pool.memset(C["eps"][:], EPS).then_inc(const, 1)
                        for m in ("identf", "identb", "maskq", "maskk", "bcast"):
                            pool.memset(C[m][:], 0.0).then_inc(const, 1)
                        pool.wait_ge(const, 6)
                        for m in ("identf", "identb"):
                            pool.affine_select(out=C[m][:, :], in_=C[m][:, :], compare_op=ALU.not_equal, fill=1.0,
                                               base=0, pattern=[[-1, P]], channel_multiplier=1).then_inc(const, 1)
                        pool.affine_select(out=C["maskq"][:, :], in_=C["maskq"][:, :], compare_op=ALU.is_ge,
                                           fill=MASKED, base=0, pattern=[[-1, P]], channel_multiplier=1)\
                            .then_inc(const, 1)
                        pool.affine_select(out=C["maskk"][:, :], in_=C["maskk"][:, :], compare_op=ALU.is_ge,
                                           fill=MASKED, base=0, pattern=[[1, P]], channel_multiplier=-1)\
                            .then_inc(const, 1)
                        bc = C["bcast"][:, :].rearrange("p (j r) -> p j r", j=4)
                        pool.affine_select(out=bc, in_=bc, compare_op=ALU.not_equal, fill=1.0, base=-DQ,
                                           pattern=[[-32, 4], [0, 32]], channel_multiplier=1).then_inc(const, 1)

                @block.vector
                def _(dve):
                    n = 0
                    if load:
                        for c in range(B):
                            dve.wait_ge(x_in_done[c], 16)
                            for t in range(TT):
                                dve.bn_stats(C["stats"][:, t, :], X[:, c * TT + t, :]).then_inc(step, 1)
                            dve.wait_ge(step, n + TT)
                            for t in range(TT):
                                dve.bn_aggr(MV[:, c * TT + t, :], C["stats"][:, t, :]).then_inc(step, 1)
                            n += 2 * TT
                            dve.wait_ge(step, n)
                    dve.wait_ge(rooted, 1)
                    dve.reciprocal(RSTD[:, :], C["root"][:, :]).then_inc(step, 1)
                    dve.wait_ge(step, n + 1)
                    dve.tensor_tensor(C["root"][:, :], RSTD[:, :], RSTD[:, :], ALU.mult).then_inc(step, 1)
                    dve.tensor_scalar(C["root2"][:, :], MV[:, :, 1], EPS, None, ALU.add).then_inc(step, 1)
                    dve.wait_ge(step, n + 3)
                    dve.tensor_tensor(C["root"][:, :], C["root"][:, :], C["root2"][:, :], ALU.mult).then_inc(step, 1)
                    dve.wait_ge(step, n + 4)
                    dve.tensor_scalar(C["root"][:, :], C["root"][:, :], -0.5, 1.5, ALU.mult, ALU.add)\
                        .then_inc(step, 1)
                    dve.wait_ge(step, n + 5)
                    dve.tensor_tensor(RSTD[:, :], RSTD[:, :], C["root"][:, :], ALU.mult).then_inc(step, 1)
                    dve.wait_ge(step, n + 6)

                @block.scalar
                def _(act):
                    if load:
                        act.wait_ge(const, 1)
                        act.wait_ge(step, 2 * NT)
                    act.activation(C["root"][:, :], MV[:, :, 1], ACT.Sqrt, bias=C["eps"][:, 0:1]).then_inc(rooted, 1)

        C["out"] = out_v
        rstd("start", True)
        if STAGES & 1:
            attention(nc, ctx, 0, X, MV, RSTD, C,
                      {k[8:]: v for k, v in a.items() if k.startswith("L0_attn")}, scratch[0])
            rstd("ffn0", False)
        if STAGES & 2:
            moe(nc, ctx, 0, X, MV, RSTD, C, {k[7:]: v for k, v in a.items() if k.startswith("L0_ffn")},
                xbuf[0], ybuf[0], "ffn0")
            rstd("attn1", False)
        if STAGES & 4:
            attention(nc, ctx, 1, X, MV, RSTD, C,
                      {k[8:]: v for k, v in a.items() if k.startswith("L1_attn")}, scratch[1])
        if STAGES & 8:
            rstd("ffn1", False)
            moe(nc, ctx, 1, X, MV, RSTD, C, {k[7:]: v for k, v in a.items() if k.startswith("L1_ffn")},
                xbuf[1], ybuf[1], "ffn1")
        else:
            stored = sem("stored")
            with nc.Block() as block:
                @block.sync
                def _(sp):
                    sp.dma_start(out_v, X[:, :, :]).then_inc(stored, 16)
                    sp.wait_ge(stored, 16)


STAGES = 15


def kernel(**inputs):
    import numpy as _np
    import concourse.bacc as _bacc
    from concourse import mybir as _mybir
    from concourse.bass_utils import run_bass_kernel_spmd as _run

    laid = {k: _np.ascontiguousarray(v) for k, v in inputs.items()}
    order = _np.arange(P).reshape(PAIRS, 2, DQ).transpose(1, 2, 0).reshape(P)
    for m in ("L0_attn_W_UQ", "L0_attn_W_UK"):
        laid[m] = _np.ascontiguousarray(laid[m][:, order])
    both = _np.concatenate([order, P + order])
    laid["L1_attn_bqk"] = _np.ascontiguousarray(laid["L1_attn_bc"][both])
    wc = laid.pop("L1_attn_Wc")
    laid["L1_attn_WcT"] = _np.ascontiguousarray(_np.concatenate([wc[both], wc[2 * P:]]).T)
    laid["L1_attn_WoT"] = _np.ascontiguousarray(laid.pop("L1_attn_Wo").T)
    laid["L0_ffn_router"] = _np.ascontiguousarray(laid.pop("L0_ffn_router_w").T)
    laid["L1_ffn_router"] = laid.pop("L1_ffn_Wr")
    for layer, w1, b1 in (("L0_ffn_", "w1", "b1"), ("L1_ffn_", "W1", "b1")):
        e, d, h = laid[layer + w1].shape
        bias = laid.pop(layer + b1).reshape(e, h // d, d).transpose(0, 2, 1)
        laid[layer + "w1"] = _np.ascontiguousarray(_np.concatenate([laid.pop(layer + w1), bias], axis=2))
    laid["L1_ffn_w2"] = laid.pop("L1_ffn_W2")
    nc = _bacc.Bacc("TRN2", target_bir_lowering=False, num_devices=1)
    arrays, aps = {}, {}
    for name, v in laid.items():
        arrays[f"in_{name}"] = v
        aps[name] = nc.dram_tensor(f"in_{name}", v.shape, _mybir.dt.from_np(v.dtype), kind="ExternalInput").ap()
    out = nc.dram_tensor("out", (B, T, D), F32, kind="ExternalOutput").ap()
    program(nc, aps, out)
    r = _run(nc, [arrays], core_ids=[0])
    return r.results[0]["out"]
```

```python
from contextlib import ExitStack

import concourse.bass as bass
from concourse import mybir

ALU = mybir.AluOpType
ACT = mybir.ActivationFunctionType
AX = mybir.AxisListType
F32 = mybir.dt.float32
BF16 = mybir.dt.bfloat16

P = 128
D = 128
T = 512
B = 8
TT = T // P
NT = B * TT
HEADS = 16
PAIRS = HEADS // 2
DQ = 8
PARTS = 3
PRODS = 6
KQ = PRODS * DQ
KM = KQ + PARTS
TWO_ONES = (0x3F803F80 - 0x3F800000) / 2**23 + 1.0
KZ = 64
EPS = 1e-5
MASKED = -1e30
EXP_AND_LN = 6


def attention(nc, ctx, layer, X, MV, RSTD, C, w, scratch):
    causal = layer == 0
    DV = 8 if layer == 0 else 64
    scale = float(DQ) ** -0.5
    L = f"L{layer}_"
    identf, identb, maskq, maskk, bcast = C["identf"], C["identb"], C["maskq"], C["maskk"], C["bcast"]

    buffers = ExitStack()

    def sb(name, shape, dt=F32):
        return buffers.enter_context(nc.sbuf_tensor(L + name, shape, dt))

    def ps(name, shape):
        return buffers.enter_context(nc.psum_tensor(L + name, shape, F32))

    def sem(name):
        return ctx.enter_context(nc.semaphore(L + name))

    with buffers:
        XN = sb("xn", [P, 2, TT, D])
        XT = sb("xT", [P, T])
        QF = sb("qkf", [P, 2, T])
        QR = sb("qk_rest", [P, 2, T])
        QP = sb("qk_parts", [P, 2, PARTS, T], BF16)
        QA, KA = C["q_stack"], C["k_stack"]
        M = sb("neg_max", [P, 2, TT, 4])
        MR = sb("max_rest", [P, TT, 4])
        MP = sb("max_parts", [P, 2, TT, 4, PARTS], BF16)
        MT = sb("max_rows", [2 * PARTS, 2, 2, T], BF16)
        PT = sb("probs", [P, 2, TT, 2, T])
        WORK = ps("work", [P, 2, 2, T])
        S = ps("scores", [P, 2, T])
        if layer == 0:
            WDKV = sb("w_dkv", [P, 32])
            WUK = sb("w_uk", [32, D])
            WUV = sb("w_uv", [32, D])
            WUQ = sb("w_uq", [P, D])
            WO = sb("w_o", [P, 4, D])
            CT = sb("ctxT", [P, 4, T])
            CKV = sb("c_kvT", [32, T])
            V = sb("v", [P, 2, TT, HEADS, 32])
            OU = sb("o_raw", [P, 2, T])
            RB = sb("recip", [P, 2, T])
            SU = sb("sums", [P, T])
            LS = sb("log_sum", [P, T])
            R0 = sb("recip0", [P, T])
            N1 = sb("newton", [P, T])
            O = ps("o", [P, 2, T])
        else:
            WC = sb("w_c", [P, 256 + HEADS * DV])
            WO = sb("w_oT", [P, PAIRS, D])
            BQK = sb("b_qk", [P, 2])
            BV = sb("b_v", [P, 2, T])
            BO = sb("b_o", [P, 1])
            CT = sb("ctxT", [P, PAIRS, T])
            V = sb("v", [P, 2, TT, HEADS, DV])
            VB = sb("v_biased", [P, 2, T])
            PS = sb("prob_sums", [P, 2, 2, T])
            RB = sb("recip", [P, T])
            SU = sb("sums", [P, T])
            LS = sb("log_sum", [P, T])
            R0 = sb("recip0", [P, T])
            N1 = sb("newton", [P, T])
            PJ = sb("proj", [P, T])
            PL = sb("proj_leaky", [P, T])
            ones64 = sb("ones64", [P, 64])
            O = ps("o", [P, 2, T])

        weights = sem("weights")
        cleared = sem("cleared")
        ln_done = sem("ln_done")
        xt_done = sem("xt_done")
        qk_raw = sem("qk_raw")
        rest_done = sem("rest_done")
        rounded = sem("rounded")
        parts_done = sem("parts_done")
        spilled = sem("spilled")
        stacked = sem("stacked")
        v_done = sem("v_done")
        w_full = [sem(f"w_full{i}") for i in range(2)]
        w_free = [sem(f"w_free{i}") for i in range(2)]
        su_done = sem("su_done")
        ls_done = sem("ls_done")
        r0_done = sem("r0_done")
        n1_done = sem("n1_done")
        max_done = sem("max_done")
        mstep = sem("mstep")
        mp_done = sem("mp_done")
        mt_done = sem("mt_done")
        m_loaded = sem("m_loaded")
        s_full = sem("s_full")
        exp_done = sem("exp_done")
        pv_done = sem("pv_done")
        ct_done = sem("ct_done")
        x_done = sem("x_done")
        stat = sem("stat")
        if layer == 0:
            ckv_done = sem("ckv_done")
            ou_done = sem("ou_done")
            rb_done = sem("rb_done")
        else:
            leaky = sem("leaky")
            ps_done = sem("ps_done")
            rb_done = sem("rb_done")
            qb_done = sem("qb_done")
            pj_done = sem("pj_done")
            pl_done = sem("pl_done")

        if layer == 0:
            AUX = [(0, 2, "XT", "nxt"), (0, 3, "MT1", "cur"), (1, 0, "CQ", "nxt"), (1, 1, "KV", "nxt"),
                   (1, 2, "BC3", "lag"), (2, 2, "MT2", "cur"), (2, 3, "OUT", "lag"), (3, 2, "BC0", "cur"),
                   (4, 2, "MT3", "cur"), (5, 2, "BC1", "cur"), (6, 2, "MT0", "nxt"), (7, 2, "BC2", "cur")]
        else:
            AUX = [(0, 2, "XT", "nxt"), (0, 3, "MT1", "cur"), (1, 0, "QK", "nxt"), (1, 1, "PJ", "lag"),
                   (2, 0, "PTR", "lag"), (2, 1, "V0", "nxt"), (2, 2, "V1", "nxt"), (2, 3, "MT2", "cur"),
                   (3, 0, "V2", "nxt"), (3, 1, "V3", "nxt"), (4, 3, "MT3", "cur"), (6, 3, "MT0", "nxt")]

        def kinds(body):
            return {"first": {"nxt"}, "zero": {"cur", "nxt"}, "mid": {"cur", "nxt", "lag"},
                    "seven": {"cur", "lag"}, "tail": {"lag"}}[body]

        SUM_AT = 2

        def after(body, p):
            return ("cur" if p > 0 else "lag") in kinds(body)

        def job_list(body):
            jobs = []
            for p in range(PAIRS):
                for q in range(TT):
                    if ("cur" if p < 4 else "nxt") in kinds(body):
                        jobs.append(("S1", p, q))
                    jobs += [(n, p, q) for (pp, qq, n, k) in AUX if (pp, qq) == (p, q) and k in kinds(body)]
                    if layer == 1 and q == SUM_AT and after(body, p):
                        jobs.append(("SUM", p, q))
            return jobs

        JOBS = {k: job_list(k) for k in ("first", "zero", "mid", "seven", "tail")}

        MID = len(JOBS["mid"])
        assert MID % 2 == 0

        def turn(body, b, name, p, q):
            before = JOBS[body].index((name, p, q))
            if body != "first":
                before += len(JOBS["first"])
            if body in ("mid", "seven", "tail"):
                before += len(JOBS["zero"])
            if body in ("seven", "tail"):
                before += (B - 2) * MID
            if body == "tail":
                before += len(JOBS["seven"])
            uses = before // 2
            return before % 2, uses if body != "mid" else (b - 1) * (MID // 2) + uses

        def bodies(eng, run):
            run("first", -1, 1)
            run("zero", 0, 0)
            with eng.Fori(0, (B - 2) // 2) as i:
                run("mid", 2 * i + 1, 1)
                run("mid", 2 * i + 2, 0)
            run("seven", B - 1, 1)
            run("tail", B, 0)

        def wait_apart(eng, semaphore, value):
            value = value if isinstance(value, int) else eng.to_reg(value)
            eng.wait_ge(weights, LANDED)
            eng.wait_ge(semaphore, value)

        def aux_at(body, p, q):
            return [n for (pp, qq, n, k) in AUX if (pp, qq) == (p, q) and k in kinds(body)]

        LANDED = 16 * (8 if layer == 0 else 5)

        STACKED = 12 * 16
        SPILLED = 4 * 16
        RS0 = 1 if layer == 0 else 0
        MROWS = 2 * 16

        with nc.Block() as block:

            @block.sync
            def _(sp):
                if layer == 0:
                    sp.dma_start(WDKV[:], w["W_DKV"]).then_inc(weights, 16)
                    sp.dma_start(WUK[:], w["W_UK"]).then_inc(weights, 16)
                    sp.dma_start(WUV[:], w["W_UV"]).then_inc(weights, 16)
                    sp.dma_start(WUQ[:], w["W_UQ"]).then_inc(weights, 16)
                    sp.wait_ge(cleared, 1)
                    rows = w["W_O"].rearrange("(g j d) n -> j d g n", g=4, j=4)
                    for j in range(4):
                        sp.dma_start(WO[32 * j:32 * j + DV, :, :], rows[j]).then_inc(weights, 16)
                else:
                    sp.dma_start(WC[:], w["WcT"]).then_inc(weights, 16)
                    sp.dma_start(WO[:], w["WoT"].rearrange("(c p) n -> p c n", p=P)).then_inc(weights, 16)
                    sp.dma_start(BQK[:], w["bqk"].rearrange("(a p) -> p a", p=P),
                                 allow_slow_non_contiguous=True).then_inc(weights, 16)
                    sp.dma_start(BO[:], w["bo"].rearrange("(p a) -> p a", a=1),
                                 allow_slow_non_contiguous=True).then_inc(weights, 16)
                    sp.dma_start(BV[:, :, :], w["bc"][256:].rearrange("(a h n) -> a h n", a=1, h=2)
                                 .broadcast_to([P, 2, T])).then_inc(weights, 16)

                def max_rows(b, par, g):
                    n = 4 * b + g
                    wait_apart(sp, mt_done, n + 1)
                    for half in range(2):
                        row = 64 * half + KQ
                        sp.dma_start(QA[row:row + PARTS, par, 2 * g:2 * g + 2, :],
                                     MT[PARTS * half:PARTS * half + PARTS, g % 2, :, :]).then_inc(m_loaded, 16)

                def body(kind, b, par):
                    k = kinds(kind)
                    nxt = 1 - par
                    if "cur" in k:
                        max_rows(b, par, 1)
                    if "nxt" in k:
                        wait_apart(sp, parts_done, b + 2)
                        sl = bass.ds(b + 1, 1)
                        for a in range(2):
                            for half in range(2):
                                sp.dma_start(scratch[sl, a, half].rearrange("o i r t -> r (o i) t"),
                                             QP[64 * half:64 * half + 64, a, :, :]).then_inc(spilled, 16)
                        wait_apart(sp, spilled, SPILLED * (b + 2))
                        if kind not in ("first", "zero"):
                            wait_apart(sp, s_full, 8 * PAIRS * b)
                        for half in range(2):
                            for a, dst in ((0, QA), (1, KA)):
                                src = scratch[sl, a, half].rearrange("o i (d r) t -> (o i) d (r t)", d=DQ)
                                for r0, n, i in ((0, 3, 0), (3, 2, 1), (5, 1, 2)):
                                    row = 64 * half + DQ * r0
                                    part = src[0:n] if a == 0 else src[i:i + 1].broadcast_to([n, DQ, PAIRS * T])
                                    sp.dma_start(dst[row:row + DQ * n, nxt, :, :].rearrange("n r t -> n (r t)"),
                                                 part).then_inc(stacked, 16)
                    if "cur" in k:
                        max_rows(b, par, 2)
                        max_rows(b, par, 3)
                    if "nxt" in k:
                        max_rows(b + 1, nxt, 0)

                bodies(sp, body)
                if layer == 0:
                    fill_slots(sp, C)

            @block.gpsimd
            def _(pool):
                if layer == 0:
                    pool.memset(WO[:], 0.0).then_inc(cleared, 1)
                    pool.memset(V[:], 0.0).then_inc(rest_done, 1)
                    pool.wait_ge(rest_done, 1)
                    pool.memset(V[:, :, :, :, DV:DV + 1], 1.0).then_inc(cleared, 1)
                else:
                    pool.memset(ones64[:], 1.0).then_inc(cleared, 1)
                def split(b):
                    pool.wait_ge(rounded, 2 * b + 1)
                    pool.tensor_tensor(QR[:, :, :], QF[:, :, :], QP[:, :, 0, :], ALU.subtract).then_inc(rest_done, 1)
                    pool.wait_ge(rounded, 2 * b + 2)
                    pool.tensor_tensor(QP[:, :, 2, :], QR[:, :, :], QP[:, :, 1, :], ALU.subtract).then_inc(parts_done, 1)

                def split_max(b, g):
                    n = 4 * b + g
                    wait_apart(pool, max_done, n + 1)
                    if not (isinstance(b, int) and n < 2):
                        wait_apart(pool, mt_done, n - 1)
                    m, mp = M[:, g % 2], MP[:, g % 2]
                    pool.tensor_copy(mp[:, :, :, 0], m).then_inc(mstep, 1)
                    pool.wait_ge(mstep, 3 * n + 1)
                    pool.tensor_tensor(MR[:, :, :], m, mp[:, :, :, 0], ALU.subtract).then_inc(mstep, 1)
                    wait_apart(pool, mstep, 3 * n + 2)
                    pool.tensor_copy(mp[:, :, :, 1], MR[:, :, :]).then_inc(mstep, 1)
                    pool.wait_ge(mstep, 3 * n + 3)
                    pool.tensor_tensor(mp[:, :, :, 2], MR[:, :, :], mp[:, :, :, 1], ALU.subtract).then_inc(mp_done, 1)

                def sum_keys(b, p, par):
                    s = PAIRS * b + p
                    pp = p % 2
                    if not (isinstance(b, int) and s < 2):
                        pool.wait_ge(r0_done, s - 1)
                    for kt in range(1, TT):
                        pool.wait_ge(exp_done, 8 * s + 2 * kt + 2)
                        a = PT[:, pp, 0] if kt == 1 else PS[:, pp]
                        if kt > 1:
                            pool.wait_ge(ps_done, 3 * s + kt - 1)
                        pool.tensor_tensor(PS[:, pp], a, PT[:, pp, kt], ALU.add).then_inc(ps_done, 1)

                def context0(b, g):
                    n = 4 * b + g
                    pool.wait_ge(ou_done, n + 1)
                    pool.wait_ge(rb_done, n + 1)
                    if g == 0 and not (isinstance(b, int) and b == 0):
                        pool.wait_ge(x_done, b)
                    pool.tensor_tensor(CT[:, g, :], OU[:, g % 2, :], RB[:, g % 2, :], ALU.mult).then_inc(ct_done, 1)

                def body(kind, b, par):
                    k = kinds(kind)
                    for p in range(PAIRS):
                        if p == 1 and "nxt" in k:
                            split(b + 1)
                        if layer == 1 and "cur" in k:
                            sum_keys(b, p, par)
                        if p % 2 == 1:
                            g = (p // 2 + 2) % 4
                            if ("cur" if p < 4 else "nxt") in k:
                                split_max(b if p < 4 else b + 1, g)
                        if layer == 0:
                            if p == 1 and "lag" in k:
                                context0(b - 1, 3)
                            if p in (3, 5, 7) and "cur" in k:
                                context0(b, (p - 3) // 2)

                bodies(pool, body)

            @block.vector
            def _(dve):
                def layernorm(b, par):
                    tile0 = b * TT
                    for t in range(TT):
                        if t == 0 and not (isinstance(b, int) and b < 2):
                            dve.wait_ge(xt_done, b - 1)
                        x = X[:, tile0 + t, :] if isinstance(b, int) else X[:, bass.ds(tile0 + t, 1), :]
                        mean = MV[:, tile0 + t, 0:1] if isinstance(b, int) else \
                            MV[:, bass.ds(tile0 + t, 1), 0:1].rearrange("p a o -> p (a o)")
                        rstd = RSTD[:, tile0 + t:tile0 + t + 1] if isinstance(b, int) else \
                            RSTD[:, bass.ds(tile0 + t, 1)]
                        o = XN[:, par, t, :] if isinstance(b, int) else XN[:, par, t:t + 1, :]
                        dve.tensor_scalar(o, x, mean, rstd, ALU.subtract, ALU.mult).then_inc(ln_done, 1)
                    if layer == 1:
                        dve.wait_ge(ln_done, 5 * b + 4)
                        xs = X[:, bass.ds(tile0, TT), :]
                        dve.tensor_tensor(xs, xs, XN[:, par], ALU.add).then_inc(ln_done, 1)

                def fetch_sums(h, u, n):
                    dve.wait_ge(w_full[h], u + 1)
                    if not (isinstance(n, int) and n < 2):
                        dve.wait_ge(n1_done, n - 1)
                    dve.tensor_copy(SU[:, :], WORK[:, h, 0, :]).then_inc(w_free[h], 1)
                    dve.wait_ge(w_free[h], u + 1)
                    dve.nop().then_inc(su_done, 1)

                def refine(recip, n, used):
                    dve.wait_ge(r0_done, n)
                    dve.tensor_tensor(N1[:, :], SU[:, :], R0[:, :], ALU.mult).then_inc(n1_done, 1)
                    dve.wait_ge(n1_done, n)
                    if not (isinstance(used, int) and used < 1):
                        dve.wait_ge(ct_done, used)
                    dve.scalar_tensor_tensor(recip, N1[:, :], 2.0, R0[:, :], ALU.subtract, ALU.mult)\
                        .then_inc(rb_done, 1)

                def max_unit(kind, b, p, q):
                    w = ("cur" if p < 4 else "nxt")
                    if w not in kinds(kind):
                        return
                    h, u = turn(kind, b, "S1", p, q)
                    W = WORK[:, h]
                    bb, pair = (b, p + 4) if p < 4 else (b + 1, p - 4)
                    n = 4 * bb + pair // 2
                    if q == 0 and pair % 2 == 0 and not (isinstance(bb, int) and n < 2):
                        dve.wait_ge(mp_done, n - 1)
                    dve.wait_ge(w_full[h], u + 1)
                    tile = q
                    width = (tile + 1) * P if causal else T
                    i = dve.tensor_reduce(M[:, (pair // 2) % 2, tile, 2 * (pair % 2):2 * (pair % 2) + 2],
                                          W[:, :, 0:width], AX.X, ALU.max, negate=True)
                    i.then_inc(w_free[h], 1)
                    if q == TT - 1 and pair % 2 == 1:
                        dve.wait_ge(w_free[h], u + 1)
                        dve.nop().then_inc(max_done, 1)

                def residual(kind, b, name, p, q):
                    h, u = turn(kind, b + 1, name, p, q)
                    W = WORK[:, h]
                    dve.wait_ge(w_full[h], u + 1)
                    xs = X[:, bass.ds(b * TT, TT), :]
                    if layer == 1:
                        dve.wait_ge(ln_done, 5 * b + 5)
                    dve.tensor_tensor(xs, xs, W[:, 0, :].rearrange("p (t d) -> p t d", t=TT),
                                      ALU.subtract if layer == 0 else ALU.add).then_inc(w_free[h], 1)
                    wait_apart(dve, w_free[h], u + 1)
                    for t in range(TT):
                        dve.bn_stats(ST[:, t, :], X[:, bass.ds(b * TT + t, 1), :]).then_inc(stat, 1)
                    wait_apart(dve, stat, 8 * b + 4)
                    for t in range(TT):
                        dve.bn_aggr(AG[:, t, :], ST[:, t, :]).then_inc(stat, 1)
                    dve.wait_ge(stat, 8 * b + 8)
                    dve.tensor_copy(MV[:, bass.ds(b * TT, TT), :], AG[:, :, :]).then_inc(x_done, 1)

                ST, AG = C["stats"], C["aggregate"]

                def body(kind, b, par):
                    k = kinds(kind)
                    nxt = 1 - par
                    for p in range(PAIRS):
                        if p == 0 and "nxt" in k:
                            layernorm(b + 1, nxt)
                        if p == 0 and kind == "first":
                            dve.wait_ge(weights, LANDED)
                        for q in range(TT):
                            max_unit(kind, b, p, q)
                            for n in aux_at(kind, p, q - 1):
                                if n.startswith("BC"):
                                    g = int(n[2])
                                    m = 4 * (b - 1 if g == 3 else b) + g
                                    refine(RB[:, g % 2, :], m + 1, m - 1)
                            if layer == 1 and q == SUM_AT + 1 and after(kind, p):
                                s1 = PAIRS * b + p
                                refine(RB[:, :], s1, s1 - 1)
                            for n in aux_at(kind, p, q):
                                h, u = turn(kind, b, n, p, q)
                                W = WORK[:, h]
                                if n.startswith("BC"):
                                    fetch_sums(h, u, 4 * (b - 1 if n == "BC3" else b) + int(n[2]) + 1)
                                elif n in ("OUT", "PTR"):
                                    residual(kind, b - 1, n, p, q)
                                elif n == "QK":
                                    dve.wait_ge(qb_done, 2 * b + 4)
                                    if not (isinstance(b, int) and b < 0):
                                        dve.wait_ge(parts_done, b + 1)
                                    dve.scalar_tensor_tensor(QF[:, :, :], QR2[:, :, :], 0.01, QR2[:, :, :],
                                                             ALU.mult, ALU.max).then_inc(qk_raw, 1)
                                elif n == "PJ":
                                    dve.wait_ge(pj_done, b)
                                    dve.scalar_tensor_tensor(PL[:, :], PJ[:, :], 0.01, PJ[:, :],
                                                             ALU.mult, ALU.max).then_inc(pl_done, 1)
                                elif n[0] == "V":
                                    t = int(n[1])
                                    dve.wait_ge(w_full[h], u + 1)
                                    dve.wait_ge(weights, LANDED)
                                    if t == 0 and not (isinstance(b, int) and b < 1):
                                        dve.wait_ge(pv_done, PAIRS * b)
                                    if not (isinstance(b, int) and b < 0 and t == 0):
                                        dve.wait_ge(v_done, TT * (b + 1) + t)
                                    dve.tensor_tensor(VB[:, :, :], W[:, :, :], BV[:, :, :], ALU.add).then_inc(w_free[h], 1)
                                    dve.wait_ge(w_free[h], u + 1)
                                    dve.scalar_tensor_tensor(V[:, nxt, t].rearrange("p h d -> p (h d)"),
                                                             VB[:, :, :].rearrange("p a n -> p (a n)"), 0.01,
                                                             VB[:, :, :].rearrange("p a n -> p (a n)"),
                                                             ALU.mult, ALU.max).then_inc(v_done, 1)
                            if layer == 1 and q == SUM_AT and after(kind, p):
                                h, u = turn(kind, b, "SUM", p, SUM_AT)
                                fetch_sums(h, u, PAIRS * b + p)
                        if layer == 1 and after(kind, p):
                            s1 = PAIRS * b + p
                            pair = (p - 1) % PAIRS
                            dve.wait_ge(pv_done, s1)
                            dve.wait_ge(rb_done, s1)
                            if pair == 0 and not (isinstance(b, int) and b == 0):
                                dve.wait_ge(pj_done, b)
                            dve.tensor_tensor(CT[:, pair, :], O[:, pair % 2, :], RB[:, :], ALU.mult).then_inc(ct_done, 1)

                QR2 = C["qk_biased"]
                bodies(dve, body)

            @block.scalar
            def _(act):
                QR2 = C["qk_biased"]

                def round_parts(b, i):
                    if i == 0:
                        act.wait_ge(qk_raw, b + 1)
                        if not (isinstance(b, int) and b == 0):
                            act.wait_ge(spilled, SPILLED * b)
                    else:
                        act.wait_ge(rest_done, RS0 + b + 1)
                    act.activation(QP[:, :, i, :], (QF if i == 0 else QR)[:, :, :], ACT.Copy).then_inc(rounded, 1)

                def first_reciprocal(n):
                    if not (isinstance(n, int) and n < 2):
                        act.wait_ge(rb_done, n - 1)
                    act.wait_ge(su_done, n)
                    act.activation(LS[:, :], SU[:, :], ACT.Ln).then_inc(ls_done, 1)
                    act.wait_ge(ls_done, n)
                    act.activation(R0[:, :], LS[:, :], ACT.Exp, scale=-1.0).then_inc(r0_done, 1)

                def body(kind, b, par):
                    k = kinds(kind)
                    nxt = 1 - par
                    for p in range(PAIRS):
                        s = PAIRS * b + p
                        for q in range(TT):
                            if "cur" in k:
                                if q == 0 and not (isinstance(b, int) and s < 2):
                                    act.wait_ge(pv_done, s - 1)
                                    if layer == 1:
                                        act.wait_ge(ps_done, 3 * (s - 1))
                                q0 = q * P if causal else 0
                                for half in range(2):
                                    act.wait_ge(s_full, 8 * s + 2 * q + half + 1)
                                    act.activation(PT[:, p % 2, q, half, q0:T], S[:, half, q0:T], ACT.Exp,
                                                   scale=scale).then_inc(exp_done, 1)
                            if layer == 1 and q == SUM_AT + 1 and after(kind, p):
                                first_reciprocal(s)
                            for n in aux_at(kind, p, q - 1):
                                if n.startswith("BC"):
                                    first_reciprocal(4 * (b - 1 if n == "BC3" else b) + int(n[2]) + 1)
                            if layer == 0 and q == 1 and p % 2 == 1:
                                if (p == 1 and "lag" in k) or (p > 1 and "cur" in k):
                                    m = 4 * b + (p - 3) // 2
                                    act.wait_ge(pv_done, 2 * m + 2)
                                    if not (isinstance(b, int) and m < 2):
                                        act.wait_ge(ct_done, m - 1)
                                    act.activation(OU[:, ((p - 3) // 2) % 2, :], O[:, ((p - 3) // 2) % 2, :],
                                                   ACT.Copy).then_inc(ou_done, 1)
                            for n in aux_at(kind, p, q):
                                h, u = turn(kind, b, n, p, q)
                                W = WORK[:, h]
                                if n in ("OUT", "PTR") or n[0] == "V" or n.startswith("BC"):
                                    continue
                                act.wait_ge(w_full[h], u + 1)
                                if n.startswith("MT"):
                                    g = int(n[2])
                                    m = 4 * (b + 1 if g == 0 else b) + g
                                    if not (isinstance(b, int) and m < 2):
                                        act.wait_ge(m_loaded, MROWS * (m - 1))
                                    act.activation(MT[:, g % 2, :, :].rearrange("r p t -> r (p t)"),
                                                   W[0:2 * PARTS, 0, :].bitcast(BF16), ACT.Copy).then_inc(w_free[h], 1)
                                    act.wait_ge(w_free[h], u + 1)
                                    act.nop().then_inc(mt_done, 1)
                                elif n == "XT":
                                    act.activation(XT[:, :], W[:, 0, :], ACT.Copy).then_inc(w_free[h], 1)
                                    act.wait_ge(w_free[h], u + 1)
                                    act.nop().then_inc(xt_done, 1)
                                elif n == "CQ":
                                    if not (isinstance(b, int) and b < 0):
                                        act.wait_ge(parts_done, b + 1)
                                    act.activation(CKV[:, :], W[0:32, 0, :], ACT.Copy).then_inc(ckv_done, 1)
                                    act.activation(QF[:, 0, :], W[:, 1, :], ACT.Copy).then_inc(w_free[h], 1)
                                elif n == "KV":
                                    if isinstance(b, int) and b < 1:
                                        act.wait_ge(cleared, 2)
                                    else:
                                        act.wait_ge(pv_done, PAIRS * b)
                                    act.activation(V[:, nxt, :, :, 0:DV],
                                                   W[:, 1, :].rearrange("p (t h d) -> p t h d", t=TT, d=DV),
                                                   ACT.Copy).then_inc(v_done, 1)
                                    act.activation(QF[:, 1, :], W[:, 0, :], ACT.Copy).then_inc(w_free[h], 1)
                                    act.wait_ge(w_free[h], u + 1)
                                    act.nop().then_inc(qk_raw, 1)
                                elif n == "QK":
                                    act.wait_ge(weights, LANDED)
                                    if not (isinstance(b, int) and b < 0):
                                        act.wait_ge(qk_raw, b + 1)
                                    act.activation(QR2[:, 0, :], W[:, 0, :], ACT.Identity,
                                                   bias=BQK[:, 0:1]).then_inc(qb_done, 1)
                                    act.activation(QR2[:, 1, :], W[:, 1, :], ACT.Identity,
                                                   bias=BQK[:, 1:2]).then_inc(w_free[h], 1)
                                    act.wait_ge(w_free[h], u + 1)
                                    act.nop().then_inc(qb_done, 1)
                                elif n == "PJ":
                                    if not (isinstance(b, int) and b < 2):
                                        act.wait_ge(pl_done, b - 1)
                                    act.activation(PJ[:, :], W[:, 0, :], ACT.Identity, scale=-1.0,
                                                   bias=BO[:, 0:1]).then_inc(w_free[h], 1)
                                    act.wait_ge(w_free[h], u + 1)
                                    act.nop().then_inc(pj_done, 1)
                            if p == 1 and q in (1, 3) and "nxt" in k:
                                round_parts(b + 1, q // 2)

                act.add_instruction(mybir.InstLoadActFuncSet(name=nc.get_next_instruction_name(), ins=[], outs=[],
                                                             act_func_set_id=EXP_AND_LN))
                bodies(act, body)

            @block.tensor
            def _(pe):
                def s1(kind, b, par, p, q):
                    w = ("cur" if p < 4 else "nxt")
                    if w not in kinds(kind):
                        return
                    h, u = turn(kind, b, "S1", p, q)
                    W = WORK[:, h]
                    bb, pb, pair = (b, par, p + 4) if p < 4 else (b + 1, 1 - par, p - 4)
                    if not (isinstance(u, int) and u == 0):
                        pe.wait_ge(w_free[h], u)
                    if p == 4 and q == 0:
                        pe.wait_ge(stacked, STACKED * (bb + 1))
                    width = (q + 1) * P if causal else T
                    for half in range(2):
                        r = 64 * half
                        i = pe.matmul(W[:, half, 0:width], QA[r:r + KQ, pb, pair, q * P:(q + 1) * P],
                                      KA[r:r + KQ, pb, pair, 0:width], start=True, stop=not causal)
                    if causal:
                        for half in range(2):
                            i = pe.matmul(W[:, half, q * P:(q + 1) * P], identb[:, :], maskq[:, :],
                                          start=False, stop=True)
                    i.then_inc(w_full[h], 1)

                def s2(b, par, p, q):
                    s = PAIRS * b + p
                    if q == 0 and p % 2 == 0:
                        pe.wait_ge(m_loaded, MROWS * (4 * b + p // 2 + 1))
                    q0 = q * P if causal else 0
                    for half in range(2):
                        if not (isinstance(b, int) and s == 0 and q == 0):
                            pe.wait_ge(exp_done, 8 * s + 2 * q + half - 1)
                        r = 64 * half
                        i = pe.matmul(S[:, half, q0:T], KA[r:r + KZ, par, p, q * P:(q + 1) * P],
                                      QA[r:r + KZ, par, p, q0:T], start=True, stop=not causal)
                        if causal:
                            i = pe.matmul(S[:, half, q0:q0 + P], identb[:, :], maskk[:, :],
                                          start=False, stop=True)
                        i.then_inc(s_full, 1)

                def pv(b, par, p, q):
                    s = PAIRS * b + p
                    if p == 0 and q == 0:
                        pe.wait_ge(v_done, (b + 1) * (1 if layer == 0 else TT))
                    q0 = q * P if causal else 0
                    for half in range(2):
                        pe.wait_ge(exp_done, 8 * s + 2 * q + half + 1)
                        if layer == 0:
                            if q == 0 and half == 0 and p % 2 == 0 and not (isinstance(b, int) and s < 4):
                                pe.wait_ge(ou_done, 4 * b + p // 2 - 1)
                            r = 32 * (2 * (p % 2) + half)
                            i = pe.matmul(O[r:r + 32, (p // 2) % 2, q0:T], V[:, par, q, 2 * p + half, :],
                                          PT[:, p % 2, q, half, q0:T], start=(q == 0), stop=(q == TT - 1))
                        else:
                            if q == 0 and half == 0 and not (isinstance(b, int) and s < 2):
                                pe.wait_ge(ct_done, s - 1)
                            r = 64 * half
                            i = pe.matmul(O[r:r + 64, p % 2, :], V[:, par, q, 2 * p + half, :],
                                          PT[:, p % 2, q, half, :], start=(q == 0), stop=(q == TT - 1))
                    if q == TT - 1:
                        i.then_inc(pv_done, 1)

                def sums(kind, b, p):
                    h, u = turn(kind, b, "SUM", p, SUM_AT)
                    s = PAIRS * b + p
                    pe.wait_ge(w_free[h], u)
                    pe.wait_ge(ps_done, 3 * s)
                    for half in range(2):
                        i = pe.matmul(WORK[64 * half:64 * half + 64, h, 0, :], ones64[:, :],
                                      PS[:, (p - 1) % 2, half, :], start=True, stop=True)
                    i.then_inc(w_full[h], 1)

                def aux(kind, b, par, n, p, q):
                    h, u = turn(kind, b, n, p, q)
                    W = WORK[:, h]
                    if not (isinstance(u, int) and u == 0):
                        pe.wait_ge(w_free[h], u)
                    nxt = 1 - par
                    if kind == "first" and n in ("CQ", "QK"):
                        pe.wait_ge(weights, LANDED)
                        pe.wait_ge(cleared, 2 if layer == 0 else 1)
                    if n.startswith("MT"):
                        g = int(n[2])
                        m = 4 * (b + 1 if g == 0 else b) + g
                        pe.wait_ge(mp_done, m + 1)
                        for pair in range(2):
                            for t in range(TT):
                                col = (pair * TT + t) * P // 2
                                i = pe.transpose(W[0:2 * PARTS, 0, col:col + P // 2].bitcast(BF16),
                                                 MP[:, g % 2, t, 2 * pair:2 * pair + 2].rearrange("p h i -> p (h i)"),
                                                 identb[:, :])
                    elif n == "XT":
                        pe.wait_ge(ln_done, 4 * (b + 2) if layer == 0 else 5 * (b + 1) + 4)
                        for t in range(TT):
                            i = pe.transpose(W[:, 0, t * P:(t + 1) * P], XN[:, nxt, t, :], identf[:, :])
                    elif n == "CQ":
                        pe.wait_ge(xt_done, b + 2)
                        pe.matmul(W[0:32, 0, :], WDKV[:, :], XT[:, :], start=True, stop=True)
                        i = pe.matmul(W[:, 1, :], WUQ[:, :], XT[:, :], start=True, stop=True)
                    elif n == "KV":
                        pe.wait_ge(ckv_done, b + 2)
                        pe.matmul(W[:, 0, :], WUK[:, :], CKV[:, :], start=True, stop=True)
                        for t in range(TT):
                            i = pe.matmul(W[:, 1, t * P:(t + 1) * P], CKV[:, t * P:(t + 1) * P], WUV[:, :],
                                          start=True, stop=True)
                    elif n == "QK":
                        pe.wait_ge(xt_done, b + 2)
                        for a in range(2):
                            i = pe.matmul(W[:, a, :], WC[:, a * P:(a + 1) * P], XT[:, :], start=True, stop=True)
                    elif n[0] == "V":
                        t = int(n[1])
                        for a in range(2):
                            i = pe.matmul(W[:, a, :], XT[:, t * P:(t + 1) * P], WC[:, 256 + a * T:256 + (a + 1) * T],
                                          start=True, stop=True)
                    elif n.startswith("BC"):
                        g = int(n[2])
                        m = 4 * (b - 1 if g == 3 else b) + g
                        pe.wait_ge(ou_done, m + 1)
                        i = pe.matmul(W[:, 0, :], bcast[:, :], OU[:, g % 2, :], start=True, stop=True)
                    elif n == "OUT":
                        pe.wait_ge(ct_done, 4 * b)
                        for t in range(TT):
                            for g in range(4):
                                i = pe.matmul(W[:, 0, t * P:(t + 1) * P], CT[:, g, t * P:(t + 1) * P], WO[:, g, :],
                                              start=(g == 0), stop=(g == 3))
                    elif n == "PJ":
                        pe.wait_ge(ct_done, PAIRS * b)
                        for c in range(PAIRS):
                            i = pe.matmul(W[:, 0, :], WO[:, c, :], CT[:, c, :], start=(c == 0), stop=(c == PAIRS - 1))
                    elif n == "PTR":
                        pe.wait_ge(pl_done, b)
                        for t in range(TT):
                            i = pe.transpose(W[:, 0, t * P:(t + 1) * P], PL[:, t * P:(t + 1) * P], identf[:, :])
                    i.then_inc(w_full[h], 1)

                def body(kind, b, par):
                    k = kinds(kind)
                    for p in range(PAIRS):
                        lagging = after(kind, p)
                        lb, lpar, lp = (b, par, p - 1) if p > 0 else (b - 1, 1 - par, PAIRS - 1)
                        for q in range(TT):
                            if "cur" in k:
                                s2(b, par, p, q)
                            s1(kind, b, par, p, q)
                            if lagging:
                                pv(lb, lpar, lp, q)
                            for n in aux_at(kind, p, q):
                                aux(kind, b, par, n, p, q)
                            if layer == 1 and q == SUM_AT and lagging:
                                sums(kind, b, p)

                bodies(pe, body)


E = 8
H = 512
HC = H // P
CAP = 768
TS = 256
SC = TS // P
DEPTH = 6
assert E * CAP // TS % DEPTH == 0


def moe(nc, ctx, layer, X, MV, RSTD, C, w, xbuf, ybuf):
    TOP = 1 if layer == 0 else 2
    NTILES = E * CAP // TS if layer == 0 else (TOP * B * T + E * (TS - 1)) // TS
    SLOTS = NTILES * TS
    func = ACT.Gelu if layer == 0 else ACT.Relu
    L = f"F{layer}_"
    buffers = ExitStack()

    def sb(name, shape, dt=F32):
        return buffers.enter_context(nc.sbuf_tensor(L + name, shape, dt))

    def sem(name):
        return ctx.enter_context(nc.semaphore(L + name))

    U32, I32 = mybir.dt.uint32, mybir.dt.int32
    with buffers:
        SLOT = sb("slot", [P, TOP, NT], U32)
        GATE = sb("gate", [P, TOP, NT])
        OWNER = sb("owner", [1, NTILES], I32)
        XN = sb("xn", [P, NT, ROW])
        routing = ExitStack()

        def rb(name, shape, dt=F32):
            return routing.enter_context(nc.sbuf_tensor(L + name, shape, dt))

        with routing:
            XT = rb("xT", [P, 2, T])
            LG = rb("logits", [P, NT, E])
            WR = rb("w_router", [P, E])
            BR = rb("b_router", [P, E])
            OH = rb("onehot", [P, TOP, NT, E])
            OHB = rb("onehot_b", [P, NT, E], BF16)
            TMP = rb("tmp", [P, NT, E])
            TM2 = rb("tmp2", [P, NT, E])
            CNT = rb("counts", [P, 2, NT + 1, E])
            TOPV = rb("top", [P, TOP, NT])
            PICK = rb("pick", [P, NT])
            RANK = rb("rank", [P, NT])
            KEEP = rb("keep", [P, NT])
            W8 = rb("w8", [P, E])
            ECAP = rb("ecap", [P, E])
            SPILL = rb("spill", [P, NT])
            TRI = rb("tri", [P, P], BF16)
            ONE = rb("one", [P, P], BF16)
            TRIF = rb("trif", [P, P])
            TN = rb("tiles", [P, 2, E])
            TNI = rb("tiles_i", [P, E], I32)
            JT = rb("jt", [1, NTILES])
            JC = rb("jc", [1, NTILES, E])
            JI = rb("jf", [1, NTILES])
            with (nc.psum_tensor(L + "xt_ps", [P, 2, T], F32) as XTP,
                  nc.psum_tensor(L + "lg_ps", [P, NT * E], F32) as LGP,
                  nc.psum_tensor(L + "rk_ps", [P, 2, T], F32) as RKP):
                w_in = sem("w_in")
                ln = sem("ln")
                xtp = sem("xtp")
                xts = sem("xts")
                lgp = sem("lgp")
                lgs = sem("lgs")
                const = sem("const")
                st = sem("st")
                chosen = sem("chosen")
                expd = sem("expd")
                ranked = sem("ranked")
                slotted = sem("slotted")

                def sl(t, n):
                    return bass.ds(t, n)

                with nc.Block() as block:
                    @block.sync
                    def _(sp):
                        sp.dma_start(WR[:, :], w["router"]).then_inc(w_in, 16)
                        if layer == 1:
                            sp.dma_start(BR[:, :], w["br"].rearrange("(a e) -> a e", a=1)
                                         .broadcast_to([P, E])).then_inc(w_in, 16)

                    @block.gpsimd
                    def _(pool):
                        pool.iota(W8[:, :], pattern=[[-1, E]], base=E, channel_multiplier=0,
                                  allow_small_or_imprecise_dtypes=True).then_inc(const, 1)
                        pool.iota(ECAP[:, :], pattern=[[CAP, E]], base=0, channel_multiplier=0,
                                  allow_small_or_imprecise_dtypes=True).then_inc(const, 1)
                        pool.iota(SPILL[:, :], pattern=[[P, NT]], base=E * CAP, channel_multiplier=1,
                                  allow_small_or_imprecise_dtypes=True).then_inc(const, 1)
                        if layer == 1:
                            pool.iota(JI[:, :], pattern=[[1, NTILES]], base=0, channel_multiplier=0,
                                      allow_small_or_imprecise_dtypes=True).then_inc(const, 1)
                        else:
                            pool.iota(OWNER[:, :], pattern=[[1, E], [0, CAP // TS]], base=0,
                                      channel_multiplier=0).then_inc(const, 1)
                        pool.memset(ONE[:, :], 1.0).then_inc(const, 1)
                        pool.memset(TRIF[:, :], 1.0).then_inc(const, 1)
                        pool.memset(CNT[:, :, 0:1, :], 0.0).then_inc(const, 1)
                        pool.wait_ge(const, 7)
                        pool.affine_select(out=TRI[:, :], in_=TRIF[:, :], compare_op=ALU.is_gt, fill=0.0,
                                           base=0, pattern=[[1, P]], channel_multiplier=-1).then_inc(const, 1)

                    @block.vector
                    def _(dve):
                        with dve.Fori(0, B) as b:
                            for t in range(TT):
                                tile = b * TT + t
                                dve.tensor_scalar(XN[:, sl(tile, 1), 0:D], X[:, sl(tile, 1), :],
                                                  MV[:, sl(tile, 1), 0:1].rearrange("p a o -> p (a o)"),
                                                  RSTD[:, sl(tile, 1)], ALU.subtract, ALU.mult).then_inc(ln, 1)
                        dve.wait_ge(w_in, 16 * (1 + layer))
                        dve.wait_ge(lgp, B)
                        lg_in = LGP[:, :].rearrange("p (t e) -> p t e", t=NT)
                        if layer == 0:
                            dve.tensor_copy(LG[:, :, :], lg_in).then_inc(lgs, 1)
                        else:
                            dve.tensor_tensor(LG[:, :, :], lg_in, BR[:, :].rearrange("p (a e) -> p a e", a=1)
                                              .broadcast_to([P, NT, E]), ALU.add).then_inc(lgs, 1)

                        n = [0]

                        def step(ins):
                            ins.then_inc(st, 1)
                            n[0] += 1
                            dve.wait_ge(st, n[0])

                        dve.wait_ge(lgs, 1)
                        dve.wait_ge(const, 8)

                        def over_e(x):
                            return x.rearrange("p (t a) -> p t a", a=1).broadcast_to([P, NT, E])

                        def over_t(x):
                            return x.rearrange("p (a e) -> p a e", a=1).broadcast_to([P, NT, E])

                        src = LG
                        for k in range(TOP):
                            step(dve.tensor_reduce(TOPV[:, k, :], src[:, :, :], AX.X, ALU.max))
                            step(dve.tensor_tensor(TMP[:, :, :], src[:, :, :], over_e(TOPV[:, k, :]), ALU.is_equal))
                            step(dve.tensor_tensor(TMP[:, :, :], TMP[:, :, :], over_t(W8[:, :]), ALU.mult))
                            step(dve.tensor_reduce(PICK[:, :], TMP[:, :, :], AX.X, ALU.max))
                            step(dve.tensor_tensor(OH[:, k], over_t(W8[:, :]), over_e(PICK[:, :]), ALU.is_equal))
                            if k + 1 < TOP:
                                step(dve.scalar_tensor_tensor(TM2[:, :, :].rearrange("p t e -> p (t e)"),
                                                              OH[:, k].rearrange("p t e -> p (t e)"), -3e38,
                                                              LG[:, :, :].rearrange("p t e -> p (t e)"),
                                                              ALU.mult, ALU.add))
                                src = TM2
                        if layer == 0:
                            step(dve.tensor_copy(OHB[:, :, :], OH[:, 0]))
                            dve.tensor_tensor(TMP[:, :, :], LG[:, :, :], over_e(TOPV[:, 0, :]), ALU.subtract)\
                                .then_inc(chosen, 1)
                        else:
                            step(dve.tensor_tensor(OHB[:, :, :], OH[:, 0], OH[:, 1], ALU.add))
                            dve.tensor_tensor(PICK[:, :], TOPV[:, 1, :], TOPV[:, 0, :], ALU.subtract).then_inc(chosen, 1)
                        dve.wait_ge(chosen, 1)
                        dve.wait_ge(expd, 1)
                        if layer == 0:
                            step(dve.tensor_reduce(PICK[:, :], TM2[:, :, :], AX.X, ALU.add))
                            step(dve.reciprocal(GATE[:, 0, :], PICK[:, :]))
                        else:
                            step(dve.tensor_scalar(RANK[:, :], KEEP[:, :], 1.0, None, ALU.add))
                            step(dve.reciprocal(GATE[:, 0, :], RANK[:, :]))
                            step(dve.tensor_tensor(GATE[:, 1, :], GATE[:, 0, :], KEEP[:, :], ALU.mult))
                        dve.wait_ge(ranked, 1)
                        step(dve.tensor_copy(CNT[:, 0, 1:NT + 1, :],
                                             RKP[:, 1, 0:NT * E].rearrange("p (t e) -> p t e", e=E)))
                        cur, d = 0, 1
                        while d < NT + 1:
                            nx = 1 - cur
                            step(dve.tensor_tensor(CNT[:, nx, d:NT + 1, :], CNT[:, cur, d:NT + 1, :],
                                                   CNT[:, cur, 0:NT + 1 - d, :], ALU.add))
                            step(dve.tensor_copy(CNT[:, nx, 0:d, :], CNT[:, cur, 0:d, :]))
                            cur, d = nx, 2 * d
                        total = CNT[:, cur, NT, :]
                        step(dve.tensor_tensor(TMP[:, :, :], RKP[:, 0, 0:NT * E].rearrange("p (t e) -> p t e", e=E),
                                               CNT[:, cur, 0:NT, :], ALU.add))
                        if layer == 0:
                            step(dve.tensor_tensor(TM2[:, :, :], TMP[:, :, :], OH[:, 0], ALU.mult))
                            step(dve.tensor_reduce(RANK[:, :], TM2[:, :, :], AX.X, ALU.add))
                            step(dve.tensor_scalar(KEEP[:, :], RANK[:, :], CAP - 0.5, None, ALU.is_lt))
                            step(dve.tensor_tensor(GATE[:, 0, :], GATE[:, 0, :], KEEP[:, :], ALU.mult))
                            step(dve.tensor_tensor(TM2[:, :, :], OH[:, 0], over_t(ECAP[:, :]), ALU.mult))
                            step(dve.tensor_reduce(PICK[:, :], TM2[:, :, :], AX.X, ALU.add))
                            step(dve.tensor_tensor(RANK[:, :], RANK[:, :], PICK[:, :], ALU.add))
                            step(dve.tensor_tensor(RANK[:, :], RANK[:, :], SPILL[:, :], ALU.subtract))
                            step(dve.tensor_tensor(RANK[:, :], RANK[:, :], KEEP[:, :], ALU.mult))
                            step(dve.tensor_tensor(RANK[:, :], RANK[:, :], SPILL[:, :], ALU.add))
                            dve.tensor_copy(SLOT[:, 0, :], RANK[:, :]).then_inc(slotted, 1)
                        else:
                            step(dve.tensor_scalar(TN[:, 0, :], total, 1.0 / TS, (TS - 1.0 - (TS - 1) / 2.0) / TS,
                                                   ALU.mult, ALU.add))
                            step(dve.tensor_copy(TNI[:, :], TN[:, 0, :]))
                            step(dve.tensor_copy(TN[:, 0, :], TNI[:, :]))
                            cur, d = 0, 1
                            while d < E:
                                nx = 1 - cur
                                step(dve.tensor_tensor(TN[:, nx, d:E], TN[:, cur, d:E], TN[:, cur, 0:E - d], ALU.add))
                                step(dve.tensor_copy(TN[:, nx, 0:d], TN[:, cur, 0:d]))
                                cur, d = nx, 2 * d
                            ends = TN[:, cur, :]
                            step(dve.tensor_tensor(JC[:, :, :], JI[:, :].rearrange("p (j a) -> p j a", a=1)
                                                   .broadcast_to([1, NTILES, E]),
                                                   ends[0:1].rearrange("p (a e) -> p a e", a=1)
                                                   .broadcast_to([1, NTILES, E]), ALU.is_ge))
                            step(dve.tensor_reduce(JT[:, :], JC[:, :, :], AX.X, ALU.add))
                            step(dve.tensor_scalar(OWNER[:, :], JT[:, :], E - 1.0, None, ALU.min))
                            step(dve.tensor_copy(ECAP[:, :], TNI[:, :]))
                            step(dve.tensor_tensor(ECAP[:, :], ends, ECAP[:, :], ALU.subtract))
                            step(dve.tensor_scalar(ECAP[:, :], ECAP[:, :], float(TS), None, ALU.mult))
                            step(dve.tensor_tensor(TMP[:, :, :], TMP[:, :, :], over_t(ECAP[:, :]), ALU.add))
                            for k in range(TOP):
                                step(dve.tensor_tensor(TM2[:, :, :], TMP[:, :, :], OH[:, k], ALU.mult))
                                step(dve.tensor_reduce(RANK[:, :], TM2[:, :, :], AX.X, ALU.add))
                                i = dve.tensor_copy(SLOT[:, k, :], RANK[:, :])
                                if k + 1 < TOP:
                                    step(i)
                                else:
                                    i.then_inc(slotted, 1)

                    @block.scalar
                    def _(act):
                        def copy_out(b, par, first):
                            act.wait_ge(xtp, b + 1)
                            if not first:
                                act.wait_ge(lgp, b - 1)
                            act.activation(XT[:, par, :], XTP[:, par, :], ACT.Copy).then_inc(xts, 1)

                        copy_out(0, 0, True)
                        copy_out(1, 1, True)
                        with act.Fori(0, (B - 2) // 2) as i:
                            for u in range(2):
                                copy_out(2 * i + u + 2, u, False)
                        act.wait_ge(chosen, 1)
                        if layer == 0:
                            act.activation(TM2[:, :, :], TMP[:, :, :], ACT.Exp).then_inc(expd, 1)
                        else:
                            act.activation(KEEP[:, :], PICK[:, :], ACT.Exp).then_inc(expd, 1)

                    @block.tensor
                    def _(pe):
                        def transpose(b, par, first):
                            pe.wait_ge(ln, TT * (b + 1))
                            if not first:
                                pe.wait_ge(xts, b - 1)
                            for t in range(TT):
                                i = pe.transpose(XTP[:, par, t * P:(t + 1) * P],
                                                 XN[:, b * TT + t, 0:D], C["identf"][:, :])
                            i.then_inc(xtp, 1)

                        def project(b, par):
                            pe.wait_ge(xts, b + 1)
                            for t in range(TT):
                                col = (b * TT + t) * E
                                i = pe.matmul(LGP[:, col:col + E], XT[:, par, t * P:(t + 1) * P],
                                              WR[:, :], start=True, stop=True)
                            i.then_inc(lgp, 1)

                        pe.wait_ge(w_in, 16 * (1 + layer))
                        transpose(0, 0, True)
                        for b in range(B):
                            if b + 1 < B:
                                transpose(b + 1, (b + 1) % 2, b < 1)
                            project(b, b % 2)
                        pe.wait_ge(chosen, 1)
                        pe.wait_ge(const, 8)
                        ohb = OHB[:, :, :].rearrange("p t e -> p (t e)")
                        pe.matmul(RKP[:, 0, 0:NT * E], TRI[:, :], ohb, start=True, stop=True)
                        pe.matmul(RKP[:, 1, 0:NT * E], ONE[:, :], ohb, start=True, stop=True).then_inc(ranked, 1)

        work = ExitStack()

        def wb(name, shape, dt=F32):
            return work.enter_context(nc.sbuf_tensor(L + name, shape, dt))

        def wp(name, shape):
            return work.enter_context(nc.psum_tensor(L + name, shape, F32))

        with work:
            W1 = wb("w1", [P, DEPTH, H + HC])
            W2 = wb("w2", [P, DEPTH, HC, D])
            B2 = wb("b2", [P, DEPTH, D])
            XS = wb("xs", [P, DEPTH, SC, ROW])
            XST = wb("xsT", [P, 2, TS])
            HT = wb("hT", [P, 2, HC, TS])
            YB = wb("y_biased", [P, SC, D])
            YS = wb("ys", [P, 2, SC, D])
            TP = wp("tp", [P, 2, T])
            HP = wp("hp", [P, 4, T])
            YP = wp("yp", [P, 2, T])
            loaded, tiles_before = C["loaded"], layer * (E * CAP // TS) // DEPTH
            tp_full = sem("tp_full")
            xst_done = sem("xst_done")
            h_full = sem("h_full")
            h_done = sem("h_done")
            y_full = sem("y_full")
            y_done = sem("y_done")
            y_out = [sem(f"y_out{u}") for u in range(2)]
            scat = sem("scat")
            dest = sem("dest")
            biased = sem("biased")
            NL = 4

            with nc.Block() as block:
                @block.sync
                def _(sp):
                    def load(j, m, before):
                        sp.wait_ge(y_out[m % 2], 16 * SC * (before + 1))
                        weights(j, m)
                        rows(j, m)

                    def weights(j, m):
                        e = sp.value_load(OWNER[0:1, j:j + 1] if isinstance(j, int) else OWNER[0:1, bass.ds(j, 1)],
                                          min_val=0, max_val=E - 1)
                        es = bass.ds(e, 1)
                        sp.dma_start(W1[:, m, :], w["w1"][es].rearrange("o p n -> (o p) n")).then_inc(loaded[m], 16)
                        sp.dma_start(W2[:, m, :, :], w["w2"][es].rearrange("o (c p) d -> (o p) c d", p=P))\
                            .then_inc(loaded[m], 16)
                        sp.dma_start(B2[:, m, :], w["b2"][es].broadcast_to([P, D])).then_inc(loaded[m], 16)

                    def rows(j, m):
                        sp.dma_start(XS[:, m, :, :], xbuf[0:SLOTS].rearrange("(j c p) d -> j p c d", c=SC, p=P)
                                     [bass.ds(j, 1)].rearrange("o p c d -> (o p) c d")).then_inc(loaded[m], 16)

                    for j in range(DEPTH):
                        weights(j, j)
                    sp.wait_ge(scat, 16 * NT * TOP)
                    for j in range(DEPTH):
                        rows(j, j)
                    with sp.Fori(1, NTILES // DEPTH) as i:
                        for m in range(DEPTH):
                            load(DEPTH * i + m, m, DEPTH // 2 * (i - 1) + m // 2)
                    for j in range(NTILES // DEPTH * DEPTH, NTILES):
                        load(j, j % DEPTH, (j - DEPTH) // 2)

                def tiles(eng, run):
                    full = (NTILES - 2) // DEPTH * DEPTH
                    for j in range(DEPTH):
                        run(j, j % DEPTH, j % 2, j, (j + 1) // DEPTH, (j - 1) // 2)
                    with eng.Fori(1, full // DEPTH) as i:
                        for v in range(DEPTH):
                            run(DEPTH * i + v, v, v % 2, None, i + (v + 1) // DEPTH, DEPTH // 2 * i + (v - 1) // 2)
                    for j in range(full, NTILES):
                        run(j, j % DEPTH, j % 2, j, (j + 1) // DEPTH, (j - 1) // 2)

                @block.tensor
                def _(pe):
                    def transpose(j, m, u, uses):
                        pe.wait_ge(loaded[m], NL * 16 * (tiles_before + uses + 1))
                        if not (isinstance(j, int) and j < 2):
                            pe.wait_ge(xst_done, j - 1)
                        for c in range(SC):
                            i = pe.transpose(TP[:, u, c * P:(c + 1) * P], XS[:, m, c, 0:D], C["identf"][:, :])
                        i.then_inc(tp_full, 1)

                    def hidden(j, m, u):
                        pe.wait_ge(xst_done, j + 1)
                        for half in range(2):
                            if not (isinstance(j, int) and j < 2):
                                pe.wait_ge(h_done, 4 * j - 8 + 2 * half + 2)
                            for a in range(2):
                                c = 2 * half + a
                                i = pe.matmul(HP[:, 2 * u + half, a * TS:(a + 1) * TS], W1[:, m, c * P:(c + 1) * P],
                                              XST[:, u, :], start=True, stop=True)
                            i.then_inc(h_full, 1)

                    def result(j, m, u):
                        pe.wait_ge(h_done, 4 * j + 4)
                        if not (isinstance(j, int) and j < 2):
                            pe.wait_ge(y_done, j - 1)
                        for s in range(SC):
                            for c in range(HC):
                                i = pe.matmul(YP[:, u, s * P:(s + 1) * P], HT[:, u, c, s * P:(s + 1) * P],
                                              W2[:, m, c, :], start=(c == 0), stop=(c == HC - 1))
                        i.then_inc(y_full, 1)

                    def run(j, m, u, k, uses, stores):
                        if k != NTILES - 1:
                            transpose(j + 1, (m + 1) % DEPTH, 1 - u, uses)
                        hidden(j, m, u)
                        if k != 0:
                            result(j - 1, (m - 1) % DEPTH, 1 - u)

                    transpose(0, 0, 0, 0)
                    tiles(pe, run)
                    result(NTILES - 1, (NTILES - 1) % DEPTH, (NTILES - 1) % 2)

                @block.scalar
                def _(act):
                    def run(j, m, u, k, uses, stores):
                        for c in range(HC):
                            act.wait_ge(h_full, 2 * j + c // 2 + 1)
                            if c == 0 and not (isinstance(j, int) and j < 2):
                                act.wait_ge(y_full, j - 1)
                            act.activation(HT[:, u, c, :], HP[:, 2 * u + c // 2, (c % 2) * TS:(c % 2 + 1) * TS],
                                           func, bias=W1[:, m, H + c:H + c + 1]).then_inc(h_done, 1)

                    tiles(act, run)

                @block.vector
                def _(dve):
                    def rows(j, m, u):
                        dve.wait_ge(tp_full, j + 1)
                        if not (isinstance(j, int) and j < 2):
                            dve.wait_ge(h_full, 2 * j - 2)
                        dve.tensor_copy(XST[:, u, :], TP[:, u, 0:TS]).then_inc(xst_done, 1)

                    def result(j, m, u, stores):
                        dve.wait_ge(y_full, j + 1)
                        if not (isinstance(j, int) and j < 1):
                            dve.wait_ge(y_done, j)
                        dve.tensor_tensor(YB[:, :, :], YP[:, u, 0:TS].rearrange("p (s d) -> p s d", s=SC),
                                          B2[:, m, :].rearrange("p (a d) -> p a d", a=1).broadcast_to([P, SC, D]),
                                          ALU.add).then_inc(biased, 1)
                        dve.wait_ge(biased, j + 1)
                        if not (isinstance(j, int) and j < 2):
                            dve.wait_ge(y_out[u], 16 * SC * stores)
                        dve.tensor_tensor(YS[:, u, :, :], YB[:, :, :],
                                          XS[:, m, :, D + 1:ROW].broadcast_to([P, SC, D]), ALU.mult)\
                            .then_inc(y_done, 1)

                    def run(j, m, u, k, uses, stores):
                        if k != NTILES - 1:
                            rows(j + 1, (m + 1) % DEPTH, 1 - u)
                        if k != 0:
                            result(j - 1, (m - 1) % DEPTH, 1 - u, stores)

                    rows(0, 0, 0)
                    tiles(dve, run)
                    result(NTILES - 1, (NTILES - 1) % DEPTH, (NTILES - 1) % 2, (NTILES - 1) // 2)

                @block.gpsimd
                def _(pool):
                    pool.wait_ge(C["zeroed"], 16 * ZERO_DMAS)
                    for k in range(TOP):
                        if k:
                            pool.wait_ge(scat, 16 * NT * k)
                        pool.iota(XN[:, :, D:D + 1].bitcast(I32).rearrange("p t a -> p (t a)"),
                                  pattern=[[P, NT]], base=k * B * T, channel_multiplier=1).then_inc(dest, 1)
                        pool.tensor_copy(XN[:, :, D + 1:ROW].rearrange("p t a -> p (t a)"),
                                         GATE[:, k, :]).then_inc(dest, 1)
                        pool.wait_ge(dest, 2 * k + 2)
                        for t in range(NT):
                            pool.indirect_dma_start(
                                xbuf, bass.IndirectOffsetOnAxis(ap=SLOT[:, k, t:t + 1], axis=0),
                                XN[:, t, :], None).then_inc(scat, 16)

                    def run(j, m, u, k, uses, stores):
                        value = j + 1 if isinstance(j, int) else pool.to_reg(j + 1)
                        pool.wait_ge(C["zeroed"], 16 * ZERO_DMAS)
                        pool.wait_ge(y_done, value)
                        for c in range(SC):
                            pool.indirect_dma_start(
                                ybuf, bass.IndirectOffsetOnAxis(ap=XS[:, m, c, D:D + 1].bitcast(U32), axis=0),
                                YS[:, u, c, :], None).then_inc(y_out[u], 16)

                    tiles(pool, run)
                    for u in range(2):
                        pool.wait_ge(y_out[u], 16 * SC * ((NTILES + 1 - u) // 2))

        with nc.sbuf_tensor(L + "yg", [P, TOP, NT, D], F32) as YG:
            rows_in, before = C["rows_in"], 16 * layer
            added = sem("added")
            aggr = sem("aggr")
            stored = sem("stored")
            results = ybuf[0:TOP * B * T].rearrange("(k t p) d -> p k t d", k=TOP, p=P)
            with nc.Block() as block:
                @block.scalar
                def _(act):
                    for b in range(B):
                        tiles_of = slice(b * TT, (b + 1) * TT)
                        for k in range(TOP):
                            act.dma_start(YG[:, k, tiles_of, :], results[:, k, tiles_of, :]).then_inc(rows_in[b], 16)

                @block.vector
                def _(dve):
                    n = 0
                    for b in range(B):
                        dve.wait_ge(rows_in[b], before + 16 * TOP)
                        for k in range(TOP):
                            if k:
                                dve.wait_ge(added, TOP * b + k)
                            of = slice(b * TT, (b + 1) * TT)
                            dve.tensor_tensor(X[:, of, :], X[:, of, :], YG[:, k, of, :], ALU.add).then_inc(added, 1)
                        if layer == 0:
                            dve.wait_ge(added, TOP * (b + 1))
                            for t in range(TT):
                                dve.bn_stats(C["stats"][:, t, :], X[:, b * TT + t, :]).then_inc(aggr, 1)
                            dve.wait_ge(aggr, n + TT)
                            for t in range(TT):
                                dve.bn_aggr(MV[:, b * TT + t, :], C["stats"][:, t, :]).then_inc(aggr, 1)
                            n += 2 * TT
                            dve.wait_ge(aggr, n)

                if layer == 1:
                    @block.sync
                    def _(sp):
                        for b in range(B):
                            sp.wait_ge(added, TOP * (b + 1))
                            sp.dma_start(C["out"][:, b * TT:(b + 1) * TT, :],
                                         X[:, b * TT:(b + 1) * TT, :]).then_inc(stored, 16)
                        sp.wait_ge(stored, 16 * B)


ZERO_ROWS = 1024
ZERO_DMAS = (E * CAP + 2 * B * T + E * TS + B * T) // ZERO_ROWS
ROW = D + 2
NOWHERE = 2 * B * T


def fill_slots(sp, C):
    sp.wait_ge(C["zero_set"], 2)
    for buf, rows in ((C["xbuf"][0], E * CAP), (C["xbuf"][1], 2 * B * T + E * TS)):
        for r in range(0, rows, ZERO_ROWS):
            sp.dma_start(buf[r:r + ZERO_ROWS].rearrange("(p c) d -> p c d", p=P),
                         C["zero"][:, :, :]).then_inc(C["zeroed"], 16)
    for r in range(0, B * T, ZERO_ROWS):
        sp.dma_start(C["ybuf"][0][r:r + ZERO_ROWS].rearrange("(p c) d -> p c d", p=P),
                     C["zero"][:, :, 0:D]).then_inc(C["zeroed"], 16)


def program(nc, a, out):
    with ExitStack() as ctx:
        def sb(name, shape, dt=F32):
            return ctx.enter_context(nc.sbuf_tensor(name, shape, dt))

        def sem(name):
            return ctx.enter_context(nc.semaphore(name))

        X = sb("x", [P, NT, D])
        MV = sb("mean_var", [P, NT, 2])
        RSTD = sb("rstd", [P, NT])
        C = {
            "identf": sb("identf", [P, P]), "identb": sb("identb", [P, P], BF16),
            "maskq": sb("maskq", [P, P], BF16), "maskk": sb("maskk", [P, P], BF16),
            "q_stack": sb("q_stack", [P, 2, PAIRS, T], BF16), "k_stack": sb("k_stack", [P, 2, PAIRS, T], BF16),
            "bcast": sb("bcast", [P, P]), "stats": sb("stats", [P, TT, 6]),
            "aggregate": sb("aggregate", [P, TT, 2]),
            "qk_biased": sb("qk_biased", [P, 2, T]),
            "root": sb("root", [P, NT]), "root2": sb("root2", [P, NT]), "eps": sb("eps", [P, 1]),
        }
        scratch = [nc.dram_tensor(f"qk_scratch{i}", [B, 2, 2, PARTS, P // 2, T], BF16).ap() for i in range(2)]

        xbuf = [nc.dram_tensor("x_slots0", [E * CAP + B * T, ROW], F32).ap(),
                nc.dram_tensor("x_slots1", [2 * B * T + E * TS, ROW], F32).ap()]
        ybuf = [nc.dram_tensor(f"results{i}", [NOWHERE + ZERO_ROWS, D], F32).ap() for i in range(2)]
        C["zero"] = sb("zero", [P, ZERO_ROWS // P, ROW])
        C["xbuf"], C["ybuf"] = xbuf, ybuf
        C["zeroed"] = sem("zeroed")
        C["loaded"] = [sem(f"loaded{i}") for i in range(DEPTH)]
        C["rows_in"] = [sem(f"rows_in{b}") for b in range(B)]
        zero_set = C["zero_set"] = sem("zero_set")

        x_in = a["L0_attn_x"].rearrange("b (t p) d -> p (b t) d", p=P)
        out_v = out.rearrange("b (t p) d -> p (b t) d", p=P)

        def rstd(tag, load):
            x_in_done = [sem(f"{tag}_x_in{c}") for c in range(B)] if load else None
            step = sem(f"{tag}_rstd_step")
            rooted = sem(f"{tag}_rooted")
            const = sem(f"{tag}_const") if load else None
            with nc.Block() as block:
                if load:
                    @block.sync
                    def _(sp):
                        for c in range(B):
                            sp.dma_start(X[:, c * TT:(c + 1) * TT, :],
                                         x_in[:, c * TT:(c + 1) * TT, :]).then_inc(x_in_done[c], 16)

                    @block.gpsimd
                    def _(pool):
                        pool.memset(C["eps"][:], EPS).then_inc(const, 1)
                        for m in ("identf", "identb", "maskq", "maskk", "bcast"):
                            pool.memset(C[m][:], 0.0).then_inc(const, 1)
                        pool.wait_ge(const, 6)
                        for m in ("identf", "identb"):
                            pool.affine_select(out=C[m][:, :], in_=C[m][:, :], compare_op=ALU.not_equal, fill=1.0,
                                               base=0, pattern=[[-1, P]], channel_multiplier=1).then_inc(const, 1)
                        pool.affine_select(out=C["maskq"][:, :], in_=C["maskq"][:, :], compare_op=ALU.is_ge,
                                           fill=MASKED, base=0, pattern=[[-1, P]], channel_multiplier=1)\
                            .then_inc(const, 1)
                        pool.affine_select(out=C["maskk"][:, :], in_=C["maskk"][:, :], compare_op=ALU.is_ge,
                                           fill=MASKED, base=0, pattern=[[1, P]], channel_multiplier=-1)\
                            .then_inc(const, 1)
                        bc = C["bcast"][:, :].rearrange("p (j r) -> p j r", j=4)
                        pool.affine_select(out=bc, in_=bc, compare_op=ALU.not_equal, fill=1.0, base=-DQ,
                                           pattern=[[-32, 4], [0, 32]], channel_multiplier=1).then_inc(const, 1)
                        pool.memset(C["q_stack"][:].bitcast(F32), 0.0).then_inc(const, 1)
                        pool.memset(C["k_stack"][:].bitcast(F32), TWO_ONES).then_inc(const, 1)
                        pool.memset(C["zero"][:, :, :], 0.0).then_inc(zero_set, 1)
                        pool.wait_ge(zero_set, 1)
                        pool.iota(C["zero"][:, :, D:D + 1].bitcast(mybir.dt.int32).rearrange("p c a -> p (c a)"),
                                  pattern=[[1, ZERO_ROWS // P]], base=NOWHERE, channel_multiplier=ZERO_ROWS // P)\
                            .then_inc(zero_set, 1)

                @block.vector
                def _(dve):
                    n = 0
                    if load:
                        for c in range(B):
                            dve.wait_ge(x_in_done[c], 16)
                            for t in range(TT):
                                dve.bn_stats(C["stats"][:, t, :], X[:, c * TT + t, :]).then_inc(step, 1)
                            dve.wait_ge(step, n + TT)
                            for t in range(TT):
                                dve.bn_aggr(MV[:, c * TT + t, :], C["stats"][:, t, :]).then_inc(step, 1)
                            n += 2 * TT
                            dve.wait_ge(step, n)
                    dve.wait_ge(rooted, 1)
                    dve.reciprocal(RSTD[:, :], C["root"][:, :]).then_inc(step, 1)
                    dve.wait_ge(step, n + 1)
                    dve.tensor_tensor(C["root"][:, :], RSTD[:, :], RSTD[:, :], ALU.mult).then_inc(step, 1)
                    dve.tensor_scalar(C["root2"][:, :], MV[:, :, 1], EPS, None, ALU.add).then_inc(step, 1)
                    dve.wait_ge(step, n + 3)
                    dve.tensor_tensor(C["root"][:, :], C["root"][:, :], C["root2"][:, :], ALU.mult).then_inc(step, 1)
                    dve.wait_ge(step, n + 4)
                    dve.tensor_scalar(C["root"][:, :], C["root"][:, :], -0.5, 1.5, ALU.mult, ALU.add)\
                        .then_inc(step, 1)
                    dve.wait_ge(step, n + 5)
                    dve.tensor_tensor(RSTD[:, :], RSTD[:, :], C["root"][:, :], ALU.mult).then_inc(step, 1)
                    dve.wait_ge(step, n + 6)

                @block.scalar
                def _(act):
                    if load:
                        act.wait_ge(const, 1)
                        act.wait_ge(step, 2 * NT)
                    act.activation(C["root"][:, :], MV[:, :, 1], ACT.Sqrt, bias=C["eps"][:, 0:1]).then_inc(rooted, 1)

        C["out"] = out_v
        rstd("start", True)
        attention(nc, ctx, 0, X, MV, RSTD, C,
                  {k[8:]: v for k, v in a.items() if k.startswith("L0_attn")}, scratch[0])
        rstd("ffn0", False)
        moe(nc, ctx, 0, X, MV, RSTD, C, {k[7:]: v for k, v in a.items() if k.startswith("L0_ffn")},
            xbuf[0], ybuf[0])
        rstd("attn1", False)
        attention(nc, ctx, 1, X, MV, RSTD, C,
                  {k[8:]: v for k, v in a.items() if k.startswith("L1_attn")}, scratch[1])
        rstd("ffn1", False)
        moe(nc, ctx, 1, X, MV, RSTD, C, {k[7:]: v for k, v in a.items() if k.startswith("L1_ffn")},
            xbuf[1], ybuf[1])


def kernel(**inputs):
    import numpy as _np
    import concourse.bacc as _bacc
    from concourse import mybir as _mybir
    from concourse.bass_utils import run_bass_kernel_spmd as _run

    laid = {k: _np.ascontiguousarray(v) for k, v in inputs.items()}
    order = _np.arange(P).reshape(PAIRS, 2, DQ).transpose(1, 2, 0).reshape(P)
    for m in ("L0_attn_W_UQ", "L0_attn_W_UK"):
        laid[m] = _np.ascontiguousarray(laid[m][:, order])
    both = _np.concatenate([order, P + order])
    laid["L1_attn_bqk"] = _np.ascontiguousarray(laid["L1_attn_bc"][both])
    wc = laid.pop("L1_attn_Wc")
    laid["L1_attn_WcT"] = _np.ascontiguousarray(_np.concatenate([wc[both], wc[2 * P:]]).T)
    laid["L1_attn_WoT"] = _np.ascontiguousarray(laid.pop("L1_attn_Wo").T)
    laid["L0_ffn_router"] = _np.ascontiguousarray(laid.pop("L0_ffn_router_w").T)
    laid["L1_ffn_router"] = laid.pop("L1_ffn_Wr")
    for layer, w1, b1 in (("L0_ffn_", "w1", "b1"), ("L1_ffn_", "W1", "b1")):
        e, d, h = laid[layer + w1].shape
        bias = laid.pop(layer + b1).reshape(e, h // d, d).transpose(0, 2, 1)
        laid[layer + "w1"] = _np.ascontiguousarray(_np.concatenate([laid.pop(layer + w1), bias], axis=2))
    laid["L1_ffn_w2"] = laid.pop("L1_ffn_W2")
    nc = _bacc.Bacc("TRN2", target_bir_lowering=False, num_devices=1)
    arrays, aps = {}, {}
    for name, v in laid.items():
        arrays[f"in_{name}"] = v
        aps[name] = nc.dram_tensor(f"in_{name}", v.shape, _mybir.dt.from_np(v.dtype), kind="ExternalInput").ap()
    out = nc.dram_tensor("out", (B, T, D), F32, kind="ExternalOutput").ap()
    program(nc, aps, out)
    r = _run(nc, [arrays], core_ids=[0])
    return r.results[0]["out"]
```
